# Optimizing a Trainium2 kernel written in Bass

```python
import numpy as np
import jax
import jax.numpy as jnp

def _softmax(x, axis=-1):
    return jax.nn.softmax(x, axis=axis)

def _gelu(x):
    return jax.nn.gelu(x, approximate=True)

def _silu(x):
    return jax.nn.silu(x)

def _sigmoid(x):
    return jax.nn.sigmoid(x)

def _layernorm(x, axis=-1, eps=1e-05):
    m = jnp.mean(x, axis=axis, keepdims=True)
    v = jnp.var(x, axis=axis, keepdims=True)
    return (x - m) / jnp.sqrt(v + eps)

def _scatter_add(tgt, idx, src, axis=0):
    return tgt.at[idx].add(src)

def _segment_sum(src, seg, n):
    return jax.ops.segment_sum(src, seg, n)
kernel_name = 'mk_flamingo_gated_d4_seqx_r8_63cf46'

def setup_inputs(seed: int=0):
    np.random.seed(seed)
    _w = jnp.asarray

    def _rec_inputs():
        import jax
        import jax.numpy as jnp
        _rk = jax.random.key(seed)
        x = -0.0002928 + 1 * jax.random.normal(jax.random.fold_in(_rk, 1), (4, 256, 128), jnp.float32)
        _lenS = 256 - jax.random.randint(jax.random.fold_in(_rk, 7), (4,), 0, max(1, 256 // 4) + 1, jnp.int32)
        _lenS2 = 1601 - jax.random.randint(jax.random.fold_in(_rk, 8), (4,), 0, max(1, 1601 // 4) + 1, jnp.int32)
        _ctx_1024P = jax.random.normal(jax.random.fold_in(_rk, 11), (4, 16, 128), jnp.float32)
        _ctx_1024c = jax.random.dirichlet(jax.random.fold_in(_rk, 511), 0.3 * jnp.ones((16,), jnp.float32), (4, 1601))
        _ctx_1024t = jnp.einsum('bsk,bkd->bsd', _ctx_1024c, _ctx_1024P)
        _ctx_1024t = _ctx_1024t * jax.lax.rsqrt(jnp.mean(jnp.square(_ctx_1024t)) + 1e-12) * 0.953939
        ctx_1024 = -1.39393e-06 + 0.999914 * (_ctx_1024t + 0.3 * jax.random.normal(jax.random.fold_in(_rk, 611), (4, 1601, 128), jnp.float32))
        _ctxb_2048x8P = jax.random.normal(jax.random.fold_in(_rk, 12), (4, 16, 8), jnp.float32)
        _ctxb_2048x8c = jax.random.dirichlet(jax.random.fold_in(_rk, 512), 0.3 * jnp.ones((16,), jnp.float32), (4, 1601))
        _ctxb_2048x8t = jnp.einsum('bsk,bkd->bsd', _ctxb_2048x8c, _ctxb_2048x8P)
        _ctxb_2048x8t = _ctxb_2048x8t * jax.lax.rsqrt(jnp.mean(jnp.square(_ctxb_2048x8t)) + 1e-12) * 0.953939
        ctxb_2048x8 = -0.00745576 + 0.997402 * (_ctxb_2048x8t + 0.3 * jax.random.normal(jax.random.fold_in(_rk, 612), (4, 1601, 8), jnp.float32))
        _validS = jnp.arange(256)[None, :] < _lenS[:, None]
        _validS2 = jnp.arange(1601)[None, :] < _lenS2[:, None]
        _causal = jnp.tril(jnp.ones((256, 256), dtype=bool))
        mask_1x1xSxS2_bk1 = jnp.broadcast_to(_validS2[0:1, None, None, :], (1, 1, 256, 1601))
        _g = jax.random.normal(jax.random.fold_in(_rk, 9001), (2, 4), jnp.float32)
        _g = jnp.sign(_g) * jnp.maximum(jnp.abs(_g), 1.0) + (_g == 0) * 1.0
        g_xattn = _g[0]
        g_ffn = _g[1]
        return (x, ctx_1024, ctxb_2048x8, mask_1x1xSxS2_bk1, g_xattn, g_ffn)
    x, ctx_1024, ctxb_2048x8, mask_1x1xSxS2_bk1, g_xattn, g_ffn = _rec_inputs()

    def _L0_xattn_setup():
        import jax, jax.numpy as jnp
        import numpy as np
        D_MODEL = 128
        NUM_HEADS = 16
        THRESHOLD = 0.1
        key = jax.random.key(seed)
        ks = jax.random.split(key, 12)
        B, L, D, C = (2, 256, D_MODEL, 8)
        s = 1.0 / np.sqrt(D)
        inp = {'q_x': jax.random.normal(ks[0], (B, L, D), jnp.float32), 'k_x': jax.random.normal(ks[1], (B, L, D), jnp.float32), 'v_x': jax.random.normal(ks[2], (B, L, D), jnp.float32), 'energy_coeffs': jax.random.normal(ks[3], (B, L, C), jnp.float32), 'Wq': jax.random.normal(ks[4], (D, D), jnp.float32) * s, 'bq': jnp.zeros((D,), jnp.float32), 'Wk': jax.random.normal(ks[5], (D, D), jnp.float32) * s, 'bk': jnp.zeros((D,), jnp.float32), 'Wv': jax.random.normal(ks[6], (D, D), jnp.float32) * s, 'bv': jnp.zeros((D,), jnp.float32), 'Wo': jax.random.normal(ks[7], (D, D), jnp.float32) * s, 'bo': jnp.zeros((D,), jnp.float32)}
        return inp
    _L0_xattn_all = _L0_xattn_setup()
    _L0_xattn_in = {k: v for k, v in _L0_xattn_all.items() if k in ('Wq', 'bq', 'Wk', 'bk', 'Wv', 'bv', 'Wo', 'bo')}
    del _L0_xattn_all

    def _L0_ffn_setup():
        import jax, jax.numpy as jnp
        import numpy as np
        EPS = 1e-06
        LN_EPS = 1e-05

        def _absmean_core(W):
            gamma = jnp.mean(jnp.abs(W)) + EPS
            Ws = W / gamma
            Wq = jnp.sign(Ws) * jnp.minimum(jnp.round(jnp.abs(Ws)), 1.0)
            return (Wq, gamma)

        @jax.custom_vjp
        def absmean(W):
            return _absmean_core(W)[0]

        def _absmean_fwd(W):
            Wq, gamma = _absmean_core(W)
            return (Wq, gamma)

        def _absmean_bwd(gamma, g):
            return (g / gamma,)
        absmean.defvjp(_absmean_fwd, _absmean_bwd)

        def layernorm(x, w, b, eps=LN_EPS):
            mu = jnp.mean(x, axis=-1, keepdims=True)
            var = jnp.mean((x - mu) ** 2, axis=-1, keepdims=True)
            return (x - mu) * jax.lax.rsqrt(var + eps) * w + b
        key = jax.random.key(seed)
        k1, k2, k3 = jax.random.split(key, 3)
        d, h = (128, 512)
        B, T = (8, 256)
        return {'x': jax.random.normal(k1, (B, T, d), jnp.float32), 'W_fc': jax.random.normal(k2, (h, d), jnp.float32), 'ln_w': jnp.ones((h,), jnp.float32), 'ln_b': jnp.zeros((h,), jnp.float32), 'W_proj': jax.random.normal(k3, (d, h), jnp.float32)}
    _L0_ffn_all = _L0_ffn_setup()
    _L0_ffn_in = {k: v for k, v in _L0_ffn_all.items() if k in ('W_fc', 'ln_w', 'ln_b', 'W_proj')}
    del _L0_ffn_all

    def _L1_xattn_setup():
        import jax, jax.numpy as jnp
        import numpy as np
        DIM = 128
        NUM_HEADS = 16
        HEAD_DIM = DIM // NUM_HEADS
        SCALE = HEAD_DIM ** (-0.5)

        def _heads(x, w, b):
            B, S, _ = x.shape
            y = x @ w.T + b
            return y.reshape(B, S, NUM_HEADS, HEAD_DIM).transpose(0, 2, 1, 3)
        key = jax.random.key(seed)
        ks = jax.random.split(key, 16)
        B, L, G = (2, 256, 64)
        s = DIM ** (-0.5)
        inp = {'local_hidden': jax.random.normal(ks[0], (B, L, DIM), jnp.float32), 'global_hidden': jax.random.normal(ks[1], (B, G, DIM), jnp.float32), 'q_w': jax.random.normal(ks[2], (DIM, DIM), jnp.float32) * s, 'q_b': jnp.zeros((DIM,), jnp.float32), 'k_w': jax.random.normal(ks[3], (DIM, DIM), jnp.float32) * s, 'k_b': jnp.zeros((DIM,), jnp.float32), 'v_w': jax.random.normal(ks[4], (DIM, DIM), jnp.float32) * s, 'v_b': jnp.zeros((DIM,), jnp.float32), 'kg_w': jax.random.normal(ks[5], (DIM, DIM), jnp.float32) * s, 'kg_b': jnp.zeros((DIM,), jnp.float32), 'vg_w': jax.random.normal(ks[6], (DIM, DIM), jnp.float32) * s, 'vg_b': jnp.zeros((DIM,), jnp.float32), 'out_w': jax.random.normal(ks[7], (DIM, DIM), jnp.float32) * s, 'out_b': jnp.zeros((DIM,), jnp.float32), 'gate': jnp.zeros((), jnp.float32)}
        return inp
    _L1_xattn_all = _L1_xattn_setup()
    _L1_xattn_in = {k: v for k, v in _L1_xattn_all.items() if k in ('q_w', 'q_b', 'k_w', 'k_b', 'v_w', 'v_b', 'kg_w', 'kg_b', 'vg_w', 'vg_b', 'out_w', 'out_b', 'gate')}
    del _L1_xattn_all

    def _L1_ffn_setup():
        import jax, jax.numpy as jnp
        import numpy as np
        DIM, E, K, H = (128, 8, 2, 512)
        key = jax.random.key(seed)
        ks = jax.random.split(key, 5)
        s_in = 1.0 / np.sqrt(DIM)
        s_h = 1.0 / np.sqrt(H)
        return {'x': jax.random.normal(ks[0], (4, 256, DIM), dtype=jnp.float32), 'Wr': jax.random.normal(ks[1], (DIM, E), dtype=jnp.float32) * s_in, 'W1': jax.random.normal(ks[2], (E, DIM, H), dtype=jnp.float32) * s_in, 'b1': jnp.zeros((E, H), dtype=jnp.float32), 'W2': jax.random.normal(ks[3], (E, H, DIM), dtype=jnp.float32) * s_h, 'b2': jnp.zeros((E, DIM), dtype=jnp.float32)}
    _L1_ffn_all = _L1_ffn_setup()
    _L1_ffn_in = {k: v for k, v in _L1_ffn_all.items() if k in ('Wr', 'W1', 'b1', 'W2', 'b2')}
    del _L1_ffn_all

    def _L2_xattn_setup():
        import jax, jax.numpy as jnp
        import numpy as np
        NUM_HEADS = 16
        key = jax.random.key(seed)
        ks = jax.random.split(key, 6)
        B, N, M, D = (4, 256, 256, 128)
        s = 1.0 / np.sqrt(D)
        return {'inputs': jax.random.normal(ks[0], (B, N, D), dtype=jnp.float32), 'encoderOutputs': jax.random.normal(ks[1], (B, M, D), dtype=jnp.float32), 'wq': jax.random.normal(ks[2], (D, D), dtype=jnp.float32) * s, 'wk': jax.random.normal(ks[3], (D, D), dtype=jnp.float32) * s, 'wv': jax.random.normal(ks[4], (D, D), dtype=jnp.float32) * s, 'wo': jax.random.normal(ks[5], (D, D), dtype=jnp.float32) * s}
    _L2_xattn_all = _L2_xattn_setup()
    _L2_xattn_in = {k: v for k, v in _L2_xattn_all.items() if k in ('wq', 'wk', 'wv', 'wo')}
    del _L2_xattn_all

    def _L2_ffn_setup():
        import jax, jax.numpy as jnp
        import numpy as np
        B, N, D = (4, 256, 128)
        SPARSITY = 0.01
        key = jax.random.key(seed)
        k1, k2, k3 = jax.random.split(key, 3)
        x = jax.random.normal(k1, (B, N, D), dtype=jnp.float32)
        spatial = jax.random.normal(k2, (D, D), dtype=jnp.float32) * 0.02
        freq = jnp.fft.fft(spatial, axis=-1)
        k = int(D * SPARSITY)
        mag = jnp.abs(freq)
        kth = jax.lax.top_k(mag, k)[0][:, -1:]
        w_sparse = jnp.where(mag >= kth, freq, 0.0 + 0j)
        bias = jax.random.normal(k3, (D,), dtype=jnp.float32) * 0.01
        return {'x': x, 'w_freq_real': jnp.real(w_sparse).astype(jnp.float32), 'w_freq_imag': jnp.imag(w_sparse).astype(jnp.float32), 'bias': bias}
    _L2_ffn_all = _L2_ffn_setup()
    _L2_ffn_in = {k: v for k, v in _L2_ffn_all.items() if k in ('w_freq_real', 'w_freq_imag', 'bias')}
    del _L2_ffn_all

    def _L3_xattn_setup():
        import jax, jax.numpy as jnp
        import numpy as np
        D_MODEL = 128
        N_HEADS = 16
        D_HEAD = D_MODEL // N_HEADS
        B, T = (4, 256)
        key = jax.random.key(seed)
        ks = jax.random.split(key, 7)
        s = 0.02
        q = jax.random.normal(ks[0], (B, T, D_MODEL), dtype=jnp.float32)
        k = jax.random.normal(ks[1], (B, T, D_MODEL), dtype=jnp.float32)
        v = jax.random.normal(ks[2], (B, T, D_MODEL), dtype=jnp.float32)
        mask = jnp.triu(jnp.ones((T, T), dtype=bool), k=1)[None, None, :, :]
        Wq = jax.random.normal(ks[3], (D_MODEL, D_MODEL), dtype=jnp.float32) * s
        Wk = jax.random.normal(ks[4], (D_MODEL, D_MODEL), dtype=jnp.float32) * s
        Wv = jax.random.normal(ks[5], (D_MODEL, D_MODEL), dtype=jnp.float32) * s
        Wo = jax.random.normal(ks[6], (D_MODEL, D_MODEL), dtype=jnp.float32) * s
        return {'q': q, 'k': k, 'v': v, 'mask': mask, 'Wq': Wq, 'Wk': Wk, 'Wv': Wv, 'Wo': Wo}
    _L3_xattn_all = _L3_xattn_setup()
    _L3_xattn_in = {k: v for k, v in _L3_xattn_all.items() if k in ('Wq', 'Wk', 'Wv', 'Wo')}
    del _L3_xattn_all

    def _L3_ffn_setup():
        import jax, jax.numpy as jnp
        import numpy as np
        B, T, C = (4, 256, 128)
        E, H, K = (8, 256, 2)
        key = jax.random.key(seed)
        ks = jax.random.split(key, 7)
        s_in = 1.0 / np.sqrt(C)
        s_hid = 1.0 / np.sqrt(H)
        return {'x': jax.random.normal(ks[0], (B, T, C), dtype=jnp.float32), 'gate_w': jax.random.uniform(ks[1], (C, E), jnp.float32, -s_in, s_in), 'gate_b': jnp.zeros((E,), jnp.float32), 'w1': jax.random.uniform(ks[2], (E, C, H), jnp.float32, -s_in, s_in), 'b1': jax.random.uniform(ks[3], (E, H), jnp.float32, -s_in, s_in), 'w2': jax.random.uniform(ks[4], (E, H, C), jnp.float32, -s_hid, s_hid), 'b2': jax.random.uniform(ks[5], (E, C), jnp.float32, -s_hid, s_hid)}
    _L3_ffn_all = _L3_ffn_setup()
    _L3_ffn_in = {k: v for k, v in _L3_ffn_all.items() if k in ('gate_w', 'gate_b', 'w1', 'b1', 'w2', 'b2')}
    del _L3_ffn_all
    return {'x': x, 'ctx_1024': ctx_1024, 'ctxb_2048x8': ctxb_2048x8, 'mask_1x1xSxS2_bk1': mask_1x1xSxS2_bk1, 'g_xattn': g_xattn, 'g_ffn': g_ffn, 'L0_xattn_Wq': _L0_xattn_in['Wq'], 'L0_xattn_bq': _L0_xattn_in['bq'], 'L0_xattn_Wk': _L0_xattn_in['Wk'], 'L0_xattn_bk': _L0_xattn_in['bk'], 'L0_xattn_Wv': _L0_xattn_in['Wv'], 'L0_xattn_bv': _L0_xattn_in['bv'], 'L0_xattn_Wo': _L0_xattn_in['Wo'], 'L0_xattn_bo': _L0_xattn_in['bo'], 'L0_ffn_W_fc': _L0_ffn_in['W_fc'], 'L0_ffn_ln_w': _L0_ffn_in['ln_w'], 'L0_ffn_ln_b': _L0_ffn_in['ln_b'], 'L0_ffn_W_proj': _L0_ffn_in['W_proj'], 'L1_xattn_q_w': _L1_xattn_in['q_w'], 'L1_xattn_q_b': _L1_xattn_in['q_b'], 'L1_xattn_k_w': _L1_xattn_in['k_w'], 'L1_xattn_k_b': _L1_xattn_in['k_b'], 'L1_xattn_v_w': _L1_xattn_in['v_w'], 'L1_xattn_v_b': _L1_xattn_in['v_b'], 'L1_xattn_kg_w': _L1_xattn_in['kg_w'], 'L1_xattn_kg_b': _L1_xattn_in['kg_b'], 'L1_xattn_vg_w': _L1_xattn_in['vg_w'], 'L1_xattn_vg_b': _L1_xattn_in['vg_b'], 'L1_xattn_out_w': _L1_xattn_in['out_w'], 'L1_xattn_out_b': _L1_xattn_in['out_b'], 'L1_xattn_gate': _L1_xattn_in['gate'], 'L1_ffn_Wr': _L1_ffn_in['Wr'], 'L1_ffn_W1': _L1_ffn_in['W1'], 'L1_ffn_b1': _L1_ffn_in['b1'], 'L1_ffn_W2': _L1_ffn_in['W2'], 'L1_ffn_b2': _L1_ffn_in['b2'], 'L2_xattn_wq': _L2_xattn_in['wq'], 'L2_xattn_wk': _L2_xattn_in['wk'], 'L2_xattn_wv': _L2_xattn_in['wv'], 'L2_xattn_wo': _L2_xattn_in['wo'], 'L2_ffn_w_freq_real': _L2_ffn_in['w_freq_real'], 'L2_ffn_w_freq_imag': _L2_ffn_in['w_freq_imag'], 'L2_ffn_bias': _L2_ffn_in['bias'], 'L3_xattn_Wq': _L3_xattn_in['Wq'], 'L3_xattn_Wk': _L3_xattn_in['Wk'], 'L3_xattn_Wv': _L3_xattn_in['Wv'], 'L3_xattn_Wo': _L3_xattn_in['Wo'], 'L3_ffn_gate_w': _L3_ffn_in['gate_w'], 'L3_ffn_gate_b': _L3_ffn_in['gate_b'], 'L3_ffn_w1': _L3_ffn_in['w1'], 'L3_ffn_b1': _L3_ffn_in['b1'], 'L3_ffn_w2': _L3_ffn_in['w2'], 'L3_ffn_b2': _L3_ffn_in['b2']}

def reference(x, ctx_1024, ctxb_2048x8, mask_1x1xSxS2_bk1, g_xattn, g_ffn, L0_xattn_Wq, L0_xattn_bq, L0_xattn_Wk, L0_xattn_bk, L0_xattn_Wv, L0_xattn_bv, L0_xattn_Wo, L0_xattn_bo, L0_ffn_W_fc, L0_ffn_ln_w, L0_ffn_ln_b, L0_ffn_W_proj, L1_xattn_q_w, L1_xattn_q_b, L1_xattn_k_w, L1_xattn_k_b, L1_xattn_v_w, L1_xattn_v_b, L1_xattn_kg_w, L1_xattn_kg_b, L1_xattn_vg_w, L1_xattn_vg_b, L1_xattn_out_w, L1_xattn_out_b, L1_xattn_gate, L1_ffn_Wr, L1_ffn_W1, L1_ffn_b1, L1_ffn_W2, L1_ffn_b2, L2_xattn_wq, L2_xattn_wk, L2_xattn_wv, L2_xattn_wo, L2_ffn_w_freq_real, L2_ffn_w_freq_imag, L2_ffn_bias, L3_xattn_Wq, L3_xattn_Wk, L3_xattn_Wv, L3_xattn_Wo, L3_ffn_gate_w, L3_ffn_gate_b, L3_ffn_w1, L3_ffn_b1, L3_ffn_w2, L3_ffn_b2):
    import jax
    import jax.numpy as jnp

    def _L0_xattn_ref(q_x, k_x, v_x, energy_coeffs, Wq, bq, Wk, bk, Wv, bv, Wo, bo):
        import jax, jax.numpy as jnp
        import numpy as np
        D_MODEL = 128
        NUM_HEADS = 16
        THRESHOLD = 0.1
        B, L, D = q_x.shape
        H = NUM_HEADS
        Dh = D // H

        def proj(x, W, b):
            y = x @ W + b
            return y.reshape(B, -1, H, Dh).transpose(0, 2, 1, 3)
        Q = proj(q_x, Wq, bq)
        K = proj(k_x, Wk, bk)
        V = proj(v_x, Wv, bv)
        scores = jnp.einsum('bhqd,bhkd->bhqk', Q, K) / np.sqrt(Dh).astype(np.float32)
        attn = jax.nn.softmax(scores, axis=-1)
        attn = jnp.nan_to_num(attn, nan=0.0)
        energy = jnp.abs(energy_coeffs).mean(axis=-1)
        gate = jax.nn.sigmoid((energy - THRESHOLD) * 10.0)[:, None, None, :]
        attn = attn * gate
        out = jnp.einsum('bhqk,bhkd->bhqd', attn, V)
        out = out.transpose(0, 2, 1, 3).reshape(B, L, D)
        return out @ Wo + bo

    def _L0_ffn_ref(x, W_fc, ln_w, ln_b, W_proj):
        import jax, jax.numpy as jnp
        import numpy as np
        EPS = 1e-06
        LN_EPS = 1e-05

        def _absmean_core(W):
            gamma = jnp.mean(jnp.abs(W)) + EPS
            Ws = W / gamma
            Wq = jnp.sign(Ws) * jnp.minimum(jnp.round(jnp.abs(Ws)), 1.0)
            return (Wq, gamma)

        @jax.custom_vjp
        def absmean(W):
            return _absmean_core(W)[0]

        def _absmean_fwd(W):
            Wq, gamma = _absmean_core(W)
            return (Wq, gamma)

        def _absmean_bwd(gamma, g):
            return (g / gamma,)
        absmean.defvjp(_absmean_fwd, _absmean_bwd)

        def layernorm(x, w, b, eps=LN_EPS):
            mu = jnp.mean(x, axis=-1, keepdims=True)
            var = jnp.mean((x - mu) ** 2, axis=-1, keepdims=True)
            return (x - mu) * jax.lax.rsqrt(var + eps) * w + b
        h = jnp.einsum('btd,hd->bth', x, absmean(W_fc))
        h = jax.nn.gelu(h, approximate=False)
        h = layernorm(h, ln_w, ln_b)
        return jnp.einsum('bth,dh->btd', h, absmean(W_proj))

    def _L1_xattn_ref(local_hidden, global_hidden, q_w, q_b, k_w, k_b, v_w, v_b, kg_w, kg_b, vg_w, vg_b, out_w, out_b, gate):
        import jax, jax.numpy as jnp
        import numpy as np
        DIM = 128
        NUM_HEADS = 16
        HEAD_DIM = DIM // NUM_HEADS
        SCALE = HEAD_DIM ** (-0.5)

        def _heads(x, w, b):
            B, S, _ = x.shape
            y = x @ w.T + b
            return y.reshape(B, S, NUM_HEADS, HEAD_DIM).transpose(0, 2, 1, 3)
        B, L, _ = local_hidden.shape
        q = _heads(local_hidden, q_w, q_b)
        k_l = _heads(local_hidden, k_w, k_b)
        v_l = _heads(local_hidden, v_w, v_b)
        attn_l = jax.nn.softmax(jnp.einsum('bhqd,bhkd->bhqk', q, k_l) * SCALE, axis=-1)
        out_l = jnp.einsum('bhqk,bhkd->bhqd', attn_l, v_l)
        k_g = _heads(global_hidden, kg_w, kg_b)
        v_g = _heads(global_hidden, vg_w, vg_b)
        attn_g = jax.nn.softmax(jnp.einsum('bhqd,bhkd->bhqk', q, k_g) * SCALE, axis=-1)
        out_g = jnp.einsum('bhqk,bhkd->bhqd', attn_g, v_g)
        g = jax.nn.sigmoid(gate)
        out = g * out_l + (1.0 - g) * out_g
        out = out.transpose(0, 2, 1, 3).reshape(B, L, DIM)
        return out @ out_w.T + out_b

    def _L1_ffn_ref(x, Wr, W1, b1, W2, b2):
        import jax, jax.numpy as jnp
        import numpy as np
        DIM, E, K, H = (128, 8, 2, 512)
        batch, seq, dim = x.shape
        x_flat = x.reshape(-1, dim)
        logits = x_flat @ Wr
        w, ind = jax.lax.top_k(logits, K)
        w = jax.nn.softmax(w, axis=-1)
        combine = jnp.einsum('tke,tk->te', jax.nn.one_hot(ind, E, dtype=x.dtype), w)

        def body(acc, params):
            W1e, b1e, W2e, b2e, ce = params
            h = jax.nn.gelu(x_flat @ W1e + b1e, approximate=False)
            y = h @ W2e + b2e
            return (acc + ce[:, None] * y, None)
        out0 = jnp.zeros_like(x_flat)
        out, _ = jax.lax.scan(body, out0, (W1, b1, W2, b2, combine.T))
        return out.reshape(batch, seq, dim)

    def _L2_xattn_ref(inputs, encoderOutputs, wq, wk, wv, wo):
        import jax, jax.numpy as jnp
        import numpy as np
        NUM_HEADS = 16
        B, N, D = inputs.shape
        M = encoderOutputs.shape[1]
        H = NUM_HEADS
        hd = D // H
        q = (inputs @ wq.T).reshape(B, N, H, hd).transpose(0, 2, 1, 3)
        k = (encoderOutputs @ wk.T).reshape(B, M, H, hd).transpose(0, 2, 1, 3)
        v = (encoderOutputs @ wv.T).reshape(B, M, H, hd).transpose(0, 2, 1, 3)
        scores = jnp.einsum('bhnd,bhmd->bhnm', q, k) / jnp.sqrt(jnp.float32(hd))
        attn = jax.nn.softmax(scores, axis=-1)
        ctx = jnp.einsum('bhnm,bhmd->bhnd', attn, v)
        ctx = ctx.transpose(0, 2, 1, 3).reshape(B, N, D)
        return ctx @ wo.T

    def _L2_ffn_ref(x, w_freq_real, w_freq_imag, bias):
        import jax, jax.numpy as jnp
        import numpy as np
        B, N, D = (4, 256, 128)
        SPARSITY = 0.01
        w = jax.lax.complex(w_freq_real, w_freq_imag)
        x_freq = jnp.fft.fft(x, axis=-1)
        y_freq = jnp.einsum('bnd,do->bno', x_freq, w)
        y = jnp.real(jnp.fft.ifft(y_freq, axis=-1))
        return y + bias

    def _L3_xattn_ref(q, k, v, mask, Wq, Wk, Wv, Wo):
        import jax, jax.numpy as jnp
        import numpy as np
        D_MODEL = 128
        N_HEADS = 16
        D_HEAD = D_MODEL // N_HEADS
        B, T = (4, 256)
        H, Dh = (N_HEADS, D_HEAD)
        scale = Dh ** (-0.5)

        def split(t):
            Bt, Tt, _ = t.shape
            return t.reshape(Bt, Tt, H, Dh).transpose(0, 2, 1, 3)
        Q = split(q @ Wq.T)
        K = split(k @ Wk.T)
        V = split(v @ Wv.T)
        scores = jnp.einsum('bhqd,bhkd->bhqk', Q, K) * scale
        scores = jnp.where(mask, -jnp.inf, scores)
        attn = jax.nn.softmax(scores, axis=-1)
        attn = jnp.nan_to_num(attn)
        out = jnp.einsum('bhqk,bhkd->bhqd', attn, V)
        out = out.transpose(0, 2, 1, 3).reshape(q.shape[0], q.shape[1], H * Dh)
        return out @ Wo.T

    def _L3_ffn_ref(x, gate_w, gate_b, w1, b1, w2, b2):
        import jax, jax.numpy as jnp
        import numpy as np
        B, T, C = (4, 256, 128)
        E, H, K = (8, 256, 2)
        b, t, c = x.shape
        xf = x.reshape(b * t, c)
        logits = xf @ gate_w + gate_b
        probs = jax.nn.softmax(logits, axis=-1)
        gates, expert_idx = jax.lax.top_k(probs, K)
        h = jax.nn.relu(jnp.einsum('nc,ech->neh', xf, w1) + b1)
        expert_out = jnp.einsum('neh,ehc->nec', h, w2) + b2
        onehot = jax.nn.one_hot(expert_idx, E, dtype=xf.dtype)
        weights = jnp.einsum('nk,nke->ne', gates, onehot)
        out = jnp.einsum('ne,nec->nc', weights, expert_out)
        return out.reshape(b, t, c)
    x = x + jnp.tanh(g_xattn[0]) * _L0_xattn_ref(_layernorm(x, axis=-1), ctx_1024, ctx_1024, ctxb_2048x8, L0_xattn_Wq, L0_xattn_bq, L0_xattn_Wk, L0_xattn_bk, L0_xattn_Wv, L0_xattn_bv, L0_xattn_Wo, L0_xattn_bo)
    x = x + jnp.tanh(g_ffn[0]) * _L0_ffn_ref(_layernorm(x, axis=-1), L0_ffn_W_fc, L0_ffn_ln_w, L0_ffn_ln_b, L0_ffn_W_proj)
    x = x + jnp.tanh(g_xattn[1]) * _L1_xattn_ref(_layernorm(x, axis=-1), ctx_1024, L1_xattn_q_w, L1_xattn_q_b, L1_xattn_k_w, L1_xattn_k_b, L1_xattn_v_w, L1_xattn_v_b, L1_xattn_kg_w, L1_xattn_kg_b, L1_xattn_vg_w, L1_xattn_vg_b, L1_xattn_out_w, L1_xattn_out_b, L1_xattn_gate)
    x = x + jnp.tanh(g_ffn[1]) * _L1_ffn_ref(_layernorm(x, axis=-1), L1_ffn_Wr, L1_ffn_W1, L1_ffn_b1, L1_ffn_W2, L1_ffn_b2)
    x = x + jnp.tanh(g_xattn[2]) * _L2_xattn_ref(_layernorm(x, axis=-1), ctx_1024, L2_xattn_wq, L2_xattn_wk, L2_xattn_wv, L2_xattn_wo)
    x = x + jnp.tanh(g_ffn[2]) * _L2_ffn_ref(_layernorm(x, axis=-1), L2_ffn_w_freq_real, L2_ffn_w_freq_imag, L2_ffn_bias)
    x = x + jnp.tanh(g_xattn[3]) * _L3_xattn_ref(_layernorm(x, axis=-1), ctx_1024, ctx_1024, mask_1x1xSxS2_bk1, L3_xattn_Wq, L3_xattn_Wk, L3_xattn_Wv, L3_xattn_Wo)
    x = x + jnp.tanh(g_ffn[3]) * _L3_ffn_ref(_layernorm(x, axis=-1), L3_ffn_gate_w, L3_ffn_gate_b, L3_ffn_w1, L3_ffn_b1, L3_ffn_w2, L3_ffn_b2)
    return x

_drawn_inputs = setup_inputs


def setup_inputs(seed=0):
    import zlib

    import numpy as np

    out = dict(_drawn_inputs(seed))
    spreads = {'L0_xattn_bq': (0.0, 0.381),
     'L0_xattn_bk': (0.0, 2.0),
     'L0_xattn_bv': (0.0, 0.1),
     'L0_xattn_bo': (0.0, 0.1),
     'L0_ffn_ln_w': (1.0, 0.2),
     'L0_ffn_ln_b': (0.0, 0.1),
     'L1_xattn_q_b': (0.0, 0.8),
     'L1_xattn_k_b': (0.0, 2.0),
     'L1_xattn_v_b': (0.0, 0.8),
     'L1_xattn_kg_b': (0.0, 2.0),
     'L1_xattn_vg_b': (0.0, 0.8),
     'L1_xattn_out_b': (0.0, 0.8),
     'L1_ffn_b1': (0.0, 2.0),
     'L1_ffn_b2': (0.0, 0.8),
     'L3_ffn_gate_b': (0.0, 0.8)}
    factors = {'ctxb_2048x8': 64.0,
     'g_ffn': 8.0,
     'L1_xattn_q_w': 7.127,
     'L1_xattn_k_w': 8.0,
     'L1_xattn_v_w': 5.18,
     'L1_xattn_kg_w': 8.0,
     'L1_xattn_vg_w': 3.324,
     'L1_xattn_out_w': 2.826,
     'L2_xattn_wq': 5.118,
     'L2_xattn_wk': 5.05,
     'L2_ffn_w_freq_real': 3.56,
     'L2_ffn_w_freq_imag': 3.647,
     'L2_ffn_bias': 62.351,
     'L3_xattn_Wq': 8.0,
     'L3_xattn_Wk': 8.0,
     'L3_xattn_Wv': 8.0,
     'L3_xattn_Wo': 8.0,
     'L3_ffn_gate_w': 8.0,
     'L3_ffn_w1': 8.0,
     'L3_ffn_b1': 8.0,
     'L3_ffn_w2': 8.0,
     'L3_ffn_b2': 46.27}
    for name, (base, spread) in spreads.items():
        noise = np.random.default_rng([zlib.crc32(name.encode()), seed]).standard_normal(out[name].shape)
        drawn = base * np.exp(spread * noise) if base else spread * noise
        out[name] = jnp.asarray(drawn.astype(out[name].dtype))
    for name, factor in factors.items():
        out[name] = (out[name] * factor).astype(out[name].dtype)
    return out
```

```python
from contextlib import ExitStack

import concourse.bass as bass
from concourse import mybir

F32 = mybir.dt.float32
F16 = mybir.dt.float16
U8 = mybir.dt.uint8
ALU = mybir.AluOpType
ACT = mybir.ActivationFunctionType
AX = mybir.AxisListType

P = 128
B, S, D = 4, 256, 128
H, DH = 16, 8
S2 = 1601
TOK = B * S
NT = TOK // P
QT = S // P
HG = 4
UNITS = B * H // HG
R = 32
KQ = 3 * DH
KM = KQ + 2
SCALE = 1.0 / DH ** 0.5
LN_EPS = 1e-5
BIG = 60000.0
MIN_MAX = -30000.0
TINY = 1e-30
FULL = S2 // P
TAIL = S2 - FULL * P
KT = FULL + 1
LKT = S // P
VW = D
E1, HID0, HID1, HID3 = 8, 512, 512, 256


def chunk_cols(nk):
    if nk == S2:
        w = S2 // 4
        return [(0, w + 1, 2), (2 * w + 1, w, 2)]
    return [(0, nk, 1)]


class Run:

    def __init__(self, index, layer, nk, mask, before):
        self.index, self.layer, self.nk, self.mask = index, layer, nk, mask
        self.ctx = {0: 0, 2: 1, 3: 2, 4: 3}.get(index)
        self.local = nk == S
        self.chunks = chunk_cols(nk)
        self.kt = (nk + P - 1) // P
        self.steps = (self.kt + 1) // 2
        self.fills = HG * self.steps
        self.c = QT * HG * len(self.chunks)
        self.uses = self.c + 1
        self.u0 = before.u0 + UNITS if before else 0
        self.use0 = before.use0 + UNITS * before.uses if before else 0
        self.fill0 = before.fill0 + UNITS * before.fills if before else 0
        self.step0 = before.step0 + UNITS * before.steps if before else 0

    def tiles(self, s):
        return [(k, min(P, self.nk - k * P)) for k in (2 * s, 2 * s + 1) if k * P < self.nk]


def runs():
    out = []
    for layer, nk, mask in ((0, S2, False), (1, S, False), (1, S2, False), (2, S2, False), (3, S2, True)):
        out.append(Run(len(out), layer, nk, mask, out[-1] if out else None))
    return out


RUNS = runs()
LOCAL = 1
FREE_SCORE, FREE_EXP, FREE_PT, FREE_PV = 2, 5, 2, 1
FREE_UP, FREE_HID, FREE_ACC = 4, 3, 8
ROUTE_V = [(3, 12, 0), (15, 24, 12)]
SQUARE = [("L0_xattn_Wq", 0), ("L0_xattn_Wk", 0), ("L0_xattn_Wv", 0), ("L0_xattn_Wo", 0),
          ("L1_xattn_q_w", 1), ("L1_xattn_k_w", 1), ("L1_xattn_v_w", 1), ("L1_xattn_kg_w", 1),
          ("L1_xattn_vg_w", 1), ("L1_xattn_out_w", 1),
          ("L2_xattn_wq", 1), ("L2_xattn_wk", 1), ("L2_xattn_wv", 1), ("L2_xattn_wo", 1),
          ("L3_xattn_Wq", 1), ("L3_xattn_Wk", 1), ("L3_xattn_Wv", 1), ("L3_xattn_Wo", 1)]
SQ = {n: i for i, (n, _) in enumerate(SQUARE)}
TURNED = [i for i, (_, t) in enumerate(SQUARE) if t]
COLS = [("L1_ffn_b1", 32), ("L3_ffn_b1", 16), ("L0_ffn_ln_w", 4), ("L0_ffn_ln_b", 4), ("L0_xattn_bq", 1),
        ("L0_xattn_bk", 1), ("L1_xattn_q_b", 1), ("L1_xattn_k_b", 1), ("L1_xattn_kg_b", 1)]
COL, _at = {}, 0
for _n, _k in COLS:
    COL[_n] = _at
    _at += _k
NCOL = _at + 1
ZCOL = _at
ROWS = [("L0_xattn_bv", D), ("L0_xattn_bo", D), ("L1_xattn_v_b", D), ("L1_xattn_vg_b", D), ("L1_xattn_out_b", D),
        ("L2_ffn_bias", D), ("zero", D), ("L3_ffn_gate_b", 8), ("g_xattn", 4), ("g_ffn", 4), ("L1_xattn_gate", 1)]
ROW, _at = {}, 0
for _n, _k in ROWS:
    ROW[_n] = _at
    _at += _k
NROW = _at
WQ = ["L0_xattn_Wq", "L1_xattn_q_w", "L2_xattn_wq", "L3_xattn_Wq"]
WO = ["L0_xattn_Wo", "L1_xattn_out_w", "L2_xattn_wo", "L3_xattn_Wo"]
WK = ["L0_xattn_Wk", "L1_xattn_k_w", "L1_xattn_kg_w", "L2_xattn_wk", "L3_xattn_Wk"]
WV = ["L0_xattn_Wv", "L1_xattn_v_w", "L1_xattn_vg_w", "L2_xattn_wv", "L3_xattn_Wv"]
BQ = ["L0_xattn_bq", "L1_xattn_q_b", None, None]
BK = ["L0_xattn_bk", "L1_xattn_k_b", "L1_xattn_kg_b", None, None]
BV = ["L0_xattn_bv", "L1_xattn_v_b", "L1_xattn_vg_b", None, None]
BO = ["L0_xattn_bo", "L1_xattn_out_b", None, None]


def flamingo(nc, a, out, last=4.0):
    ctx = ExitStack()
    with ctx:
        def sb(name, shape, dt=F32):
            return ctx.enter_context(nc.sbuf_tensor(name, shape, dt))

        def sem(name):
            return ctx.enter_context(nc.semaphore(name))

        def dram(name, shape, dt):
            return nc.dram_tensor(name, shape, dt, kind="Internal").ap()

        x = sb("x", [P, NT, D])
        xn = sb("xn", [P, NT, D])
        xnT = sb("xnT", [P, TOK])
        wsq = sb("wsq", [P, len(SQUARE), D])
        ident = sb("ident", [P, P])
        ident16 = sb("ident16", [P, P], F16)
        mask_eye = sb("mask_eye", [P, P], F16)
        ones = sb("ones", [P, P])
        rows = sb("rows", [1, NROW])
        spread = sb("spread", [P, NROW])
        cols_raw = sb("cols_raw", [NCOL, P])
        cols = sb("cols", [P, NCOL])
        ctxT = sb("ctxT", [P, 2, S2])
        k1c = sb("k1c", [P, 2, S2 + 1], F16)
        k2c = sb("k2c", [P, 2, S2 + 1], F16)
        v_all = sb("v_all", [P, B, KT, VW])
        v_loc = sb("v_loc", [P, B, LKT, VW])
        gate = sb("gate", [P, B, KT])
        gate_e = sb("gate_e", [P, B, KT])
        one16 = sb("one16", [P, S2], F16)
        qf = sb("qf", [P, TOK])
        q1c = sb("q1c", [P, TOK], F16)
        q2c = sb("q2c", [P, TOK], F16)
        kp1 = [sb(f"kp1_{i}", [P, S2 + 1], F16) for i in range(2)]
        kp2 = [sb(f"kp2_{i}", [P, S2 + 1], F16) for i in range(2)]
        qp1 = [sb(f"qp1_{i}", [P, S], F16) for i in range(2)]
        qp2 = [sb(f"qp2_{i}", [P, S], F16) for i in range(2)]
        vg = [sb(f"vg_{i}", [P, KT, HG, R]) for i in range(2)]
        pt = [sb(f"pt_{i}", [P, HG, 2, S]) for i in range(2)]
        mx = [sb(f"mx_{i}", [P, QT * HG, 2]) for i in range(2)]
        nm = [sb(f"nm_{i}", [P, QT, HG]) for i in range(2)]
        nmc = [sb(f"nmc_{i}", [P, QT, HG]) for i in range(2)]
        m16 = [sb(f"m16_{i}", [P, QT, 2, HG], F16) for i in range(2)]
        ms = [sb(f"ms_{i}", [2 * HG, S], F16) for i in range(2)]
        mask01 = sb("mask01", [P, QT, S2], F16)
        mask_add = sb("mask_add", [P, QT, 4, S2 // 4 + 1], F16)
        masked = [sb(f"masked_{i}", [P, 2, S2 // 4 + 1], F16) for i in range(2)]
        o_all = sb("o_all", [P, UNITS, S])
        on = sb("on", [P, NT, D])
        on_loc = sb("on_loc", [P, NT, D])
        rec = sb("rec", [P, NT, H])
        rec0 = sb("rec0", [P, NT, H])
        stats = sb("stats", [P, NT, 6])
        mv = sb("mv", [P, NT, 2])
        var_eps = sb("var_eps", [P, NT])
        rstd = sb("rstd", [P, NT])
        minus_half = sb("minus_half", [P, NT])
        tg = sb("tg", [P, 8])
        lgate = sb("lgate", [P, 3])
        wabs = sb("wabs", [P, 2])
        whalf = sb("whalf", [P, 2, 2])
        wfcT = sb("wfcT", [P, HID0])
        wprT = sb("wprT", [P, 4, D])
        dft = sb("dft", [P, 3, P])
        wfreq = sb("wfreq", [P, 2, D])
        a12 = sb("a12", [P, 2, D])
        mfreq = sb("mfreq", [P, D])
        w_up = [sb(f"w_up_{i}", [P, HID1]) for i in range(2)]
        w_dn = [sb(f"w_dn_{i}", [P, 4, D]) for i in range(2)]
        b1_now = [sb(f"b1_now_{i}", [P, 4]) for i in range(2)]
        wr = sb("wr", [P, 2, E1])
        b2 = sb("b2", [E1, 2, D])
        lg = sb("lg", [P, NT, E1])
        lmax = sb("lmax", [P, NT])
        lex = sb("lex", [P, NT, E1])
        lsh = sb("lsh", [P, NT, E1])
        lsum = sb("lsum", [P, NT])
        lrec = sb("lrec", [P, NT])
        prob = sb("prob", [P, NT, E1])
        earlier = sb("earlier", [P, E1, E1])
        rank = sb("rank", [P, NT, E1])
        chosen = sb("chosen", [P, NT, E1])
        comb = sb("comb", [P, NT, E1])
        combT = sb("combT", [E1, TOK])

        early = pt[0][:, :, :, :].rearrange("p a b q -> p (a b q)")
        wraw = early[:, 0:len(TURNED) * D].rearrange("p (k d) -> p k d", d=D)
        early = pt[1][:, :, :, :].rearrange("p a b q -> p (a b q)")
        tern = early[:, 0:2 * HID0].rearrange("p (k d) -> p k d", k=2)
        tern_neg = early[:, 2 * HID0:4 * HID0].rearrange("p (k d) -> p k d", k=2)
        h0 = o_all[:, :, :].rearrange("p u q -> p (u q)").rearrange("p (t n) -> p t n", n=HID0)
        hT = [pt[i][:, :, :, :].rearrange("p c b q -> p c (b q)") for i in range(2)]
        ctx_raw = o_all[:, :, :].rearrange("p u q -> p (u q)")[:, 0:KT * D].rearrange("p (k d) -> p k d", d=D)
        mask8 = kp1[1][:, 0:S2].bitcast(U8).rearrange("p (t n) -> p t n", t=QT)
        wfc_raw = kp1[0][:, 0:2 * HID0].bitcast(F32).rearrange("p (c d) -> p c d", d=D)
        wpr_raw = kp2[0][:, 0:2 * HID0].bitcast(F32)
        gate_in = kp2[1][:, 0:2 * B * KT * 8].bitcast(F32).rearrange("p (b k c) -> p b k c", b=B, k=KT)
        above, tied = [k2c[:, i, 0:2 * NT * E1 * E1].bitcast(F32).rearrange("p (t e j) -> p t e j", t=NT, e=E1)
                       for i in range(2)]
        onT = qf
        acc = on
        ytmp = on_loc

        pa = [ctx.enter_context(nc.psum_tensor(f"score_ring_{i}", [P, 2, 512], F32)) for i in range(2)]
        pe_ = [ctx.enter_context(nc.psum_tensor(f"exp_ring_{i}", [P, 512], F32)) for i in range(3)]
        po = ctx.enter_context(nc.psum_tensor("pv_bank", [P, 512], F32))
        PB = [pa[0][:, 0, :], pa[0][:, 1, :], pa[1][:, 0, :], pa[1][:, 1, :],
              pe_[0][:, :], pe_[1][:, :], pe_[2][:, :], po[:, :]]

        ctxT_d = dram("ctxT_d", [B, P, S2], F32)
        k_d = [dram(f"k_d{r.index}", [UNITS, P, r.nk], F16) for r in RUNS]
        q_d = [dram(f"q_d{l}", [UNITS, P, S], F16) for l in range(4)]

        ld_x, ld_w, ld_cols, ld_rows, ld_mask, ld_gate, ld_misc, ld_fc = [
            sem(n) for n in ("ld_x", "ld_w", "ld_cols", "ld_rows", "ld_mask", "ld_gate", "ld_misc", "ld_fc")]
        consts = sem("consts")
        dconst = sem("dconst")
        padded = sem("padded")
        w_turned, w_kept = sem("w_turned"), sem("w_kept")
        prep_v = sem("prep_v")
        prep_a = sem("prep_a")
        prep_p = sem("prep_p")
        ctx_in, ctx_t, ctx_e = sem("ctx_in"), sem("ctx_t"), sem("ctx_e")
        prep_w, prep_p0, f_rs, r_acc = sem("prep_w"), sem("prep_p0"), sem("f_rs"), sem("r_acc")
        ctx_out, c_ld, k_out, in1, in2, m_in, e_w = [
            [sem(f"{n}_{i}") for i in range(2)] for n in ("ctx_out", "c_ld", "k_out", "in1", "in2", "m_in", "e_w")]
        ln_st, ln_mv, ln_ve, ln_rs, ln_xn, ln_t, ln_xt = [
            sem(n) for n in ("ln_st", "ln_mv", "ln_ve", "ln_rs", "ln_xn", "ln_t", "ln_xt")]
        q_ps, q_f, q_1, q_2, q_out = [sem(n) for n in ("q_ps", "q_f", "q_1", "q_2", "q_out")]
        k_ps, v_ps, k_1, k_2, v_ok, v_gated = [sem(n) for n in ("k_ps", "v_ps", "k_1", "k_2", "v_ok", "v_gated")]
        lk_ps, lk_1, lk_2, lk_out, lv_ok = [sem(n) for n in ("lk_ps", "lk_1", "lk_2", "lk_out", "lv_ok")]
        score, score_free = sem("score"), sem("score_free")
        mx_done, m_ok = sem("mx_done"), sem("m_ok")
        fill, exped = sem("fill"), sem("exped")
        pv, o_ok, vg_ok = sem("pv"), sem("o_ok"), sem("vg_ok")
        o_t, o_rec, o_n, o_add, on_t, on_e, y_ps, y_t, x_ok = [
            sem(n) for n in ("o_t", "o_rec", "o_n", "o_add", "on_t", "on_e", "y_ps", "y_t", "x_ok")]
        f_up, f_act, f_st, f_n, f_t, f_ht, f_dn, f_x = [
            sem(n) for n in ("f_up", "f_act", "f_st", "f_n", "f_t", "f_ht", "f_dn", "f_x")]
        r_ps, r_v, r_a, r_ct, r_cc, r_b = [sem(n) for n in ("r_ps", "r_v", "r_a", "r_ct", "r_cc", "r_b")]
        e_up, e_act, e_dn, e_acc, e_b = [sem(n) for n in ("e_up", "e_act", "e_dn", "e_acc", "e_b")]
        stored, passed = sem("stored"), sem("passed")

        block = ctx.enter_context(nc.Block())
        sq = lambda name: wsq[:, SQ[name], :]
        col = lambda name, k=0: cols[:, (COL[name] if name else ZCOL) + k:(COL[name] if name else ZCOL) + k + 1]
        row = lambda name, n: spread[:, ROW[name or "zero"]:ROW[name or "zero"] + n]
        over = lambda ap, n: ap.unsqueeze(1).broadcast_to([P, n, ap.shape[-1]])

        parts = [l for l in range(4) if l < last]
        ffns = [l for l in range(4) if l + 0.5 < last]
        done = [r for r in RUNS if r.layer in parts]
        LN_T, LN_X = NT, 2

        def ln_at(layer, ffn):
            return 2 * layer + ffn

        def bases(n):
            return 16 * n

        units = range(UNITS)

        @block.sync
        def _(sp):
            sp.dma_start(x[:, :, :], a["x"].rearrange("b (t p) d -> p (b t) d", p=P)).then_inc(ld_x, 16)
            for b in range(B):
                if b:
                    sp.wait_ge(ctx_t, 4 * b)
                sp.dma_start(ctx_raw[:, 0:FULL, :],
                             a["ctx_1024"][b, 0:FULL * P, :].rearrange("(t p) d -> p t d", p=P)).then_inc(ctx_in, 16)
                sp.dma_start(ctx_raw[0:TAIL, FULL, :], a["ctx_1024"][b, FULL * P:S2, :]).then_inc(ctx_in, 16)
                if b:
                    sp.wait_ge(ctx_e, 4 * b)
                    sp.dma_start(ctxT_d[b - 1], ctxT[:, (b - 1) % 2, :]).then_inc(ctx_out[(b - 1) % 2], 16)
            sp.wait_ge(ctx_e, 4 * B)
            sp.dma_start(ctxT_d[B - 1], ctxT[:, (B - 1) % 2, :]).then_inc(ctx_out[(B - 1) % 2], 16)
            sp.wait_ge(dconst, 1)
            for r in RUNS:
                for b in range(B):
                    sp.dma_start(k_d[r.index][4 * b:4 * b + 4].rearrange("g (i r) n -> (g i) r n", r=R)[:, KQ:R, :],
                                 one16[:, 0:r.nk]).then_inc(padded, 16)
            for l in range(4):
                for b in range(B):
                    sp.dma_start(q_d[l][4 * b:4 * b + 4].rearrange("g (i r) n -> (g i) r n", r=R)[:, KQ:R, :],
                                 one16[:, 0:S]).then_inc(padded, 16)
            sp.wait_ge(padded, 16 * B * (len(RUNS) + 4))
            for i in range(2):
                sp.wait_ge(ctx_out[i], 16 * B // 2)

            def split_rows(dst, b, part):
                v = dst[4 * b:4 * b + 4].rearrange("g (i r) n -> (g i) r n", r=R)
                return v[:, DH * part:DH * part + DH, :]

            def k_prep(r):
                g = r.ctx
                for b in range(B):
                    n = B * g + b
                    if n >= 2:
                        sp.wait_ge(k_ps, 4 * (n - 1))
                        sp.wait_ge(v_ps, 4 * (n - 1))
                    sp.dma_start(ctxT[:, b % 2, :], ctxT_d[b]).then_inc(c_ld[b % 2], 16)
                    if b:
                        k_store(r, g, b - 1)
                k_store(r, g, B - 1)

            def k_store(r, g, b):
                n = B * g + b
                sp.wait_ge(k_1, 4 * (n + 1))
                for part in (0, 2):
                    sp.dma_start(split_rows(k_d[r.index], b, part), k1c[:, b % 2, 0:S2]).then_inc(k_out[b % 2], 16)
                sp.wait_ge(k_2, 4 * (n + 1))
                sp.dma_start(split_rows(k_d[r.index], b, 1), k2c[:, b % 2, 0:S2]).then_inc(k_out[b % 2], 16)

            def q_store(l):
                sp.wait_ge(q_2, 2 * (l + 1))
                for b in range(B):
                    for part, src in ((0, q1c), (1, q1c), (2, q2c)):
                        sp.dma_start(split_rows(q_d[l], b, part), src[:, b * S:b * S + S]).then_inc(q_out, 16)
                sp.wait_ge(q_out, 16 * 12 * (l + 1))

            def local_store():
                sp.wait_ge(lk_2, 2)
                for b in range(B):
                    for part, src in ((0, k1c), (2, k1c), (1, k2c)):
                        sp.dma_start(split_rows(k_d[LOCAL], b, part), src[:, 0, b * S:b * S + S]).then_inc(lk_out, 16)
                sp.wait_ge(lk_out, 16 * 12)

            def loads(r):
                kd, qd = k_d[r.index], q_d[r.layer]

                def pass1(n, par):
                    sp.dma_start(kp1[par][:, 0:r.nk], kd[n]).then_inc(in1[par], 16)
                    sp.dma_start(qp1[par][:, :], qd[n]).then_inc(in1[par], 16)

                def pass2(n, par):
                    sp.dma_start(kp2[par][:, 0:r.nk], kd[n]).then_inc(in2[par], 16)
                    sp.dma_start(qp2[par][:, :], qd[n]).then_inc(in2[par], 16)

                def maxima(n, par):
                    sp.wait_ge(in2[par], 16 * (r.u0 + n - par + 2))
                    sp.wait_ge(score_free, 2 + r.use0 + (n + 1) * r.uses)
                    for part in range(2):
                        sp.dma_start(qp2[par][KQ + part:KQ + part + R * (HG - 1) + 1:R, :],
                                     ms[par][HG * part:HG * part + HG, :]).then_inc(m_in[par], 16)

                def unit(n, par, p1=True, p2=True):
                    maxima(n, par)
                    if p1:
                        pass1(n + 2, par)
                    if p2:
                        sp.wait_ge(fill, r.fill0 + n * r.fills)
                        pass2(n + 1, 1 - par)

                pass1(0, 0)
                pass1(1, 1)
                pass2(0, 0)
                maxima(0, 0)
                pass1(2, 0)
                pass2(1, 1)
                with sp.Fori(0, (UNITS - 4) // 2) as t:
                    unit(2 * t + 1, 1)
                    unit(2 * t + 2, 0)
                unit(UNITS - 3, 1)
                unit(UNITS - 2, 0, p1=False)
                unit(UNITS - 1, 1, p1=False, p2=False)

            def experts(l, which, w_up_d, w_dn_d, hid):
                cc = hid // P
                with sp.Fori(0, E1 // 2) as t:
                    for k in range(2):
                        sp.wait_ge(e_dn, FREE_HID + 2 * E1 * which + 2 * (2 * t + k) - 2)
                        sp.dma_start(w_up[k][:, 0:hid], w_up_d[2 * t + k]).then_inc(e_w[k], 16)
                        sp.dma_start(w_dn[k][:, 0:cc, :],
                                     w_dn_d[2 * t + k].rearrange("(c p) d -> p c d", p=P)).then_inc(e_w[k], 16)

            for l in parts:
                for r in done:
                    if r.layer == l and not r.local:
                        k_prep(r)
                        for i in range(2):
                            sp.wait_ge(k_out[i], 48 * (B // 2) * (r.ctx + 1))
                q_store(l)
                if l == 1:
                    local_store()
                for r in done:
                    if r.layer == l:
                        loads(r)
                if l in ffns and l == 1:
                    experts(l, 0, a["L1_ffn_W1"], a["L1_ffn_W2"], HID1)
                if l in ffns and l == 3:
                    experts(l, 1, a["L3_ffn_w1"], a["L3_ffn_w2"], HID3)
            sp.wait_ge(x_ok, NT * len(parts) + NT * len(ffns))
            sp.dma_start(out.rearrange("b (t p) d -> p (b t) d", p=P), x[:, :, :]).then_inc(stored, 16)
            sp.wait_ge(stored, 16)

        @block.gpsimd
        def _(pool):
            pool.memset(ident[:, :], 0.0).then_inc(consts, 1)
            pool.memset(ident16[:, :], 0.0).then_inc(consts, 1)
            pool.memset(mask_eye[:, :], 0.0).then_inc(consts, 1)
            pool.memset(earlier[:, :, :], 1.0).then_inc(consts, 1)
            pool.wait_ge(consts, 4)
            for m, v in ((ident, 1.0), (ident16, 1.0), (mask_eye, -BIG)):
                pool.affine_select(out=m[:, :], in_=m[:, :], compare_op=ALU.not_equal, fill=v, base=0,
                                   pattern=[[-1, P]], channel_multiplier=1).then_inc(consts, 1)
            pool.affine_select(out=earlier[:, :, :], in_=earlier[:, :, :], compare_op=ALU.is_gt, fill=0.0, base=0,
                               pattern=[[1, E1], [-1, E1]], channel_multiplier=0).then_inc(consts, 1)
            pool.memset(ones[:, :], 1.0).then_inc(consts, 1)
            pool.memset(minus_half[:, :], -0.5).then_inc(consts, 1)
            for i in range(2):
                pool.memset(vg[i][:, :, :, :], 1.0).then_inc(consts, 1)
            for i, (name, turned) in enumerate(SQUARE):
                dst = wraw[:, TURNED.index(i), :] if turned else wsq[:, i, :]
                pool.dma_start(dst, a[name]).then_inc(ld_w, 16)

            def norm(s):
                pool.wait_ge(ln_mv, NT * (s + 1))
                pool.tensor_scalar(var_eps[:, :], mv[:, :, 1], LN_EPS, None, ALU.add).then_inc(ln_ve, 1)
                pool.wait_ge(ln_ve, s + 1)
                pool.tensor_tensor(rstd[:, :], var_eps[:, :], minus_half[:, :], ALU.pow).then_inc(ln_rs, 1)

            def expert_bias(which, hid, bcol):
                cc = hid // P
                biases = cols[:, COL[bcol]:COL[bcol] + E1 * cc].rearrange("p (e c) -> p e c", c=cc)
                with pool.Fori(0, E1 // 2) as t:
                    for k in range(2):
                        pool.wait_ge(e_dn, FREE_HID + 2 * E1 * which + 2 * (2 * t + k) - 2)
                        pool.tensor_copy(b1_now[k][:, 0:cc], biases[:, 2 * t + k, :]).then_inc(e_b, 1)

            def unit_v(r):
                v = v_loc if r.local else v_all
                if r.local:
                    pool.wait_ge(lv_ok, NT)
                elif r.layer == 0:
                    pool.wait_ge(v_gated, B)
                else:
                    pool.wait_ge(v_ok, 4 * B * (r.ctx + 1))

                def copy(b, g, par):
                    pool.tensor_copy(vg[par][:, 0:r.kt, :, 0:DH],
                                     v[:, b, :, R * g:R * g + R].rearrange("p k (j d) -> p k j d", d=DH)
                                     ).then_inc(vg_ok, 1)

                for g in range(2):
                    if r.u0:
                        pool.wait_ge(pv, FREE_PT + r.step0)
                    copy(0, g, g)
                for g in range(2, 4):
                    pool.wait_ge(pv, FREE_PT + r.step0 + (g - 1) * r.steps)
                    copy(0, g, g % 2)
                with pool.Fori(1, B) as b:
                    for g in range(4):
                        pool.wait_ge(pv, FREE_PT + r.step0 + (4 * b + g - 1) * r.steps)
                        copy(b, g, g % 2)

            for l in parts:
                if l == 0:
                    pool.wait_ge(prep_v, 3)
                    for b in range(B):
                        pool.wait_ge(v_ok, 4 * (b + 1))
                        pool.tensor_tensor(v_all[:, b, :, :], v_all[:, b, :, :],
                                           gate[:, b, :].unsqueeze(2).broadcast_to([P, KT, VW]),
                                           ALU.mult).then_inc(v_gated, 1)
                norm(ln_at(l, 0))
                for r in done:
                    if r.layer == l:
                        unit_v(r)
                if l == 1:
                    pool.wait_ge(o_n, NT * 3)
                    pool.tensor_tensor(on[:, :, :], on[:, :, :], on_loc[:, :, :], ALU.add).then_inc(o_add, 1)
                if l in ffns:
                    norm(ln_at(l, 1))
                    if l in (1, 3):
                        expert_bias(l // 2, HID1 if l == 1 else HID3, "L1_ffn_b1" if l == 1 else "L3_ffn_b1")
                    if l == 0:
                        pool.wait_ge(f_rs, 1)
                        pool.tensor_tensor(rstd[:, :], var_eps[:, :], minus_half[:, :], ALU.pow).then_inc(f_rs, 1)

        @block.scalar
        def _(act):
            act.sem_inc(exped, FREE_EXP)
            act.sem_inc(o_ok, FREE_PV)
            act.sem_inc(e_act, FREE_UP)
            act.dma_start(mask8[:, :, :], a["mask_1x1xSxS2_bk1"].rearrange("a b (t p) n -> p (a b t) n", p=P)
                          ).then_inc(ld_mask, 16)
            act.dma_start(wfc_raw[:, :, :], a["L0_ffn_W_fc"].rearrange("(c p) d -> p c d", p=P)).then_inc(ld_fc, 16)
            act.dma_start(wpr_raw[:, :], a["L0_ffn_W_proj"]).then_inc(ld_fc, 16)
            act.wait_ge(dconst, 4)
            for name, k in COLS:
                src = a[name]
                if len(src.shape) == 2:
                    src = src.rearrange("e (c p) -> (e c) p", p=P)
                else:
                    src = src.rearrange("(c p) -> c p", p=P)
                act.dma_start(cols_raw[COL[name]:COL[name] + k, :], src).then_inc(ld_cols, 16)
            for name, k in ROWS:
                if name != "zero":
                    src = a[name]
                    src = src.rearrange("(a n) -> a n", a=1) if len(src.shape) == 1 else src
                    act.dma_start(rows[0:1, ROW[name]:ROW[name] + k], src).then_inc(ld_rows, 16)
            for b in range(B):
                act.dma_start(gate_in[:, b, 0:FULL, :],
                              a["ctxb_2048x8"][b, 0:FULL * P, :].rearrange("(t p) c -> p t c", p=P)
                              ).then_inc(ld_gate, 16)
                act.dma_start(gate_in[0:TAIL, b, FULL, :], a["ctxb_2048x8"][b, FULL * P:S2, :]).then_inc(ld_gate, 16)
            for k, name in enumerate(("dft_cos", "dft_sin", "dft_nsin")):
                act.dma_start(dft[:, k, :], a[name]).then_inc(ld_misc, 16)
            act.dma_start(wfreq[:, 0, :], a["L2_ffn_w_freq_real"]).then_inc(ld_misc, 16)
            act.dma_start(wfreq[:, 1, :], a["L2_ffn_w_freq_imag"]).then_inc(ld_misc, 16)
            act.dma_start(wr[:, 0, :], a["L1_ffn_Wr"]).then_inc(ld_misc, 16)
            act.dma_start(wr[:, 1, :], a["L3_ffn_gate_w"]).then_inc(ld_misc, 16)
            act.dma_start(b2[:, 0, :], a["L1_ffn_b2"]).then_inc(ld_misc, 16)
            act.dma_start(b2[:, 1, :], a["L3_ffn_b2"]).then_inc(ld_misc, 16)
            for m in range(0, len(TURNED), 4):
                k = min(4, len(TURNED) - m)
                act.wait_ge(w_turned, m // 4 + 1)
                act.activation(wsq[:, TURNED[m]:TURNED[m] + k, :], PB[m // 4][:, 0:k * D].rearrange(
                    "p (k d) -> p k d", k=k), ACT.Copy).then_inc(w_kept, 1)
            act.wait_ge(prep_p, 1)
            act.activation(cols[:, :], PB[4][:, 0:NCOL], ACT.Copy).then_inc(prep_a, 1)
            act.wait_ge(prep_p, 2)
            act.activation(spread[:, 0:512], PB[5], ACT.Copy).then_inc(prep_a, 1)
            act.wait_ge(prep_p, 3)
            act.activation(spread[:, 512:NROW], PB[6][:, 0:NROW - 512], ACT.Copy).then_inc(prep_a, 1)
            act.wait_ge(prep_a, 3)
            act.activation(tg[:, :], spread[:, ROW["g_xattn"]:ROW["g_xattn"] + 8], ACT.Tanh).then_inc(prep_a, 1)
            act.activation(lgate[:, 0:1], row("L1_xattn_gate", 1), ACT.Exp, scale=-1.0).then_inc(prep_a, 1)
            act.wait_ge(prep_v, 1)
            act.activation(gate_e[:, :, :], gate[:, :, :], ACT.Exp, scale=-10.0 / 8, bias=1.0).then_inc(prep_a, 1)
            act.wait_ge(prep_p, 4)
            act.activation(wfcT[:, :], PB[7], ACT.Copy).then_inc(prep_a, 1)
            act.wait_ge(prep_p, 5)
            act.activation(wprT[:, :, :], PB[4].rearrange("p (c d) -> p c d", c=4), ACT.Copy).then_inc(prep_a, 1)
            act.wait_ge(prep_p, 6)
            act.activation(a12[:, :, :], PB[5][:, 0:2 * D].rearrange("p (k d) -> p k d", k=2), ACT.Copy
                           ).then_inc(prep_a, 1)
            act.wait_ge(prep_p, 7)
            act.activation(mfreq[:, :], PB[6][:, 0:D], ACT.Copy, scale=1.0 / D).then_inc(prep_a, 1)
            for b in range(B):
                if b >= 2:
                    act.wait_ge(ctx_out[b % 2], 16 * (b // 2))
                for m in range(4):
                    k = min(4 * P, S2 - m * 4 * P)
                    act.wait_ge(ctx_t, 4 * b + m + 1)
                    act.activation(ctxT[:, b % 2, m * 4 * P:m * 4 * P + k], PB[m][:, 0:k], ACT.Copy
                                   ).then_inc(ctx_e, 1)

            def normT(s):
                for m in range(2):
                    act.wait_ge(ln_t, 2 * s + m + 1)
                    act.activation(xnT[:, m * 512:m * 512 + 512], PB[m], ACT.Copy).then_inc(ln_xt, 1)

            def k_split(r):
                g = r.ctx
                w = S2 // 4
                for b in range(B):
                    n = B * g + b
                    if n >= 2:
                        act.wait_ge(k_out[b % 2], 48 * (n // 2))
                    for c in range(4):
                        lo = c * w + min(c, 1)
                        act.wait_ge(k_ps, 4 * n + c + 1)
                        act.activation(k1c[:, b % 2, lo:lo + w + (c == 0)], PB[c][:, 0:w + (c == 0)], ACT.Identity,
                                       bias=col(BK[r.index])).then_inc(k_1, 1)

            def q_split(l):
                for m in range(2):
                    act.wait_ge(q_f, 2 * l + m + 1)
                    if l:
                        act.wait_ge(q_out, 16 * 12 * l)
                    act.activation(q1c[:, m * 512:m * 512 + 512], qf[:, m * 512:m * 512 + 512], ACT.Copy
                                   ).then_inc(q_1, 1)

            def local_split():
                for i in range(2):
                    act.wait_ge(k_out[i], 48 * (B // 2) * 2)
                for m in range(2):
                    act.wait_ge(lk_ps, m + 1)
                    act.activation(k1c[:, 0, m * 512:m * 512 + 512], PB[2 + m], ACT.Identity,
                                   bias=col(BK[LOCAL])).then_inc(lk_1, 1)

            def attention(r):
                def evac(n):
                    act.wait_ge(pv, FREE_PT + r.step0 + (n + 1) * r.steps)
                    act.activation(o_all[:, n, :], po[:, 0:S], ACT.Copy).then_inc(o_ok, 1)

                def unit(n, par, prev=True):
                    for s in range(r.steps):
                        tiles = r.tiles(s)
                        rows_, cols_ = tiles[0][1], S * len(tiles)
                        g = par * r.steps + s
                        act.wait_ge(pv, r.step0 + n * r.steps + s + 1)
                        for i in range(HG):
                            act.wait_ge(fill, r.fill0 + n * r.fills + HG * s + i + 1)
                            bank = pe_[(par * r.fills + HG * s + i) % 3]
                            act.activation(pt[g % 2][0:rows_, i, 0:len(tiles), :],
                                           bank[0:rows_, 0:cols_].rearrange("p (k q) -> p k q", q=S),
                                           ACT.Exp).then_inc(exped, 1)
                        if s == 0 and prev:
                            evac(n - 1)

                unit(0, 0, prev=False)
                with act.Fori(0, UNITS // 2 - 1) as t:
                    unit(2 * t + 1, 1)
                    unit(2 * t + 2, 0)
                unit(UNITS - 1, 1)
                evac(UNITS - 1)

            def post(l):
                for m in range(2):
                    act.wait_ge(on_t, 2 * l + m + 1)
                    act.activation(onT[:, m * 512:m * 512 + 512], PB[4 + m], ACT.Copy).then_inc(on_e, 1)

            def ffn0():
                for T in range(NT):
                    act.wait_ge(f_up, T + 1)
                    act.activation(h0[:, T, :], PB[2 + T % 4], ACT.Gelu).then_inc(f_act, 1)
                for m in range(2):
                    for c in range(4):
                        act.wait_ge(f_t, 4 * m + c + 1)
                        act.activation(hT[m][:, c, :], PB[c], ACT.Identity, scale=col("L0_ffn_ln_w", c),
                                       bias=col("L0_ffn_ln_b", c)).then_inc(f_ht, 1)

            def route(which):
                act.wait_ge(r_v, ROUTE_V[which][0])
                act.activation(lex[:, :, :], lsh[:, :, :], ACT.Exp).then_inc(r_a, 1)
                for m in range(2):
                    act.wait_ge(r_ct, 2 * which + m + 1)
                    act.activation(combT[:, m * 512:m * 512 + 512], PB[2 + m][0:E1, :], ACT.Copy).then_inc(r_cc, 1)

            def experts(which, hid, func):
                cc = hid // P
                up0 = which and 2 * E1 * (HID1 // P)
                with act.Fori(0, E1 // 2) as t:
                    for k in range(2):
                        act.wait_ge(e_b, E1 * which + 2 * t + k + 1)
                        for hf in range(2):
                            act.wait_ge(e_dn, FREE_HID + 2 * E1 * which + 2 * (2 * t + k) + hf - 1)
                            for c in range(cc):
                                act.wait_ge(e_up, up0 + (2 * t + k) * 2 * cc + hf * cc + c + 1)
                                act.activation(hT[hf][:, c, :], PB[(hf * cc + c) % 4], func, bias=b1_now[k][:, c:c + 1]).then_inc(e_act, 1)

            for l in parts:
                for r in done:
                    if r.layer == l and not r.local:
                        k_split(r)
                normT(ln_at(l, 0))
                q_split(l)
                if l == 1:
                    local_split()
                for r in done:
                    if r.layer == l:
                        attention(r)
                post(l)
                if l in ffns:
                    normT(ln_at(l, 1))
                    if l == 0:
                        ffn0()
                    if l == 1:
                        route(0)
                        experts(0, HID1, ACT.Gelu)
                    if l == 3:
                        route(1)
                        experts(1, HID3, ACT.Relu)

        @block.vector
        def _(dve):
            dve.memset(one16[:, :], 1.0).then_inc(dconst, 1)
            dve.memset(cols_raw[:, :], 0.0).then_inc(dconst, 1)
            dve.memset(rows[0:1, :], 0.0).then_inc(dconst, 1)
            dve.memset(gate_in[:, :, :, :], 0.0).then_inc(dconst, 1)
            dve.memset(v_all[:, :, FULL, :], 0.0).then_inc(dconst, 1)
            dve.wait_ge(dconst, 5)
            dve.wait_ge(ld_fc, 32)
            dve.tensor_reduce(wabs[:, 0:1], wfc_raw[:, :, :].rearrange("p c d -> p (c d)"), AX.X, ALU.add,
                              apply_absolute_value=True).then_inc(prep_w, 1)
            dve.tensor_reduce(wabs[:, 1:2], wpr_raw[:, :], AX.X, ALU.add, apply_absolute_value=True).then_inc(prep_w, 1)
            dve.wait_ge(prep_p0, 1)
            half = 0.5 / (HID0 * D)
            dve.tensor_scalar(whalf[:, 0, :], PB[7][:, 0:2], half, 0.5e-6, ALU.mult, ALU.add).then_inc(prep_w, 1)
            dve.wait_ge(prep_w, 3)
            dve.tensor_scalar(whalf[:, 1, :], whalf[:, 0, :], -1.0, None, ALU.mult).then_inc(prep_w, 1)
            dve.wait_ge(prep_w, 4)
            for k, src in enumerate((wfc_raw[:, :, :].rearrange("p c d -> p (c d)"), wpr_raw[:, :])):
                dve.tensor_scalar(tern[:, k, :], src, whalf[:, 0, k:k + 1], None, ALU.is_gt).then_inc(prep_w, 1)
                dve.tensor_scalar(tern_neg[:, k, :], src, whalf[:, 1, k:k + 1], None, ALU.is_lt).then_inc(prep_w, 1)
            dve.wait_ge(prep_w, 8)
            for k in range(2):
                dve.tensor_tensor(tern[:, k, :], tern[:, k, :], tern_neg[:, k, :], ALU.subtract).then_inc(prep_w, 1)
            dve.wait_ge(ld_gate, 32 * B)
            dve.tensor_reduce(gate[:, :, :], gate_in[:, :, :, :], AX.X, ALU.add, apply_absolute_value=True
                              ).then_inc(prep_v, 1)
            dve.wait_ge(prep_a, 6)
            dve.tensor_scalar(gate_e[:, :, :], gate_e[:, :, :], 1.0, None, ALU.add).then_inc(prep_v, 1)
            dve.wait_ge(prep_v, 2)
            dve.reciprocal(gate[:, :, :], gate_e[:, :, :]).then_inc(prep_v, 1)
            dve.tensor_scalar(lgate[:, 1:2], lgate[:, 0:1], 1.0, None, ALU.add).then_inc(prep_v, 1)
            dve.wait_ge(prep_v, 4)
            dve.reciprocal(lgate[:, 0:1], lgate[:, 1:2]).then_inc(prep_v, 1)
            dve.wait_ge(prep_v, 5)
            dve.tensor_scalar(lgate[:, 2:3], lgate[:, 0:1], -1.0, 1.0, ALU.mult, ALU.add).then_inc(prep_v, 1)
            dve.wait_ge(ld_mask, 16)
            dve.tensor_copy(mask01[:, :, :], mask8[:, :, :]).then_inc(prep_v, 1)
            for c, (lo, w, nb) in enumerate(chunk_cols(S2)):
                for z in range(nb):
                    at = lo + z * (S2 // 4)
                    dve.tensor_scalar(mask_add[:, :, 2 * c + z, 0:w], mask8[:, :, at:at + w], -BIG, None, ALU.mult
                                      ).then_inc(prep_v, 1)
            dve.wait_ge(prep_v, 11)
            dve.sem_inc(score_free, FREE_SCORE)
            dve.sem_inc(e_acc, FREE_ACC)
            dve.wait_ge(ld_x, 16)

            def norm(s):
                if s:
                    dve.wait_ge(x_ok, NT * s)
                for T in range(NT):
                    dve.bn_stats(stats[:, T, :], x[:, T, :]).then_inc(ln_st, 1)
                for T in range(NT):
                    dve.wait_ge(ln_st, NT * s + T + 1)
                    dve.bn_aggr(mv[:, T, :], stats[:, T, :]).then_inc(ln_mv, 1)
                dve.wait_ge(ln_rs, s + 1)
                for T in range(NT):
                    dve.tensor_scalar(xn[:, T, :], x[:, T, :], mv[:, T, 0:1], rstd[:, T:T + 1],
                                      ALU.subtract, ALU.mult).then_inc(ln_xn, 1)

            def k_split(r):
                g = r.ctx
                w = S2 // 4
                for b in range(B):
                    n = B * g + b
                    if n >= 2:
                        dve.wait_ge(k_out[b % 2], 48 * (n // 2))
                    for c in range(4):
                        lo = c * w + min(c, 1)
                        hi = lo + w + (c == 0)
                        dve.wait_ge(k_1, 4 * n + c + 1)
                        dve.scalar_tensor_tensor(out=k2c[:, b % 2, lo:hi], in0=PB[c][:, 0:hi - lo],
                                                 scalar=col(BK[r.index]), in1=k1c[:, b % 2, lo:hi],
                                                 op0=ALU.add, op1=ALU.subtract).then_inc(k_2, 1)
                    for c in range(4):
                        k = 4 if c < 3 else 1
                        pr = P if c < 3 else TAIL
                        dve.wait_ge(v_ps, 4 * n + c + 1)
                        dve.tensor_tensor(v_all[0:pr, b, 4 * c:4 * c + k, :],
                                          PB[4 + c][0:pr, 0:k * VW].rearrange("p (k d) -> p k d", k=k),
                                          row(BV[r.index], D)[0:pr].unsqueeze(1).broadcast_to([pr, k, D]),
                                          ALU.add).then_inc(v_ok, 1)

            def q_split(l):
                if l:
                    dve.wait_ge(q_2, 2 * l)
                for m in range(2):
                    sl = slice(m * 512, m * 512 + 512)
                    dve.wait_ge(q_ps, 2 * l + m + 1)
                    dve.tensor_scalar(qf[:, sl], PB[2 + m], col(BQ[l]), SCALE, ALU.add, ALU.mult).then_inc(q_f, 1)
                for m in range(2):
                    sl = slice(m * 512, m * 512 + 512)
                    dve.wait_ge(q_1, 2 * l + m + 1)
                    dve.tensor_tensor(q2c[:, sl], qf[:, sl], q1c[:, sl], ALU.subtract).then_inc(q_2, 1)

            def local_split():
                for m in range(2):
                    sl = slice(m * 512, m * 512 + 512)
                    dve.wait_ge(lk_1, m + 1)
                    dve.scalar_tensor_tensor(out=k2c[:, 0, sl], in0=PB[2 + m], scalar=col(BK[LOCAL]),
                                             in1=k1c[:, 0, sl], op0=ALU.add, op1=ALU.subtract).then_inc(lk_2, 1)
                for m in range(2):
                    dve.wait_ge(lk_ps, 3 + m)
                    dve.tensor_tensor(v_loc[:, 2 * m:2 * m + 2, :, :],
                                      PB[4 + m].rearrange("p (b k d) -> p b k d", b=2, k=2),
                                      row(BV[LOCAL], D).unsqueeze(1).unsqueeze(1).broadcast_to([P, 2, 2, D]),
                                      ALU.add).then_inc(lv_ok, 4)

            def attention(r):
                cpt = len(r.chunks)

                def unit(n, par):
                    use = r.use0 + n * r.uses
                    for k in range(r.c):
                        qt, c, i = k // (cpt * HG), k // HG % cpt, k % HG
                        lo, w, nb = r.chunks[c]
                        src = pa[(par + k) % 2][:, 0:nb, 0:w]
                        dst = mx[par][:, qt * HG + i, c:c + 1]
                        dve.wait_ge(score, use + k + 1)
                        if r.mask:
                            dve.wait_ge(score_free, use + k + 1)
                            dve.sem_inc(passed, 1)
                            dve.tensor_tensor_reduce(
                                out=masked[k % 2][:, :, 0:w], in0=src,
                                in1=mask_add[:, qt, 2 * c:2 * c + 2, 0:w],
                                scale=1.0, scalar=-3.0e38, op0=ALU.add, op1=ALU.max,
                                accum_out=dst).then_inc(score_free, 1)
                        else:
                            dve.tensor_reduce(dst, src, AX.XY, ALU.max).then_inc(score_free, 1)
                    dve.wait_ge(score_free, 2 + use + r.c)
                    dve.tensor_reduce(nm[par][:, :, :].rearrange("p q i -> p (q i)"), mx[par][:, :, 0:cpt], AX.X,
                                      ALU.max, negate=True).then_inc(mx_done, 1)
                    dve.wait_ge(mx_done, 2 * (r.u0 + n) + 1)
                    dve.tensor_scalar(nmc[par][:, :, :], nm[par][:, :, :], -MIN_MAX if r.mask else 3.0e38, None,
                                      ALU.min).then_inc(mx_done, 1)
                    dve.wait_ge(mx_done, 2 * (r.u0 + n) + 2)
                    dve.tensor_copy(m16[par][:, :, 0, :], nmc[par][:, :, :]).then_inc(m_ok, 1)
                    dve.wait_ge(m_ok, 2 * (r.u0 + n) + 1)
                    dve.tensor_tensor(m16[par][:, :, 1, :], nmc[par][:, :, :], m16[par][:, :, 0, :],
                                      ALU.subtract).then_inc(m_ok, 1)
                    dve.wait_ge(score, use + r.c + 1)
                    dve.tensor_copy(ms[par][:, :], pa[(par + r.c) % 2][:, 0, :].bitcast(F16)[0:2 * HG, 0:S]
                                    ).then_inc(score_free, 1)

                with dve.Fori(0, UNITS // 2) as t:
                    unit(2 * t, 0)
                    unit(2 * t + 1, 1)

            def heads_out(r):
                dst = on_loc if r.local else on
                for T in range(NT):
                    n = NT * r.index + T
                    bank = PB[T % 4].rearrange("p (h c) -> p h c", c=R)
                    dve.wait_ge(o_t, n + 1)
                    dve.tensor_scalar(rec0[:, T, :], bank[:, :, DH], TINY, None, ALU.max).then_inc(o_rec, 1)
                    dve.wait_ge(o_rec, 2 * n + 1)
                    dve.reciprocal(rec[:, T, :], rec0[:, T, :]).then_inc(o_rec, 1)
                    dve.wait_ge(o_rec, 2 * n + 2)
                    coef = 1.0 if r.layer != 1 else lgate[:, 0:1] if r.local else lgate[:, 2:3]
                    dve.scalar_tensor_tensor(
                        out=dst[:, T, :].rearrange("p (h d) -> p h d", d=DH), in0=bank[:, :, 0:DH], scalar=coef,
                        in1=rec[:, T, :].unsqueeze(2).broadcast_to([P, H, DH]), op0=ALU.mult, op1=ALU.mult
                        ).then_inc(o_n, 1)

            def residual(s, bank_of, bias, gate_col, ready, at):
                for m in range(2):
                    dve.wait_ge(ready, at + m + 1)
                    dve.tensor_tensor(ytmp[:, 4 * m:4 * m + 4, :], PB[bank_of + m].rearrange("p (k d) -> p k d", k=4),
                                      row(bias, D).unsqueeze(1).broadcast_to([P, 4, D]), ALU.add).then_inc(y_t, 1)
                    dve.wait_ge(y_t, 2 * s + m + 1)
                    dve.scalar_tensor_tensor(out=x[:, 4 * m:4 * m + 4, :], in0=ytmp[:, 4 * m:4 * m + 4, :],
                                             scalar=tg[:, gate_col:gate_col + 1], in1=x[:, 4 * m:4 * m + 4, :],
                                             op0=ALU.mult, op1=ALU.add).then_inc(x_ok, 4)

            def ffn0():
                for T in range(NT):
                    dve.wait_ge(f_act, T + 1)
                    dve.bn_stats(stats[:, T, :], h0[:, T, :]).then_inc(f_st, 1)
                    dve.wait_ge(f_st, 2 * T + 1)
                    dve.bn_aggr(mv[:, T, :], stats[:, T, :]).then_inc(f_st, 1)
                dve.wait_ge(f_st, 2 * NT)
                dve.tensor_scalar(var_eps[:, :], mv[:, :, 1], LN_EPS, None, ALU.add).then_inc(f_rs, 1)
                dve.wait_ge(f_rs, 2)
                for T in range(NT):
                    dve.tensor_scalar(h0[:, T, :], h0[:, T, :], mv[:, T, 0:1], rstd[:, T:T + 1],
                                      ALU.subtract, ALU.mult).then_inc(f_n, 1)

            def route(which):
                cnt = [ROUTE_V[which][2]]

                def step(ins, n=1):
                    ins.then_inc(r_v, 1)
                    cnt[0] += 1

                dve.wait_ge(r_ps, which + 1)
                step(dve.tensor_tensor(lg[:, :, :], PB[2][:, 0:NT * E1].rearrange("p (t e) -> p t e", e=E1),
                                       (row("L3_ffn_gate_b", E1) if which else row("zero", E1)
                                        ).unsqueeze(1).broadcast_to([P, NT, E1]), ALU.add))
                dve.wait_ge(r_v, cnt[0])
                step(dve.tensor_reduce(lmax[:, :], lg[:, :, :], AX.X, ALU.max))
                dve.wait_ge(r_v, cnt[0])
                step(dve.tensor_tensor(lsh[:, :, :], lg[:, :, :], lmax[:, :].unsqueeze(2).broadcast_to([P, NT, E1]),
                                       ALU.subtract))
                assert cnt[0] == ROUTE_V[which][0]
                dve.wait_ge(r_a, which + 1)
                if which:
                    step(dve.tensor_reduce(lsum[:, :], lex[:, :, :], AX.X, ALU.add))
                    dve.wait_ge(r_v, cnt[0])
                    step(dve.reciprocal(lrec[:, :], lsum[:, :]))
                    dve.wait_ge(r_v, cnt[0])
                    step(dve.tensor_tensor(prob[:, :, :], lex[:, :, :],
                                           lrec[:, :].unsqueeze(2).broadcast_to([P, NT, E1]), ALU.mult))
                    dve.wait_ge(r_v, cnt[0])
                key = prob if which else lg
                val = prob if which else lex
                by_j = key[:, :, :].unsqueeze(2).broadcast_to([P, NT, E1, E1])
                by_e = key[:, :, :].unsqueeze(3).broadcast_to([P, NT, E1, E1])
                step(dve.tensor_tensor(above[:, :, :, :], by_j, by_e, ALU.is_gt))
                step(dve.tensor_tensor(tied[:, :, :, :], by_j, by_e, ALU.is_equal))
                dve.wait_ge(r_v, cnt[0])
                step(dve.tensor_tensor(tied[:, :, :, :], tied[:, :, :, :],
                                       earlier[:, :, :].unsqueeze(1).broadcast_to([P, NT, E1, E1]), ALU.mult))
                dve.wait_ge(r_v, cnt[0])
                step(dve.tensor_tensor(above[:, :, :, :], above[:, :, :, :], tied[:, :, :, :], ALU.add))
                dve.wait_ge(r_v, cnt[0])
                step(dve.tensor_reduce(rank[:, :, :], above[:, :, :, :], AX.X, ALU.add))
                dve.wait_ge(r_v, cnt[0])
                step(dve.scalar_tensor_tensor(out=(comb if which else chosen)[:, :, :], in0=rank[:, :, :], scalar=1.5,
                                              in1=val[:, :, :], op0=ALU.is_lt, op1=ALU.mult))
                dve.wait_ge(r_v, cnt[0])
                if not which:
                    step(dve.tensor_reduce(lsum[:, :], chosen[:, :, :], AX.X, ALU.add))
                    dve.wait_ge(r_v, cnt[0])
                    step(dve.reciprocal(lrec[:, :], lsum[:, :]))
                    dve.wait_ge(r_v, cnt[0])
                    step(dve.tensor_tensor(comb[:, :, :], chosen[:, :, :],
                                           lrec[:, :].unsqueeze(2).broadcast_to([P, NT, E1]), ALU.mult))
                assert cnt[0] == ROUTE_V[which][1], cnt
                for m in range(2):
                    dve.wait_ge(r_b, 2 * which + m + 1)
                    dve.tensor_copy(acc[:, 4 * m:4 * m + 4, :], PB[6 + m].rearrange("p (k d) -> p k d", k=4)
                                    ).then_inc(r_acc, 1)

            def experts(which):
                dve.wait_ge(r_acc, 2 * which + 2)
                by_expert = comb[:, :, :].rearrange("p t e -> p e t")
                with dve.Fori(0, E1 // 2) as t:
                    for k in range(2):
                        for hf in range(2):
                            q = 2 * E1 * which + 2 * (2 * t + k) + hf
                            dve.wait_ge(e_dn, FREE_HID + q + 1)
                            dve.wait_ge(e_acc, 4 * q + 4)
                            for T in range(4):
                                dve.scalar_tensor_tensor(
                                    out=acc[:, 4 * hf + T, :], in0=PB[4 + hf][:, T * D:T * D + D],
                                    scalar=by_expert[:, 2 * t + k, 4 * hf + T:4 * hf + T + 1], in1=acc[:, 4 * hf + T, :],
                                    op0=ALU.mult, op1=ALU.add).then_inc(e_acc, 1)

            def experts_out(which, s, gate_col):
                dve.wait_ge(e_acc, 8 + 4 * 2 * E1 * (which + 1))
                for m in range(2):
                    dve.scalar_tensor_tensor(out=x[:, 4 * m:4 * m + 4, :], in0=acc[:, 4 * m:4 * m + 4, :],
                                             scalar=tg[:, gate_col:gate_col + 1], in1=x[:, 4 * m:4 * m + 4, :],
                                             op0=ALU.mult, op1=ALU.add).then_inc(x_ok, 4)

            n_res = 0
            for l in parts:
                for r in done:
                    if r.layer == l and not r.local:
                        k_split(r)
                norm(ln_at(l, 0))
                q_split(l)
                if l == 1:
                    local_split()
                for r in done:
                    if r.layer == l:
                        attention(r)
                        heads_out(r)
                residual(n_res, 6, BO[l], l, y_ps, 2 * l)
                n_res += 1
                if l in ffns:
                    norm(ln_at(l, 1))
                    if l == 0:
                        ffn0()
                        residual(n_res, 6, None, 4, f_dn, 0)
                        n_res += 1
                    if l == 2:
                        residual(n_res, 6, "L2_ffn_bias", 6, f_dn, 2)
                        n_res += 1
                    if l in (1, 3):
                        route(l // 2)
                        experts(l // 2)
                        experts_out(l // 2, n_res, 4 + l)

        @block.tensor
        def _(pe):
            pe.wait_ge(consts, 12)
            pe.sem_inc(pv, FREE_PT)
            pe.sem_inc(e_dn, FREE_HID)
            pe.wait_ge(ld_w, 16 * len(SQUARE))
            for m in range(len(TURNED)):
                ins = pe.transpose(PB[m // 4][:, (m % 4) * D:(m % 4) * D + D], wraw[:, m, :], ident[:, :])
                if m % 4 == 3 or m == len(TURNED) - 1:
                    ins.then_inc(w_turned, 1)
            pe.wait_ge(prep_w, 2)
            pe.matmul(PB[7][:, 0:2], ones[:, :], wabs[:, :], start=True, stop=True).then_inc(prep_p0, 1)
            pe.wait_ge(ld_cols, 16 * len(COLS))
            pe.transpose(PB[4][:, 0:NCOL], cols_raw[:, :], ident[0:NCOL, 0:NCOL]).then_inc(prep_p, 1)
            pe.wait_ge(ld_rows, 16 * (len(ROWS) - 1))
            pe.matmul(PB[5], ones[0:1, :], rows[0:1, 0:512], start=True, stop=True).then_inc(prep_p, 1)
            pe.matmul(PB[6][:, 0:NROW - 512], ones[0:1, :], rows[0:1, 512:NROW], start=True, stop=True
                      ).then_inc(prep_p, 1)
            pe.wait_ge(prep_w, 10)
            for c in range(4):
                ins = pe.transpose(PB[7][:, c * P:c * P + P], tern[:, 0, c * D:c * D + D], ident[:, :])
            ins.then_inc(prep_p, 1)
            pe.wait_ge(prep_a, 1)
            for c in range(4):
                ins = pe.transpose(PB[4][:, c * D:c * D + D], tern[:, 1, c * P:c * P + P], ident[:, :])
            ins.then_inc(prep_p, 1)
            pe.wait_ge(ld_misc, 16 * 9)
            pe.wait_ge(prep_a, 3)
            C_, S_, N_ = dft[:, 0, :], dft[:, 1, :], dft[:, 2, :]
            pe.matmul(PB[5][:, 0:D], wfreq[:, 0, :], C_, start=True, stop=False)
            pe.matmul(PB[5][:, 0:D], wfreq[:, 1, :], S_, start=False, stop=True)
            pe.matmul(PB[5][:, D:2 * D], wfreq[:, 1, :], C_, start=True, stop=False)
            pe.matmul(PB[5][:, D:2 * D], wfreq[:, 0, :], N_, start=False, stop=True).then_inc(prep_p, 1)
            pe.wait_ge(prep_a, 9)
            pe.matmul(PB[6][:, 0:D], a12[:, 0, :], C_, start=True, stop=False)
            pe.matmul(PB[6][:, 0:D], a12[:, 1, :], N_, start=False, stop=True).then_inc(prep_p, 1)
            pe.wait_ge(w_kept, 4)
            for b in range(B):
                pe.wait_ge(ctx_in, 32 * (b + 1))
                for m in range(4):
                    if b:
                        pe.wait_ge(ctx_e, 4 * (b - 1) + m + 1)
                    for k in range(4 * m, min(4 * m + 4, KT)):
                        pr = P if k < FULL else TAIL
                        ins = pe.transpose(PB[m][:, (k % 4) * P:(k % 4) * P + pr], ctx_raw[0:pr, k, :],
                                           ident[0:pr, 0:pr])
                    ins.then_inc(ctx_t, 1)
            pe.wait_ge(ctx_e, 4 * B)
            pe.wait_ge(prep_a, 10)

            def normT(s):
                for T in range(NT):
                    pe.wait_ge(ln_xn, NT * s + T + 1)
                    ins = pe.transpose(PB[T // 4][:, (T % 4) * P:(T % 4) * P + P], xn[:, T, :], ident[:, :])
                    if T % 4 == 3:
                        ins.then_inc(ln_t, 1)

            def kv(r):
                g = r.ctx
                w = S2 // 4
                if r.layer:
                    pe.wait_ge(x_ok, 2 * NT * r.layer)
                for b in range(B):
                    n = B * g + b
                    pe.wait_ge(c_ld[b % 2], 16 * (n // 2 + 1))
                    for c in range(4):
                        if b:
                            pe.wait_ge(k_2, 4 * (n - 1) + c + 1)
                        lo = c * w + min(c, 1)
                        pe.matmul(PB[c][:, 0:w + (c == 0)], sq(WK[r.index]), ctxT[:, b % 2, lo:lo + w + (c == 0)],
                                  start=True, stop=True).then_inc(k_ps, 1)
                    for c in range(4):
                        if b:
                            pe.wait_ge(v_ok, 4 * (n - 1) + c + 1)
                        for k in range(4 * c, min(4 * c + 4, KT)):
                            pr = P if k < FULL else TAIL
                            ins = pe.matmul(PB[4 + c][0:pr, (k % 4) * VW:(k % 4) * VW + VW],
                                            ctxT[:, b % 2, k * P:k * P + pr], sq(WV[r.index]), start=True, stop=True)
                        ins.then_inc(v_ps, 1)

            def queries(l):
                for m in range(2):
                    pe.wait_ge(ln_xt, 2 * ln_at(l, 0) + m + 1)
                    pe.matmul(PB[2 + m], sq(WQ[l]), xnT[:, m * 512:m * 512 + 512], start=True, stop=True
                              ).then_inc(q_ps, 1)

            def local_kv():
                pe.wait_ge(q_f, 4)
                for m in range(2):
                    pe.matmul(PB[2 + m], sq(WK[LOCAL]), xnT[:, m * 512:m * 512 + 512], start=True, stop=True
                              ).then_inc(lk_ps, 1)
                for m in range(2):
                    for T in range(4 * m, 4 * m + 4):
                        ins = pe.matmul(PB[4 + m][:, (T % 4) * VW:(T % 4) * VW + VW], xnT[:, T * P:T * P + P],
                                        sq(WV[LOCAL]), start=True, stop=True)
                    ins.then_inc(lk_ps, 1)
                pe.wait_ge(lk_2, 2)
                pe.wait_ge(lv_ok, NT)

            def attention(r):
                cpt = len(r.chunks)

                def piece(n, par, k):
                    use = r.use0 + n * r.uses + k
                    slot = pa[(par + k) % 2]
                    pe.wait_ge(score_free, use + 1)
                    if k == r.c:
                        pe.wait_ge(m_ok, 2 * (r.u0 + n) + 2)
                        for qt in range(QT):
                            ins = pe.transpose(slot[:, 0, :].bitcast(F16)[0:2 * HG, qt * P:qt * P + P],
                                               m16[par][:, qt, :, :].rearrange("p a i -> p (a i)"), ident16[:, :])
                        ins.then_inc(score, 1)
                        return
                    if k == 0:
                        pe.wait_ge(in1[par], 16 * (r.u0 + n - par + 2))
                    qt, c, i = k // (cpt * HG), k // HG % cpt, k % HG
                    lo, w, nb = r.chunks[c]
                    for z in range(nb):
                        at = lo + z * (S2 // 4)
                        ins = pe.matmul(slot[:, z, 0:w], qp1[par][R * i:R * i + KQ, qt * P:qt * P + P],
                                        kp1[par][R * i:R * i + KQ, at:at + w], start=True, stop=True)
                    ins.then_inc(score, 1)

                def fills(n, par, s, i):
                    f = par * r.fills + HG * s + i
                    back = {0: 2, 1: 2, 2: 5}.get(f, 3)
                    pe.wait_ge(exped, r.fill0 + n * r.fills + HG * s + i - back + 1 + FREE_EXP)
                    if s == 0 and i == 0:
                        pe.wait_ge(in2[par], 16 * (r.u0 + n - par + 2))
                        pe.wait_ge(m_in[par], 16 * (r.u0 + n - par + 2))
                    bank = pe_[f % 3]
                    for z, (kt, rows_) in enumerate(r.tiles(s)):
                        ins = pe.matmul(bank[0:rows_, z * S:z * S + S], kp2[par][R * i:R * i + KM, kt * P:kt * P + rows_],
                                        qp2[par][R * i:R * i + KM, :], start=True, stop=True, skip_group_check=r.mask)
                        if r.mask:
                            for qt in range(QT):
                                ins = pe.matmul(bank[0:rows_, z * S + qt * P:z * S + qt * P + P],
                                                mask01[:, qt, kt * P:kt * P + rows_], mask_eye[:, :],
                                                start=False, stop=True, skip_group_check=True)
                    ins.then_inc(fill, 1)

                def product(n, par, s):
                    if s == 0:
                        pe.wait_ge(vg_ok, r.u0 + n + 1)
                        pe.wait_ge(o_ok, r.u0 + n + 1)
                    pe.wait_ge(exped, FREE_EXP + r.fill0 + n * r.fills + HG * s + HG)
                    g = par * r.steps + s
                    for z, (kt, rows_) in enumerate(r.tiles(s)):
                        for j in range(HG):
                            ins = pe.matmul(po[R * j:R * j + R, 0:S], vg[par][0:rows_, kt, j, :],
                                            pt[g % 2][0:rows_, j, z, :], start=(kt == 0), stop=(kt == r.kt - 1))
                    ins.then_inc(pv, 1)

                def unit(n, par, prev=True, nxt=True):
                    k = 0
                    for s in range(r.steps):
                        for i in range(HG):
                            fills(n, par, s, i)
                            while nxt and k < (HG * s + i + 1) * r.uses // r.fills:
                                piece(n + 1, 1 - par, k)
                                k += 1
                        if s:
                            product(n, par, s - 1)
                        elif prev:
                            product(n - 1, 1 - par, r.steps - 1)

                for k in range(r.uses):
                    piece(0, 0, k)
                unit(0, 0, prev=False)
                with pe.Fori(0, UNITS // 2 - 1) as t:
                    unit(2 * t + 1, 1)
                    unit(2 * t + 2, 0)
                unit(UNITS - 1, 1, nxt=False)
                product(UNITS - 1, 1, r.steps - 1)

            def heads_out(r):
                for T in range(NT):
                    b, qt = T // QT, T % QT
                    if T == 0:
                        pe.wait_ge(o_ok, 1 + r.u0 + UNITS)
                    if T >= 4:
                        pe.wait_ge(o_n, NT * r.index + T - 3)
                    for g in range(HG):
                        ins = pe.transpose(PB[T % 4][:, g * P:g * P + P], o_all[:, HG * b + g, qt * P:qt * P + P],
                                           ident[:, :])
                    ins.then_inc(o_t, 1)
                pe.wait_ge(o_n, NT * r.index + NT)

            def project(l):
                if l == 1:
                    pe.wait_ge(o_add, 1)
                for T in range(NT):
                    ins = pe.transpose(PB[4 + T // 4][:, (T % 4) * P:(T % 4) * P + P], on[:, T, :], ident[:, :])
                    if T % 4 == 3:
                        ins.then_inc(on_t, 1)
                for T in range(NT):
                    if T % 4 == 0:
                        pe.wait_ge(on_e, 2 * l + T // 4 + 1)
                    ins = pe.matmul(PB[6 + T // 4][:, (T % 4) * D:(T % 4) * D + D], onT[:, T * P:T * P + P],
                                    sq(WO[l]), start=True, stop=True)
                    if T % 4 == 3:
                        ins.then_inc(y_ps, 1)

            def ffn0():
                for T in range(NT):
                    if T % 4 == 0:
                        pe.wait_ge(ln_xt, 2 * ln_at(0, 1) + T // 4 + 1)
                    if T >= 4:
                        pe.wait_ge(f_act, T - 3)
                    pe.matmul(PB[2 + T % 4], xnT[:, T * P:T * P + P], wfcT[:, :], start=True, stop=True
                              ).then_inc(f_up, 1)
                pe.wait_ge(f_act, NT)
                for m in range(2):
                    for c in range(4):
                        if m:
                            pe.wait_ge(f_ht, c + 1)
                        for k in range(4):
                            pe.wait_ge(f_n, 4 * m + k + 1)
                            ins = pe.transpose(PB[c][:, k * P:k * P + P], h0[:, 4 * m + k, c * P:c * P + P],
                                               ident[:, :])
                        ins.then_inc(f_t, 1)
                for m in range(2):
                    for k in range(4):
                        for c in range(4):
                            pe.wait_ge(f_ht, 4 * m + c + 1)
                            ins = pe.matmul(PB[6 + m][:, k * D:k * D + D], hT[m][:, c, k * P:k * P + P],
                                            wprT[:, c, :], start=(c == 0), stop=(c == 3))
                    ins.then_inc(f_dn, 1)

            def ffn2():
                for T in range(NT):
                    if T % 4 == 0:
                        pe.wait_ge(ln_xt, 2 * ln_at(2, 1) + T // 4 + 1)
                    ins = pe.matmul(PB[6 + T // 4][:, (T % 4) * D:(T % 4) * D + D], xnT[:, T * P:T * P + P],
                                    mfreq[:, :], start=True, stop=True)
                    if T % 4 == 3:
                        ins.then_inc(f_dn, 1)

            def route(which, l):
                for T in range(NT):
                    if T % 4 == 0:
                        pe.wait_ge(ln_xt, 2 * ln_at(l, 1) + T // 4 + 1)
                    ins = pe.matmul(PB[2][:, T * E1:T * E1 + E1], xnT[:, T * P:T * P + P], wr[:, which, :],
                                    start=True, stop=True)
                ins.then_inc(r_ps, 1)
                pe.wait_ge(r_v, ROUTE_V[which][1])
                for T in range(NT):
                    ins = pe.transpose(PB[2 + T // 4][0:E1, (T % 4) * P:(T % 4) * P + P], comb[:, T, :], ident[:, :])
                    if T % 4 == 3:
                        ins.then_inc(r_ct, 1)
                for T in range(NT):
                    if T % 4 == 0:
                        pe.wait_ge(r_cc, 2 * which + T // 4 + 1)
                    ins = pe.matmul(PB[6 + T // 4][:, (T % 4) * D:(T % 4) * D + D], combT[:, T * P:T * P + P],
                                    b2[:, which, :], start=True, stop=True)
                    if T % 4 == 3:
                        ins.then_inc(r_b, 1)

            def experts(which, hid):
                cc = hid // P
                act0 = which and 2 * E1 * (HID1 // P)
                with pe.Fori(0, E1 // 2) as t:
                    for k in range(2):
                        e = 2 * t + k
                        pe.wait_ge(e_w[k], 16 * (E1 * which + 2 * t + 2))
                        for hf in range(2):
                            for c in range(cc):
                                pe.wait_ge(e_act, FREE_UP + act0 + e * 2 * cc + hf * cc + c - 3)
                                pe.matmul(PB[(hf * cc + c) % 4], w_up[k][:, c * P:c * P + P],
                                          xnT[:, hf * 512:hf * 512 + 512], start=True, stop=True).then_inc(e_up, 1)
                        for hf in range(2):
                            q = 2 * E1 * which + 2 * e + hf
                            pe.wait_ge(e_acc, 4 * q + 4)
                            pe.wait_ge(e_act, FREE_UP + act0 + e * 2 * cc + (hf + 1) * cc)
                            for T in range(4):
                                for c in range(cc):
                                    ins = pe.matmul(PB[4 + hf][:, T * D:T * D + D], hT[hf][:, c, T * P:T * P + P],
                                                    w_dn[k][:, c, :], start=(c == 0), stop=(c == cc - 1))
                            ins.then_inc(e_dn, 1)

            for l in parts:
                for r in done:
                    if r.layer == l and not r.local:
                        kv(r)
                normT(ln_at(l, 0))
                queries(l)
                if l == 1:
                    local_kv()
                for r in done:
                    if r.layer == l:
                        attention(r)
                        heads_out(r)
                project(l)
                if l in ffns:
                    normT(ln_at(l, 1))
                    if l == 0:
                        ffn0()
                    if l == 2:
                        ffn2()
                    if l in (1, 3):
                        route(l // 2, l)
                        experts(l // 2, HID1 if l == 1 else HID3)


_OUT = (B, S, D)
_NAMES = (["x", "ctx_1024", "ctxb_2048x8", "mask_1x1xSxS2_bk1"] + [n for n, _ in SQUARE] + [n for n, _ in COLS]
          + [n for n, _ in ROWS if n != "zero"]
          + ["L0_ffn_W_fc", "L0_ffn_W_proj", "L1_ffn_Wr", "L1_ffn_W1", "L1_ffn_W2", "L1_ffn_b2",
             "L2_ffn_w_freq_real", "L2_ffn_w_freq_imag", "L3_ffn_gate_w", "L3_ffn_w1", "L3_ffn_w2", "L3_ffn_b2"])


def kernel(last=4.0, **inputs):
    import numpy as np
    import concourse.bacc as bacc
    from concourse.bass_utils import run_bass_kernel_spmd

    nc = bacc.Bacc("TRN2", target_bir_lowering=False, num_devices=1)
    arrays, args = {}, {}
    angle = 2.0 * np.pi * (np.outer(np.arange(D), np.arange(D)) % D) / D
    tables = {"dft_cos": np.cos(angle), "dft_sin": np.sin(angle), "dft_nsin": -np.sin(angle)}
    for name in _NAMES + list(tables):
        v = tables[name].astype(np.float32) if name in tables else np.ascontiguousarray(inputs[name])
        if v.ndim == 0:
            v = v.reshape(1)
        arrays[f"in_{name}"] = v
        args[name] = nc.dram_tensor(f"in_{name}", v.shape, mybir.dt.from_np(v.dtype), kind="ExternalInput").ap()
    out = nc.dram_tensor("out", _OUT, F32, kind="ExternalOutput").ap()
    flamingo(nc, args, out, last)
    got = run_bass_kernel_spmd(nc, [arrays], core_ids=[0])
    return got.results[0]["out"]
```

```python
from contextlib import ExitStack

import concourse.bass as bass
from concourse import mybir

F32 = mybir.dt.float32
F16 = mybir.dt.float16
U8 = mybir.dt.uint8
ALU = mybir.AluOpType
ACT = mybir.ActivationFunctionType
AX = mybir.AxisListType

P = 128
B, S, D = 4, 256, 128
H, DH = 16, 8
S2 = 1601
TOK = B * S
NT = TOK // P
QT = S // P
HG = 4
UNITS = B * H // HG
PAIRS = HG // 2
R = 32
KQ = 3 * DH
KM = KQ + 2
SCALE = 1.0 / DH ** 0.5
LN_EPS = 1e-5
BIG = 60000.0
MIN_MAX = -30000.0
TINY = 1e-30
FULL = S2 // P
TAIL = S2 - FULL * P
KT = FULL + 1
LKT = S // P
VW = D
E1, HID0, HID1, HID3 = 8, 512, 512, 256




def chunk_cols(nk):
    if nk == S2:
        w = S2 // 4
        return [(0, w + 1, 2), (2 * w + 1, w, 2)]
    return [(0, nk, 1)]


def ring(n, size):
    banks = [f % size for f in range(n)]
    if banks[-1] == banks[0]:
        banks[-1] = banks[-3]
    return banks


class Run:

    def __init__(self, index, layer, nk, mask, before):
        self.index, self.layer, self.nk, self.mask = index, layer, nk, mask
        self.ctx = {0: 0, 2: 1, 3: 2, 4: 3}.get(index)
        self.local = nk == S
        self.turn, self.ahead = (2, 9) if self.local else (2, 6)
        self.chunks = chunk_cols(nk)
        self.kt = (nk + P - 1) // P
        self.fills = PAIRS * self.kt
        self.c = QT * HG * len(self.chunks)
        self.uses = self.c + 1
        self.banks = ring(2 * self.fills, 3)
        self.u0 = before.u0 + UNITS if before else 0
        self.use0 = before.use0 + UNITS * before.uses if before else 0
        self.fill0 = before.fill0 + UNITS * before.fills if before else 0
        self.step0 = before.step0 + UNITS * before.kt if before else 0

    def keys(self, s):
        return min(P, self.nk - s * P)

    def back(self, f):
        return next(d for d in range(1, 9) if self.banks[f - d] == self.banks[f])

    def use(self, n, k, first=False):
        return self.use0 + (k - (k > self.turn) if first else n * self.uses - 1 + k)

    def slot(self, par, k, first=False):
        return (k - (k > self.turn) if first else par + 1 + k) % 2

    def pieces(self, first=False):
        return [(k, None if k == self.turn else k - (k > self.turn)) for k in range(self.uses) if not (first and k == self.turn)]


def runs():
    out = []
    for layer, nk, mask in ((0, S2, False), (1, S, False), (1, S2, False), (2, S2, False), (3, S2, True)):
        out.append(Run(len(out), layer, nk, mask, out[-1] if out else None))
    return out


RUNS = runs()
LOCAL = 1
IN_DMAS = 16 * (1 + HG) // 2
FREE_SCORE, FREE_EXP, FREE_PT, FREE_PV = 2, 5, 2, 1
FREE_UP, FREE_HID, FREE_ACC = 4, 3, 8
ROUTE_V = [(3, 12, 0), (15, 24, 12)]
SQUARE = [("L0_xattn_Wq", 0), ("L0_xattn_Wk", 0), ("L0_xattn_Wv", 0), ("L0_xattn_Wo", 0),
          ("L1_xattn_q_w", 1), ("L1_xattn_k_w", 1), ("L1_xattn_v_w", 1), ("L1_xattn_kg_w", 1),
          ("L1_xattn_vg_w", 1), ("L1_xattn_out_w", 1),
          ("L2_xattn_wq", 1), ("L2_xattn_wk", 1), ("L2_xattn_wv", 1), ("L2_xattn_wo", 1),
          ("L3_xattn_Wq", 1), ("L3_xattn_Wk", 1), ("L3_xattn_Wv", 1), ("L3_xattn_Wo", 1)]
SQ = {n: i for i, (n, _) in enumerate(SQUARE)}
TURNED = [i for i, (_, t) in enumerate(SQUARE) if t]
COLS = [("L1_ffn_b1", 32), ("L3_ffn_b1", 16), ("L0_ffn_ln_w", 4), ("L0_ffn_ln_b", 4), ("L0_xattn_bq", 1),
        ("L0_xattn_bk", 1), ("L1_xattn_q_b", 1), ("L1_xattn_k_b", 1), ("L1_xattn_kg_b", 1)]
COL, _at = {}, 0
for _n, _k in COLS:
    COL[_n] = _at
    _at += _k
NCOL = _at + 1
ZCOL = _at
ROWS = [("L0_xattn_bv", D), ("L0_xattn_bo", D), ("L1_xattn_v_b", D), ("L1_xattn_vg_b", D), ("L1_xattn_out_b", D),
        ("L2_ffn_bias", D), ("zero", D), ("L3_ffn_gate_b", 8), ("g_xattn", 4), ("g_ffn", 4), ("L1_xattn_gate", 1)]
ROW, _at = {}, 0
for _n, _k in ROWS:
    ROW[_n] = _at
    _at += _k
NROW = _at
WQ = ["L0_xattn_Wq", "L1_xattn_q_w", "L2_xattn_wq", "L3_xattn_Wq"]
WO = ["L0_xattn_Wo", "L1_xattn_out_w", "L2_xattn_wo", "L3_xattn_Wo"]
WK = ["L0_xattn_Wk", "L1_xattn_k_w", "L1_xattn_kg_w", "L2_xattn_wk", "L3_xattn_Wk"]
WV = ["L0_xattn_Wv", "L1_xattn_v_w", "L1_xattn_vg_w", "L2_xattn_wv", "L3_xattn_Wv"]
BQ = ["L0_xattn_bq", "L1_xattn_q_b", None, None]
BK = ["L0_xattn_bk", "L1_xattn_k_b", "L1_xattn_kg_b", None, None]
BV = ["L0_xattn_bv", "L1_xattn_v_b", "L1_xattn_vg_b", None, None]
BO = ["L0_xattn_bo", "L1_xattn_out_b", None, None]


def flamingo(nc, a, out, last=4.0):
    ctx = ExitStack()
    with ctx:
        def sb(name, shape, dt=F32):
            return ctx.enter_context(nc.sbuf_tensor(name, shape, dt))

        def sem(name):
            return ctx.enter_context(nc.semaphore(name))

        def dram(name, shape, dt):
            return nc.dram_tensor(name, shape, dt, kind="Internal").ap()

        x = sb("x", [P, NT, D])
        xn = sb("xn", [P, NT, D])
        xnT = sb("xnT", [P, TOK])
        wsq = sb("wsq", [P, len(SQUARE), D])
        ident = sb("ident", [P, P])
        ident16 = sb("ident16", [P, P], F16)
        mask_eye = sb("mask_eye", [P, P], F16)
        ones = sb("ones", [P, P])
        rows = sb("rows", [1, NROW])
        spread = sb("spread", [P, NROW])
        cols_raw = sb("cols_raw", [NCOL, P])
        cols = sb("cols", [P, NCOL])
        ctxT = sb("ctxT", [P, 2, S2])
        k1c = sb("k1c", [P, 2, S2 + 1], F16)
        k2c = sb("k2c", [P, 2, S2 + 1], F16)
        v_all = sb("v_all", [P, B, KT, VW])
        v_loc = sb("v_loc", [P, B, LKT, VW])
        gate = sb("gate", [P, B, KT])
        gate_e = sb("gate_e", [P, B, KT])
        qf = sb("qf", [P, TOK])
        q1c = sb("q1c", [P, TOK], F16)
        q2c = sb("q2c", [P, TOK], F16)
        kp1 = [sb(f"kp1_{i}", [P, S2 + 1], F16) for i in range(2)]
        kp2 = [sb(f"kp2_{i}", [P, S2 + 1], F16) for i in range(2)]
        qp1 = [sb(f"qp1_{i}", [P, HG, S], F16) for i in range(2)]
        qp2 = [sb(f"qp2_{i}", [P, HG, S], F16) for i in range(2)]
        vg = [sb(f"vg_{i}", [P, KT, HG, R]) for i in range(2)]
        early_mem = [sb(f"early_{i}", [P, 2, HG, S]) for i in range(2)]
        pt = [m[:, 0, :, :] for m in early_mem]
        mx = [sb(f"mx_{i}", [P, QT * HG, 2]) for i in range(2)]
        nm = [sb(f"nm_{i}", [P, QT, HG]) for i in range(2)]
        nmc = [sb(f"nmc_{i}", [P, QT, HG]) for i in range(2)]
        m16 = [sb(f"m16_{i}", [P, QT, 2, HG], F16) for i in range(2)]
        ms = [sb(f"ms_{i}", [2 * HG, S], F16) for i in range(2)]
        mask01 = sb("mask01", [P, QT, S2], F16)
        mask_add = sb("mask_add", [P, QT, 4, S2 // 4 + 1], F16)
        o_all = sb("o_all", [P, UNITS, S])
        on = sb("on", [P, NT, D])
        on_loc = sb("on_loc", [P, NT, D])
        rec = sb("rec", [P, NT, H])
        rec0 = sb("rec0", [P, NT, H])
        stats = sb("stats", [P, NT, 6])
        mv = sb("mv", [P, NT, 2])
        var_eps = sb("var_eps", [P, NT])
        rstd = sb("rstd", [P, NT])
        minus_half = sb("minus_half", [P, NT])
        tg = sb("tg", [P, 8])
        lgate = sb("lgate", [P, 3])
        wabs = sb("wabs", [P, 2])
        whalf = sb("whalf", [P, 2, 2])
        wfcT = sb("wfcT", [P, HID0])
        wprT = sb("wprT", [P, 4, D])
        dft = sb("dft", [P, 3, P])
        wfreq = sb("wfreq", [P, 2, D])
        a12 = sb("a12", [P, 2, D])
        mfreq = sb("mfreq", [P, D])
        w_up = [sb(f"w_up_{i}", [P, HID1]) for i in range(2)]
        w_dn = [sb(f"w_dn_{i}", [P, 4, D]) for i in range(2)]
        b1_now = [sb(f"b1_now_{i}", [P, 4]) for i in range(2)]
        wr = sb("wr", [P, 2, E1])
        b2 = sb("b2", [E1, 2, D])
        lg = sb("lg", [P, NT, E1])
        lmax = sb("lmax", [P, NT])
        lex = sb("lex", [P, NT, E1])
        lsh = sb("lsh", [P, NT, E1])
        lsum = sb("lsum", [P, NT])
        lrec = sb("lrec", [P, NT])
        prob = sb("prob", [P, NT, E1])
        earlier = sb("earlier", [P, E1, E1])
        rank = sb("rank", [P, NT, E1])
        chosen = sb("chosen", [P, NT, E1])
        comb = sb("comb", [P, NT, E1])
        combT = sb("combT", [E1, TOK])

        early = early_mem[0][:, :, :, :].rearrange("p a b q -> p (a b q)")
        wraw = early[:, 0:len(TURNED) * D].rearrange("p (k d) -> p k d", d=D)
        early = early_mem[1][:, :, :, :].rearrange("p a b q -> p (a b q)")
        tern = early[:, 0:2 * HID0].rearrange("p (k d) -> p k d", k=2)
        tern_neg = early[:, 2 * HID0:4 * HID0].rearrange("p (k d) -> p k d", k=2)
        h0 = o_all[:, :, :].rearrange("p u q -> p (u q)").rearrange("p (t n) -> p t n", n=HID0)
        hT = [m[:, :, :, :].rearrange("p a b q -> p (a b q)").rearrange("p (c n) -> p c n", c=4) for m in early_mem]
        one16 = v_loc[:, :, :, :].rearrange("p b k d -> p (b k d)").bitcast(F16)[:, 0:S2]
        masked = [m.bitcast(F16)[:, 0:2 * (S2 // 4 + 1)].rearrange("p (z n) -> p z n", z=2)
                  for m in (wfcT[:, :], wprT[:, :, :].rearrange("p c d -> p (c d)"))]
        ctx_raw = o_all[:, :, :].rearrange("p u q -> p (u q)")[:, 0:2 * KT * D].rearrange(
            "p (b k d) -> p b k d", b=2, d=D)
        mask8 = kp1[1][:, 0:S2].bitcast(U8).rearrange("p (t n) -> p t n", t=QT)
        wfc_raw = kp1[0][:, 0:2 * HID0].bitcast(F32).rearrange("p (c d) -> p c d", d=D)
        wpr_raw = kp2[0][:, 0:2 * HID0].bitcast(F32)
        gate_in = kp2[1][:, 0:2 * B * KT * 8].bitcast(F32).rearrange("p (b k c) -> p b k c", b=B, k=KT)
        above, tied = [k2c[:, i, 0:2 * NT * E1 * E1].bitcast(F32).rearrange("p (t e j) -> p t e j", t=NT, e=E1)
                       for i in range(2)]
        onT = qf
        acc = on
        ytmp = on_loc

        pa = [ctx.enter_context(nc.psum_tensor(f"score_ring_{i}", [P, 2, 512], F32)) for i in range(2)]
        pe_ = [ctx.enter_context(nc.psum_tensor(f"exp_ring_{i}", [P, 512], F32)) for i in range(3)]
        po = ctx.enter_context(nc.psum_tensor("pv_bank", [P, 512], F32))
        PB = [pa[0][:, 0, :], pa[0][:, 1, :], pa[1][:, 0, :], pa[1][:, 1, :],
              pe_[0][:, :], pe_[1][:, :], pe_[2][:, :], po[:, :]]

        ctxT_d = dram("ctxT_d", [B, P, S2], F32)
        k_d = [dram(f"k_d{r.index}", [UNITS, P, r.nk], F16) for r in RUNS]
        q_d = [dram(f"q_d{l}", [UNITS, P, S], F16) for l in range(4)]

        ld_x, ld_w, ld_wt, ld_cols, ld_rows, ld_mask, ld_gate, ld_misc, ld_fc = [
            sem(n) for n in ("ld_x", "ld_w", "ld_wt", "ld_cols", "ld_rows", "ld_mask", "ld_gate", "ld_misc", "ld_fc")]
        consts = sem("consts")
        dconst = sem("dconst")
        padded0, padded = sem("padded0"), sem("padded")
        w_turned, w_kept = sem("w_turned"), sem("w_kept")
        prep_v = sem("prep_v")
        prep_a = sem("prep_a")
        prep_p = sem("prep_p")
        ctx_t, ctx_e = sem("ctx_t"), sem("ctx_e")
        prep_w, prep_p0, f_rs, r_acc = sem("prep_w"), sem("prep_p0"), sem("f_rs"), sem("r_acc")
        ctx_in, ctx_out, c_ld, k_out, in1, in2, m_in, e_w = [
            [sem(f"{n}_{i}") for i in range(2)] for n in ("ctx_in", "ctx_out", "c_ld", "k_out", "in1", "in2", "m_in", "e_w")]
        ln_st, ln_mv, ln_ve, ln_rs, ln_xn, ln_t, ln_xt = [
            sem(n) for n in ("ln_st", "ln_mv", "ln_ve", "ln_rs", "ln_xn", "ln_t", "ln_xt")]
        q_ps, q_f, q_1, q_2, q_out = [sem(n) for n in ("q_ps", "q_f", "q_1", "q_2", "q_out")]
        k_ps, v_ps, k_1, k_2, v_ok = [sem(n) for n in ("k_ps", "v_ps", "k_1", "k_2", "v_ok")]
        lk_ps, lk_1, lk_2, lk_out, lv_ok = [sem(n) for n in ("lk_ps", "lk_1", "lk_2", "lk_out", "lv_ok")]
        score, score_free = sem("score"), sem("score_free")
        mx_done, m_ok = sem("mx_done"), sem("m_ok")
        fill, exped = sem("fill"), sem("exped")
        pv, o_ok, vg_ok = sem("pv"), sem("o_ok"), sem("vg_ok")
        o_t, o_rec, o_n, o_add, on_t, on_e, y_ps, y_t, x_ok = [
            sem(n) for n in ("o_t", "o_rec", "o_n", "o_add", "on_t", "on_e", "y_ps", "y_t", "x_ok")]
        f_up, f_act, f_st, f_n, f_t, f_ht, f_dn, f_x = [
            sem(n) for n in ("f_up", "f_act", "f_st", "f_n", "f_t", "f_ht", "f_dn", "f_x")]
        r_ps, r_v, r_a, r_ct, r_cc, r_b = [sem(n) for n in ("r_ps", "r_v", "r_a", "r_ct", "r_cc", "r_b")]
        e_up, e_act, e_dn, e_acc, e_b = [sem(n) for n in ("e_up", "e_act", "e_dn", "e_acc", "e_b")]
        stored, passed = sem("stored"), sem("passed")

        block = ctx.enter_context(nc.Block())
        sq = lambda name: wsq[:, SQ[name], :]
        col = lambda name, k=0: cols[:, (COL[name] if name else ZCOL) + k:(COL[name] if name else ZCOL) + k + 1]
        row = lambda name, n: spread[:, ROW[name or "zero"]:ROW[name or "zero"] + n]
        over = lambda ap, n: ap.unsqueeze(1).broadcast_to([P, n, ap.shape[-1]])

        parts = [l for l in range(4) if l < last]
        ffns = [l for l in range(4) if l + 0.5 < last]
        done = [r for r in RUNS if r.layer in parts]
        LN_T, LN_X = NT, 2

        def ln_at(layer, ffn):
            return 2 * layer + ffn

        def bases(n):
            return 16 * n

        units = range(UNITS)

        @block.sync
        def _(sp):
            sp.dma_start(x[:, :, :], a["x"].rearrange("b (t p) d -> p (b t) d", p=P)).then_inc(ld_x, 16)
            def ctx_load(b):
                if b >= 2:
                    sp.wait_ge(ctx_t, 4 * (b - 1))
                sp.dma_start(ctx_raw[:, b % 2, 0:FULL, :],
                             a["ctx_1024"][b, 0:FULL * P, :].rearrange("(t p) d -> p t d", p=P)
                             ).then_inc(ctx_in[b % 2], 16)
                sp.dma_start(ctx_raw[0:TAIL, b % 2, FULL, :], a["ctx_1024"][b, FULL * P:S2, :]
                             ).then_inc(ctx_in[b % 2], 16)

            ctx_load(0)
            sp.wait_ge(dconst, 3)
            for name, k in COLS:
                src = a[name]
                if len(src.shape) == 2:
                    src = src.rearrange("e (c p) -> (e c) p", p=P)
                else:
                    src = src.rearrange("(c p) -> c p", p=P)
                sp.dma_start(cols_raw[COL[name]:COL[name] + k, :], src).then_inc(ld_cols, 16)
            for name, k in ROWS:
                if name != "zero":
                    src = a[name]
                    src = src.rearrange("(a n) -> a n", a=1) if len(src.shape) == 1 else src
                    sp.dma_start(rows[0:1, ROW[name]:ROW[name] + k], src).then_inc(ld_rows, 16)
            ctx_load(1)
            for b in range(B):
                sp.dma_start(gate_in[:, b, 0:FULL, :],
                             a["ctxb_2048x8"][b, 0:FULL * P, :].rearrange("(t p) c -> p t c", p=P)
                             ).then_inc(ld_gate, 16)
                sp.dma_start(gate_in[0:TAIL, b, FULL, :], a["ctxb_2048x8"][b, FULL * P:S2, :]).then_inc(ld_gate, 16)
            for k, name in enumerate(("dft_cos", "dft_sin", "dft_nsin")):
                sp.dma_start(dft[:, k, :], a[name]).then_inc(ld_misc, 16)
            sp.dma_start(wfreq[:, 0, :], a["L2_ffn_w_freq_real"]).then_inc(ld_misc, 16)
            sp.dma_start(wfreq[:, 1, :], a["L2_ffn_w_freq_imag"]).then_inc(ld_misc, 16)
            sp.dma_start(wr[:, 0, :], a["L1_ffn_Wr"]).then_inc(ld_misc, 16)
            sp.dma_start(wr[:, 1, :], a["L3_ffn_gate_w"]).then_inc(ld_misc, 16)
            sp.dma_start(b2[:, 0, :], a["L1_ffn_b2"]).then_inc(ld_misc, 16)
            sp.dma_start(b2[:, 1, :], a["L3_ffn_b2"]).then_inc(ld_misc, 16)

            def split_rows(dst, b, part):
                v = dst[4 * b:4 * b + 4].rearrange("g (i r) n -> (g i) r n", r=R)
                return v[:, DH * part:DH * part + DH, :]

            def constant_rows(r):
                for b in range(B):
                    sp.dma_start(k_d[r.index][4 * b:4 * b + 4].rearrange("g (i r) n -> (g i) r n", r=R)[:, KQ:R, :],
                                 one16[:, 0:r.nk]).then_inc(padded0, 16)

            def k_prep(r):
                g = r.ctx
                if r.layer == 0:
                    sp.wait_ge(dconst, 4)
                    constant_rows(r)
                    ctx_load(2)
                else:
                    for i in range(2):
                        sp.wait_ge(ctx_out[i], 16 * B // 2)
                    c_load(r, g, 0)
                    c_load(r, g, 1)
                q_store(r.layer)
                if r.layer == 1:
                    local_store()
                for b in range(B):
                    if r.layer == 0:
                        sp.wait_ge(ctx_e, 4 * b + 4)
                        sp.dma_start(ctxT_d[b], ctxT[:, b % 2, :]).then_inc(ctx_out[b % 2], 16)
                        if b == 0:
                            ctx_load(3)
                    k_store(r, g, b)
                    if r.layer and b + 2 < B:
                        c_load(r, g, b + 2)

            def c_load(r, g, b):
                n = B * g + b
                sp.wait_ge(k_ps, 4 * (n - 1))
                sp.wait_ge(v_ps, 4 * (n - 1))
                sp.dma_start(ctxT[:, b % 2, :], ctxT_d[b]).then_inc(c_ld[b % 2], 16)

            def k_store(r, g, b):
                n = B * g + b
                sp.wait_ge(k_1, 4 * (n + 1))
                for part in (0, 2):
                    sp.dma_start(split_rows(k_d[r.index], b, part), k1c[:, b % 2, 0:S2]).then_inc(k_out[b % 2], 16)
                sp.wait_ge(k_2, 4 * (n + 1))
                sp.dma_start(split_rows(k_d[r.index], b, 1), k2c[:, b % 2, 0:S2]).then_inc(k_out[b % 2], 16)

            def q_store(l):
                sp.wait_ge(q_2, 2 * (l + 1))
                for b in range(B):
                    for part, src in ((0, q1c), (1, q1c), (2, q2c)):
                        sp.dma_start(split_rows(q_d[l], b, part), src[:, b * S:b * S + S]).then_inc(q_out, 16)

            def local_store():
                sp.wait_ge(lk_2, 2)
                for b in range(B):
                    for part, src in ((0, k1c), (2, k1c), (1, k2c)):
                        sp.dma_start(split_rows(k_d[LOCAL], b, part), src[:, 0, b * S:b * S + S]).then_inc(lk_out, 16)

            def loads(r):
                kd, qd = k_d[r.index], q_d[r.layer]

                def q_blocks(dst, n, sem_):
                    for i in range(HG):
                        sp.dma_start(dst[R * i:R * i + KQ, i, :], qd[n, R * i:R * i + KQ, :]).then_inc(sem_, 16)

                def pass1(n, par):
                    sp.dma_start(kp1[par][:, 0:r.nk], kd[n]).then_inc(in1[par], 16)
                    q_blocks(qp1[par], n, in1[par])

                def pass2(n, par):
                    sp.dma_start(kp2[par][:, 0:r.nk], kd[n]).then_inc(in2[par], 16)
                    q_blocks(qp2[par], n, in2[par])

                def maxima(n, par):
                    sp.dma_start(qp2[par][KQ:KQ + 2, :, :], ms[par][:, :]).then_inc(m_in[par], 16)

                def unit(n, par, p1=True, p2=True, first=False):
                    sp.wait_ge(score_free, FREE_SCORE + (r.use(n + 1, r.turn) if p2 else
                                                         r.use0 + UNITS * r.uses - 1) + 1)
                    maxima(n, par)
                    if p1:
                        pass1(n + 2, par)
                    if p2:
                        if not first:
                            sp.wait_ge(fill, r.fill0 + n * r.fills)
                        pass2(n + 1, 1 - par)

                pass1(0, 0)
                pass1(1, 1)
                pass2(0, 0)
                unit(0, 0, first=True)
                with sp.Fori(0, (UNITS - 4) // 2) as t:
                    unit(2 * t + 1, 1)
                    unit(2 * t + 2, 0)
                unit(UNITS - 3, 1)
                unit(UNITS - 2, 0, p1=False)
                unit(UNITS - 1, 1, p1=False, p2=False)

            def experts(l, which, w_up_d, w_dn_d, hid):
                cc = hid // P
                with sp.Fori(0, E1 // 2) as t:
                    for k in range(2):
                        sp.wait_ge(e_dn, FREE_HID + 2 * E1 * which + 2 * (2 * t + k) - 2)
                        sp.dma_start(w_up[k][:, 0:hid], w_up_d[2 * t + k]).then_inc(e_w[k], 16)
                        sp.dma_start(w_dn[k][:, 0:cc, :],
                                     w_dn_d[2 * t + k].rearrange("(c p) d -> p c d", p=P)).then_inc(e_w[k], 16)

            for l in parts:
                for r in done:
                    if r.layer == l and not r.local:
                        k_prep(r)
                sp.wait_ge(q_out, 16 * 12 * (l + 1))
                if l == 0:
                    sp.wait_ge(padded0, 16 * B)
                    sp.wait_ge(dconst, 9)
                if l == 1:
                    sp.wait_ge(padded, 16 * B * (len(RUNS) - 1))
                    sp.wait_ge(lk_out, 16 * 12)
                for r in done:
                    if r.layer == l:
                        if not r.local:
                            for i in range(2):
                                sp.wait_ge(k_out[i], 48 * (B // 2) * (r.ctx + 1))
                        loads(r)
                if l in ffns and l == 1:
                    experts(l, 0, a["L1_ffn_W1"], a["L1_ffn_W2"], HID1)
                if l in ffns and l == 3:
                    experts(l, 1, a["L3_ffn_w1"], a["L3_ffn_w2"], HID3)
            sp.wait_ge(x_ok, NT * len(parts) + NT * len(ffns))
            sp.dma_start(out.rearrange("b (t p) d -> p (b t) d", p=P), x[:, :, :]).then_inc(stored, 16)
            sp.wait_ge(stored, 16)

        @block.gpsimd
        def _(pool):
            pool.memset(ident[:, :], 0.0).then_inc(consts, 1)
            pool.memset(ident16[:, :], 0.0).then_inc(consts, 1)
            pool.memset(mask_eye[:, :], 0.0).then_inc(consts, 1)
            pool.memset(earlier[:, :, :], 1.0).then_inc(consts, 1)
            pool.wait_ge(consts, 4)
            for m, v in ((ident, 1.0), (ident16, 1.0), (mask_eye, -BIG)):
                pool.affine_select(out=m[:, :], in_=m[:, :], compare_op=ALU.not_equal, fill=v, base=0,
                                   pattern=[[-1, P]], channel_multiplier=1).then_inc(consts, 1)
            pool.affine_select(out=earlier[:, :, :], in_=earlier[:, :, :], compare_op=ALU.is_gt, fill=0.0, base=0,
                               pattern=[[1, E1], [-1, E1]], channel_multiplier=0).then_inc(consts, 1)
            pool.memset(ones[:, :], 1.0).then_inc(consts, 1)
            pool.memset(minus_half[:, :], -0.5).then_inc(consts, 1)
            for i in range(2):
                pool.memset(vg[i][:, :, :, :], 1.0).then_inc(consts, 1)
            def weights(which):
                for i, (name, turned) in which:
                    dst = wraw[:, TURNED.index(i), :] if turned else wsq[:, i, :]
                    pool.dma_start(dst, a[name]).then_inc(ld_wt if turned else ld_w, 16)

            weights([w for w in enumerate(SQUARE) if not w[1][1]])

            def norm(s):
                pool.wait_ge(ln_mv, NT * (s + 1))
                pool.tensor_scalar(var_eps[:, :], mv[:, :, 1], LN_EPS, None, ALU.add).then_inc(ln_ve, 1)
                pool.wait_ge(ln_ve, s + 1)
                pool.tensor_tensor(rstd[:, :], var_eps[:, :], minus_half[:, :], ALU.pow).then_inc(ln_rs, 1)

            def expert_bias(which, hid, bcol):
                cc = hid // P
                biases = cols[:, COL[bcol]:COL[bcol] + E1 * cc].rearrange("p (e c) -> p e c", c=cc)
                with pool.Fori(0, E1 // 2) as t:
                    for k in range(2):
                        pool.wait_ge(e_dn, FREE_HID + 2 * E1 * which + 2 * (2 * t + k) - 2)
                        pool.tensor_copy(b1_now[k][:, 0:cc], biases[:, 2 * t + k, :]).then_inc(e_b, 1)

            def unit_v(r):
                v = v_loc if r.local else v_all
                if r.local:
                    pool.wait_ge(lv_ok, NT)
                else:
                    pool.wait_ge(v_ok, 4 * B * (r.ctx + 1))

                def copy(b, g, par):
                    src = v[:, b, :, R * g:R * g + R].rearrange("p k (j d) -> p k j d", d=DH)
                    if r.layer == 0:
                        pool.tensor_tensor(vg[par][:, :, :, 0:DH], src,
                                           gate[:, b, :].unsqueeze(2).unsqueeze(3).broadcast_to([P, KT, HG, DH]),
                                           ALU.mult).then_inc(vg_ok, 1)
                    else:
                        pool.tensor_copy(vg[par][:, 0:r.kt, :, 0:DH], src).then_inc(vg_ok, 1)

                for g in range(2):
                    if r.u0:
                        pool.wait_ge(pv, FREE_PT + r.step0)
                    copy(0, g, g)
                for g in range(2, 4):
                    pool.wait_ge(pv, FREE_PT + r.step0 + (g - 1) * r.kt)
                    copy(0, g, g % 2)
                with pool.Fori(1, B) as b:
                    for g in range(4):
                        pool.wait_ge(pv, FREE_PT + r.step0 + (4 * b + g - 1) * r.kt)
                        copy(b, g, g % 2)

            for l in parts:
                norm(ln_at(l, 0))
                if l == 0:
                    weights([w for w in enumerate(SQUARE) if w[1][1]])
                    pool.wait_ge(dconst, 4)
                    for r in RUNS[1:]:
                        for b in range(B):
                            pool.dma_start(
                                k_d[r.index][4 * b:4 * b + 4].rearrange("g (i r) n -> (g i) r n", r=R)[:, KQ:R, :],
                                one16[:, 0:r.nk]).then_inc(padded, 16)
                    pool.wait_ge(prep_v, 3)
                for r in done:
                    if r.layer == l:
                        unit_v(r)
                if l == 1:
                    pool.wait_ge(o_n, NT * 3)
                    pool.tensor_tensor(on[:, :, :], on[:, :, :], on_loc[:, :, :], ALU.add).then_inc(o_add, 1)
                if l in ffns:
                    norm(ln_at(l, 1))
                    if l in (1, 3):
                        expert_bias(l // 2, HID1 if l == 1 else HID3, "L1_ffn_b1" if l == 1 else "L3_ffn_b1")
                    if l == 0:
                        pool.wait_ge(f_rs, 1)
                        pool.tensor_tensor(rstd[:, :], var_eps[:, :], minus_half[:, :], ALU.pow).then_inc(f_rs, 1)

        @block.scalar
        def _(act):
            act.sem_inc(exped, FREE_EXP)
            act.sem_inc(o_ok, FREE_PV)
            act.sem_inc(e_act, FREE_UP)
            act.dma_start(mask8[:, :, :], a["mask_1x1xSxS2_bk1"].rearrange("a b (t p) n -> p (a b t) n", p=P)
                          ).then_inc(ld_mask, 16)
            act.dma_start(wfc_raw[:, :, :], a["L0_ffn_W_fc"].rearrange("(c p) d -> p c d", p=P)).then_inc(ld_fc, 16)
            act.dma_start(wpr_raw[:, :], a["L0_ffn_W_proj"]).then_inc(ld_fc, 16)
            def spread_vectors():
                act.wait_ge(prep_p, 1)
                act.activation(cols[:, :], PB[0][:, 0:NCOL], ACT.Copy).then_inc(prep_a, 1)
                act.wait_ge(prep_p, 2)
                act.activation(spread[:, 0:512], PB[1], ACT.Copy).then_inc(prep_a, 1)
                act.wait_ge(prep_p, 3)
                act.activation(spread[:, 512:NROW], PB[2][:, 0:NROW - 512], ACT.Copy).then_inc(prep_a, 1)
                act.wait_ge(prep_a, 3)
                act.activation(tg[:, :], spread[:, ROW["g_xattn"]:ROW["g_xattn"] + 8], ACT.Tanh).then_inc(prep_a, 1)
                act.activation(lgate[:, 0:1], row("L1_xattn_gate", 1), ACT.Exp, scale=-1.0).then_inc(prep_a, 1)

            def weights():
                for m in range(0, len(TURNED), 4):
                    k = min(4, len(TURNED) - m)
                    act.wait_ge(w_turned, m // 4 + 1)
                    act.activation(wsq[:, TURNED[m]:TURNED[m] + k, :], PB[m // 4][:, 0:k * D].rearrange(
                        "p (k d) -> p k d", k=k), ACT.Copy).then_inc(w_kept, 1)
                act.wait_ge(prep_v, 1)
                act.activation(gate_e[:, :, :], gate[:, :, :], ACT.Exp, scale=-10.0 / 8, bias=1.0).then_inc(prep_a, 1)
                act.wait_ge(prep_p, 4)
                act.activation(wfcT[:, :], PB[7], ACT.Copy).then_inc(prep_a, 1)
                act.wait_ge(prep_p, 5)
                act.activation(wprT[:, :, :], PB[4].rearrange("p (c d) -> p c d", c=4), ACT.Copy).then_inc(prep_a, 1)
                act.wait_ge(prep_p, 6)
                act.activation(a12[:, :, :], PB[5][:, 0:2 * D].rearrange("p (k d) -> p k d", k=2), ACT.Copy
                               ).then_inc(prep_a, 1)
                act.wait_ge(prep_p, 7)
                act.activation(mfreq[:, :], PB[6][:, 0:D], ACT.Copy, scale=1.0 / D).then_inc(prep_a, 1)

            def ctx_turned(b):
                if b >= 2:
                    act.wait_ge(ctx_out[b % 2], 16 * (b // 2))
                for m in range(4):
                    k = min(4 * P, S2 - m * 4 * P)
                    act.wait_ge(ctx_t, 4 * b + m + 1)
                    act.activation(ctxT[:, b % 2, m * 4 * P:m * 4 * P + k], PB[4 + m][:, 0:k], ACT.Copy
                                   ).then_inc(ctx_e, 1)

            def normT(s):
                for m in range(2):
                    act.wait_ge(ln_t, 2 * s + m + 1)
                    act.activation(xnT[:, m * 512:m * 512 + 512], PB[m], ACT.Copy).then_inc(ln_xt, 1)

            def k_split(r):
                g = r.ctx
                w = S2 // 4
                for b in range(B):
                    n = B * g + b
                    if r.layer == 0:
                        if b == 2:
                            weights()
                        if b:
                            ctx_turned(b)
                    if r.layer == 1 and b == 0:
                        act.wait_ge(lk_out, 16 * 12)
                    if n >= 2:
                        act.wait_ge(k_out[b % 2], 48 * (n // 2))
                    for c in range(4):
                        lo = c * w + min(c, 1)
                        act.wait_ge(k_ps, 4 * n + c + 1)
                        act.activation(k1c[:, b % 2, lo:lo + w + (c == 0)], PB[c][:, 0:w + (c == 0)], ACT.Identity,
                                       bias=col(BK[r.index])).then_inc(k_1, 1)

            def q_split(l):
                for m in range(2):
                    act.wait_ge(q_f, 2 * l + m + 1)
                    if l:
                        act.wait_ge(q_out, 16 * 12 * l)
                    act.activation(q1c[:, m * 512:m * 512 + 512], qf[:, m * 512:m * 512 + 512], ACT.Copy
                                   ).then_inc(q_1, 1)

            def local_split():
                for i in range(2):
                    act.wait_ge(k_out[i], 48 * (B // 2))
                for m in range(2):
                    act.wait_ge(lk_ps, m + 1)
                    act.activation(k1c[:, 0, m * 512:m * 512 + 512], PB[2 + m], ACT.Identity,
                                   bias=col(BK[LOCAL])).then_inc(lk_1, 1)

            def attention(r):
                def evac(n):
                    act.wait_ge(pv, FREE_PT + r.step0 + (n + 1) * r.kt)
                    act.activation(o_all[:, n, :], po[:, 0:S], ACT.Copy).then_inc(o_ok, 1)

                def unit(n, par, prev=True):
                    for s in range(r.kt):
                        g = (par * r.kt + s) % 2
                        rows_ = r.keys(s)
                        act.wait_ge(pv, FREE_PT - 1 + r.step0 + n * r.kt + s)
                        for h in range(PAIRS):
                            act.wait_ge(fill, r.fill0 + n * r.fills + PAIRS * s + h + 1)
                            bank = pe_[r.banks[par * r.fills + PAIRS * s + h]]
                            act.activation(pt[g][0:rows_, 2 * h:2 * h + 2, :],
                                           bank[0:rows_, :].rearrange("p (i q) -> p i q", q=S),
                                           ACT.Exp).then_inc(exped, 1)
                        if s == 0 and prev:
                            evac(n - 1)

                unit(0, 0, prev=False)
                with act.Fori(0, UNITS // 2 - 1) as t:
                    unit(2 * t + 1, 1)
                    unit(2 * t + 2, 0)
                unit(UNITS - 1, 1)
                evac(UNITS - 1)

            def post(l):
                for m in range(2):
                    act.wait_ge(on_t, 2 * l + m + 1)
                    act.activation(onT[:, m * 512:m * 512 + 512], PB[4 + m], ACT.Copy).then_inc(on_e, 1)

            def ffn0():
                for T in range(NT):
                    act.wait_ge(f_up, T + 1)
                    act.activation(h0[:, T, :], PB[2 + T % 4], ACT.Gelu).then_inc(f_act, 1)
                for m in range(2):
                    for c in range(4):
                        act.wait_ge(f_t, 4 * m + c + 1)
                        act.activation(hT[m][:, c, :], PB[c], ACT.Identity, scale=col("L0_ffn_ln_w", c),
                                       bias=col("L0_ffn_ln_b", c)).then_inc(f_ht, 1)

            def route(which):
                act.wait_ge(r_v, ROUTE_V[which][0])
                act.activation(lex[:, :, :], lsh[:, :, :], ACT.Exp).then_inc(r_a, 1)
                for m in range(2):
                    act.wait_ge(r_ct, 2 * which + m + 1)
                    act.activation(combT[:, m * 512:m * 512 + 512], PB[2 + m][0:E1, :], ACT.Copy).then_inc(r_cc, 1)

            def experts(which, hid, func):
                cc = hid // P
                up0 = which and 2 * E1 * (HID1 // P)
                with act.Fori(0, E1 // 2) as t:
                    for k in range(2):
                        act.wait_ge(e_b, E1 * which + 2 * t + k + 1)
                        for hf in range(2):
                            act.wait_ge(e_dn, FREE_HID + 2 * E1 * which + 2 * (2 * t + k) + hf - 1)
                            for c in range(cc):
                                act.wait_ge(e_up, up0 + (2 * t + k) * 2 * cc + hf * cc + c + 1)
                                act.activation(hT[hf][:, c, :], PB[(hf * cc + c) % 4], func, bias=b1_now[k][:, c:c + 1]).then_inc(e_act, 1)

            ctx_turned(0)
            spread_vectors()
            for l in parts:
                normT(ln_at(l, 0))
                q_split(l)
                if l == 1:
                    local_split()
                for r in done:
                    if r.layer == l and not r.local:
                        k_split(r)
                for r in done:
                    if r.layer == l:
                        attention(r)
                post(l)
                if l in ffns:
                    normT(ln_at(l, 1))
                    if l == 0:
                        ffn0()
                    if l == 1:
                        route(0)
                        experts(0, HID1, ACT.Gelu)
                    if l == 3:
                        route(1)
                        experts(1, HID3, ACT.Relu)

        @block.vector
        def _(dve):
            dve.memset(cols_raw[:, :], 0.0).then_inc(dconst, 1)
            dve.memset(rows[0:1, :], 0.0).then_inc(dconst, 1)
            dve.memset(gate_in[:, :, :, :], 0.0).then_inc(dconst, 1)
            dve.memset(one16[:, :], 1.0).then_inc(dconst, 1)
            dve.memset(v_all[:, :, FULL, :], 0.0).then_inc(dconst, 1)
            for m in qp1 + qp2:
                dve.memset(m[:, :, :], 0.0).then_inc(dconst, 1)
            def weights():
                dve.wait_ge(dconst, 5)
                dve.wait_ge(ld_fc, 32)
                dve.tensor_reduce(wabs[:, 0:1], wfc_raw[:, :, :].rearrange("p c d -> p (c d)"), AX.X, ALU.add,
                                  apply_absolute_value=True).then_inc(prep_w, 1)
                dve.tensor_reduce(wabs[:, 1:2], wpr_raw[:, :], AX.X, ALU.add, apply_absolute_value=True).then_inc(prep_w, 1)
                dve.wait_ge(prep_p0, 1)
                half = 0.5 / (HID0 * D)
                dve.tensor_scalar(whalf[:, 0, :], PB[7][:, 0:2], half, 0.5e-6, ALU.mult, ALU.add).then_inc(prep_w, 1)
                dve.wait_ge(prep_w, 3)
                dve.tensor_scalar(whalf[:, 1, :], whalf[:, 0, :], -1.0, None, ALU.mult).then_inc(prep_w, 1)
                dve.wait_ge(prep_w, 4)
                for k, src in enumerate((wfc_raw[:, :, :].rearrange("p c d -> p (c d)"), wpr_raw[:, :])):
                    dve.tensor_scalar(tern[:, k, :], src, whalf[:, 0, k:k + 1], None, ALU.is_gt).then_inc(prep_w, 1)
                    dve.tensor_scalar(tern_neg[:, k, :], src, whalf[:, 1, k:k + 1], None, ALU.is_lt).then_inc(prep_w, 1)
                dve.wait_ge(prep_w, 8)
                for k in range(2):
                    dve.tensor_tensor(tern[:, k, :], tern[:, k, :], tern_neg[:, k, :], ALU.subtract).then_inc(prep_w, 1)
                dve.wait_ge(ld_gate, 32 * B)
                dve.tensor_reduce(gate[:, :, :], gate_in[:, :, :, :], AX.X, ALU.add, apply_absolute_value=True
                                  ).then_inc(prep_v, 1)
                dve.wait_ge(prep_a, 6)
                dve.tensor_scalar(gate_e[:, :, :], gate_e[:, :, :], 1.0, None, ALU.add).then_inc(prep_v, 1)
                dve.wait_ge(prep_v, 2)
                dve.reciprocal(gate[:, :, :], gate_e[:, :, :]).then_inc(prep_v, 1)
                dve.tensor_scalar(lgate[:, 1:2], lgate[:, 0:1], 1.0, None, ALU.add).then_inc(prep_v, 1)
                dve.wait_ge(prep_v, 4)
                dve.reciprocal(lgate[:, 0:1], lgate[:, 1:2]).then_inc(prep_v, 1)
                dve.wait_ge(prep_v, 5)
                dve.tensor_scalar(lgate[:, 2:3], lgate[:, 0:1], -1.0, 1.0, ALU.mult, ALU.add).then_inc(prep_v, 1)
                dve.wait_ge(ld_mask, 16)
                dve.tensor_copy(mask01[:, :, :], mask8[:, :, :]).then_inc(prep_v, 1)
                for c, (lo, w, nb) in enumerate(chunk_cols(S2)):
                    for z in range(nb):
                        at = lo + z * (S2 // 4)
                        dve.tensor_scalar(mask_add[:, :, 2 * c + z, 0:w], mask8[:, :, at:at + w], -BIG, None, ALU.mult
                                          ).then_inc(prep_v, 1)
                dve.wait_ge(prep_v, 11)

            dve.sem_inc(score_free, FREE_SCORE)
            dve.sem_inc(e_acc, FREE_ACC)
            dve.wait_ge(ld_x, 16)

            def norm(s):
                if s:
                    dve.wait_ge(x_ok, NT * s)
                for T in range(NT):
                    dve.bn_stats(stats[:, T, :], x[:, T, :]).then_inc(ln_st, 1)
                for T in range(NT):
                    dve.wait_ge(ln_st, NT * s + T + 1)
                    dve.bn_aggr(mv[:, T, :], stats[:, T, :]).then_inc(ln_mv, 1)
                dve.wait_ge(ln_rs, s + 1)
                for T in range(NT):
                    dve.tensor_scalar(xn[:, T, :], x[:, T, :], mv[:, T, 0:1], rstd[:, T:T + 1],
                                      ALU.subtract, ALU.mult).then_inc(ln_xn, 1)

            def k_split(r):
                g = r.ctx
                w = S2 // 4
                for b in range(B):
                    n = B * g + b
                    if r.layer == 0 and b == 2:
                        weights()
                    if r.layer == 1 and b == 0:
                        dve.wait_ge(lk_out, 16 * 12)
                    if n >= 2:
                        dve.wait_ge(k_out[b % 2], 48 * (n // 2))
                    for c in range(4):
                        lo = c * w + min(c, 1)
                        hi = lo + w + (c == 0)
                        dve.wait_ge(k_1, 4 * n + c + 1)
                        dve.scalar_tensor_tensor(out=k2c[:, b % 2, lo:hi], in0=PB[c][:, 0:hi - lo],
                                                 scalar=col(BK[r.index]), in1=k1c[:, b % 2, lo:hi],
                                                 op0=ALU.add, op1=ALU.subtract).then_inc(k_2, 1)
                    for c in range(4):
                        k = 4 if c < 3 else 1
                        pr = P if c < 3 else TAIL
                        dve.wait_ge(v_ps, 4 * n + c + 1)
                        dve.tensor_tensor(v_all[0:pr, b, 4 * c:4 * c + k, :],
                                          PB[4 + c][0:pr, 0:k * VW].rearrange("p (k d) -> p k d", k=k),
                                          row(BV[r.index], D)[0:pr].unsqueeze(1).broadcast_to([pr, k, D]),
                                          ALU.add).then_inc(v_ok, 1)

            def q_split(l):
                if l:
                    dve.wait_ge(q_2, 2 * l)
                for m in range(2):
                    sl = slice(m * 512, m * 512 + 512)
                    dve.wait_ge(q_ps, 2 * l + m + 1)
                    dve.tensor_scalar(qf[:, sl], PB[2 + m], col(BQ[l]), SCALE, ALU.add, ALU.mult).then_inc(q_f, 1)
                for m in range(2):
                    sl = slice(m * 512, m * 512 + 512)
                    dve.wait_ge(q_1, 2 * l + m + 1)
                    dve.tensor_tensor(q2c[:, sl], qf[:, sl], q1c[:, sl], ALU.subtract).then_inc(q_2, 1)

            def local_split():
                dve.wait_ge(padded, 16 * B * (len(RUNS) - 1))
                for m in range(2):
                    sl = slice(m * 512, m * 512 + 512)
                    dve.wait_ge(lk_1, m + 1)
                    dve.scalar_tensor_tensor(out=k2c[:, 0, sl], in0=PB[2 + m], scalar=col(BK[LOCAL]),
                                             in1=k1c[:, 0, sl], op0=ALU.add, op1=ALU.subtract).then_inc(lk_2, 1)
                for m in range(2):
                    dve.wait_ge(lk_ps, 3 + m)
                    dve.tensor_tensor(v_loc[:, 2 * m:2 * m + 2, :, :],
                                      PB[4 + m].rearrange("p (b k d) -> p b k d", b=2, k=2),
                                      row(BV[LOCAL], D).unsqueeze(1).unsqueeze(1).broadcast_to([P, 2, 2, D]),
                                      ALU.add).then_inc(lv_ok, 4)

            def attention(r):
                cpt = len(r.chunks)

                def piece(n, par, k, j, first):
                    qt, c, i = j // (cpt * HG), j // HG % cpt, j % HG
                    lo, w, nb = r.chunks[c]
                    src = pa[r.slot(par, k, first)][:, 0:nb, 0:w]
                    dst = mx[par][:, qt * HG + i, c:c + 1]
                    dve.wait_ge(score, r.use(n, k, first) + 1)
                    if r.mask:
                        dve.wait_ge(score_free, r.use(n, k, first) + (k != r.turn + 1))
                        dve.sem_inc(passed, 1)
                        dve.tensor_tensor_reduce(
                            out=masked[j % 2][:, :, 0:w], in0=src,
                            in1=mask_add[:, qt, 2 * c:2 * c + 2, 0:w],
                            scale=1.0, scalar=-3.0e38, op0=ALU.add, op1=ALU.max,
                            accum_out=dst).then_inc(score_free, 1)
                    else:
                        dve.tensor_reduce(dst, src, AX.XY, ALU.max).then_inc(score_free, 1)

                def split_maxima(n, par, first):
                    dve.wait_ge(score_free, FREE_SCORE + r.use(n, r.uses - 1, first) + 1)
                    dve.tensor_reduce(nm[par][:, :, :].rearrange("p q i -> p (q i)"), mx[par][:, :, 0:cpt], AX.X,
                                      ALU.max, negate=True).then_inc(mx_done, 1)
                    dve.wait_ge(mx_done, 2 * (r.u0 + n) + 1)
                    dve.tensor_scalar(nmc[par][:, :, :], nm[par][:, :, :], -MIN_MAX if r.mask else 3.0e38, None,
                                      ALU.min).then_inc(mx_done, 1)
                    dve.wait_ge(mx_done, 2 * (r.u0 + n) + 2)
                    dve.tensor_copy(m16[par][:, :, 0, :], nmc[par][:, :, :]).then_inc(m_ok, 1)
                    dve.wait_ge(m_ok, 2 * (r.u0 + n) + 1)
                    dve.tensor_tensor(m16[par][:, :, 1, :], nmc[par][:, :, :], m16[par][:, :, 0, :],
                                      ALU.subtract).then_inc(m_ok, 1)

                def keep_rows(par, slot, use):
                    dve.wait_ge(score, use + 1)
                    dve.tensor_copy(ms[par][:, :], pa[slot][:, 0, :].bitcast(F16)[0:2 * HG, 0:S]
                                    ).then_inc(score_free, 1)

                def unit(n, par, first=False):
                    for k, j in r.pieces(first):
                        if j is None:
                            keep_rows(1 - par, r.slot(par, k), r.use(n, k))
                        else:
                            piece(n, par, k, j, first)
                    split_maxima(n, par, first)

                unit(0, 0, first=True)
                with dve.Fori(0, UNITS // 2 - 1) as t:
                    unit(2 * t + 1, 1)
                    unit(2 * t + 2, 0)
                unit(UNITS - 1, 1)
                keep_rows(1, 1, r.use0 + UNITS * r.uses - 1)

            def heads_out(r):
                dst = on_loc if r.local else on
                for T in range(NT):
                    n = NT * r.index + T
                    bank = PB[T % 4].rearrange("p (h c) -> p h c", c=R)
                    dve.wait_ge(o_t, n + 1)
                    dve.tensor_scalar(rec0[:, T, :], bank[:, :, DH], TINY, None, ALU.max).then_inc(o_rec, 1)
                    dve.wait_ge(o_rec, 2 * n + 1)
                    dve.reciprocal(rec[:, T, :], rec0[:, T, :]).then_inc(o_rec, 1)
                    dve.wait_ge(o_rec, 2 * n + 2)
                    coef = 1.0 if r.layer != 1 else lgate[:, 0:1] if r.local else lgate[:, 2:3]
                    dve.scalar_tensor_tensor(
                        out=dst[:, T, :].rearrange("p (h d) -> p h d", d=DH), in0=bank[:, :, 0:DH], scalar=coef,
                        in1=rec[:, T, :].unsqueeze(2).broadcast_to([P, H, DH]), op0=ALU.mult, op1=ALU.mult
                        ).then_inc(o_n, 1)

            def residual(s, bank_of, bias, gate_col, ready, at):
                for m in range(2):
                    dve.wait_ge(ready, at + m + 1)
                    dve.tensor_tensor(ytmp[:, 4 * m:4 * m + 4, :], PB[bank_of + m].rearrange("p (k d) -> p k d", k=4),
                                      row(bias, D).unsqueeze(1).broadcast_to([P, 4, D]), ALU.add).then_inc(y_t, 1)
                    dve.wait_ge(y_t, 2 * s + m + 1)
                    dve.scalar_tensor_tensor(out=x[:, 4 * m:4 * m + 4, :], in0=ytmp[:, 4 * m:4 * m + 4, :],
                                             scalar=tg[:, gate_col:gate_col + 1], in1=x[:, 4 * m:4 * m + 4, :],
                                             op0=ALU.mult, op1=ALU.add).then_inc(x_ok, 4)

            def ffn0():
                for T in range(NT):
                    dve.wait_ge(f_act, T + 1)
                    dve.bn_stats(stats[:, T, :], h0[:, T, :]).then_inc(f_st, 1)
                    dve.wait_ge(f_st, 2 * T + 1)
                    dve.bn_aggr(mv[:, T, :], stats[:, T, :]).then_inc(f_st, 1)
                dve.wait_ge(f_st, 2 * NT)
                dve.tensor_scalar(var_eps[:, :], mv[:, :, 1], LN_EPS, None, ALU.add).then_inc(f_rs, 1)
                dve.wait_ge(f_rs, 2)
                for T in range(NT):
                    dve.tensor_scalar(h0[:, T, :], h0[:, T, :], mv[:, T, 0:1], rstd[:, T:T + 1],
                                      ALU.subtract, ALU.mult).then_inc(f_n, 1)

            def route(which):
                cnt = [ROUTE_V[which][2]]

                def step(ins, n=1):
                    ins.then_inc(r_v, 1)
                    cnt[0] += 1

                dve.wait_ge(r_ps, which + 1)
                step(dve.tensor_tensor(lg[:, :, :], PB[2][:, 0:NT * E1].rearrange("p (t e) -> p t e", e=E1),
                                       (row("L3_ffn_gate_b", E1) if which else row("zero", E1)
                                        ).unsqueeze(1).broadcast_to([P, NT, E1]), ALU.add))
                dve.wait_ge(r_v, cnt[0])
                step(dve.tensor_reduce(lmax[:, :], lg[:, :, :], AX.X, ALU.max))
                dve.wait_ge(r_v, cnt[0])
                step(dve.tensor_tensor(lsh[:, :, :], lg[:, :, :], lmax[:, :].unsqueeze(2).broadcast_to([P, NT, E1]),
                                       ALU.subtract))
                assert cnt[0] == ROUTE_V[which][0]
                dve.wait_ge(r_a, which + 1)
                if which:
                    step(dve.tensor_reduce(lsum[:, :], lex[:, :, :], AX.X, ALU.add))
                    dve.wait_ge(r_v, cnt[0])
                    step(dve.reciprocal(lrec[:, :], lsum[:, :]))
                    dve.wait_ge(r_v, cnt[0])
                    step(dve.tensor_tensor(prob[:, :, :], lex[:, :, :],
                                           lrec[:, :].unsqueeze(2).broadcast_to([P, NT, E1]), ALU.mult))
                    dve.wait_ge(r_v, cnt[0])
                key = prob if which else lg
                val = prob if which else lex
                by_j = key[:, :, :].unsqueeze(2).broadcast_to([P, NT, E1, E1])
                by_e = key[:, :, :].unsqueeze(3).broadcast_to([P, NT, E1, E1])
                step(dve.tensor_tensor(above[:, :, :, :], by_j, by_e, ALU.is_gt))
                step(dve.tensor_tensor(tied[:, :, :, :], by_j, by_e, ALU.is_equal))
                dve.wait_ge(r_v, cnt[0])
                step(dve.tensor_tensor(tied[:, :, :, :], tied[:, :, :, :],
                                       earlier[:, :, :].unsqueeze(1).broadcast_to([P, NT, E1, E1]), ALU.mult))
                dve.wait_ge(r_v, cnt[0])
                step(dve.tensor_tensor(above[:, :, :, :], above[:, :, :, :], tied[:, :, :, :], ALU.add))
                dve.wait_ge(r_v, cnt[0])
                step(dve.tensor_reduce(rank[:, :, :], above[:, :, :, :], AX.X, ALU.add))
                dve.wait_ge(r_v, cnt[0])
                step(dve.scalar_tensor_tensor(out=(comb if which else chosen)[:, :, :], in0=rank[:, :, :], scalar=1.5,
                                              in1=val[:, :, :], op0=ALU.is_lt, op1=ALU.mult))
                dve.wait_ge(r_v, cnt[0])
                if not which:
                    step(dve.tensor_reduce(lsum[:, :], chosen[:, :, :], AX.X, ALU.add))
                    dve.wait_ge(r_v, cnt[0])
                    step(dve.reciprocal(lrec[:, :], lsum[:, :]))
                    dve.wait_ge(r_v, cnt[0])
                    step(dve.tensor_tensor(comb[:, :, :], chosen[:, :, :],
                                           lrec[:, :].unsqueeze(2).broadcast_to([P, NT, E1]), ALU.mult))
                assert cnt[0] == ROUTE_V[which][1], cnt
                for m in range(2):
                    dve.wait_ge(r_b, 2 * which + m + 1)
                    dve.tensor_copy(acc[:, 4 * m:4 * m + 4, :], PB[6 + m].rearrange("p (k d) -> p k d", k=4)
                                    ).then_inc(r_acc, 1)

            def experts(which):
                dve.wait_ge(r_acc, 2 * which + 2)
                by_expert = comb[:, :, :].rearrange("p t e -> p e t")
                with dve.Fori(0, E1 // 2) as t:
                    for k in range(2):
                        for hf in range(2):
                            q = 2 * E1 * which + 2 * (2 * t + k) + hf
                            dve.wait_ge(e_dn, FREE_HID + q + 1)
                            dve.wait_ge(e_acc, 4 * q + 4)
                            for T in range(4):
                                dve.scalar_tensor_tensor(
                                    out=acc[:, 4 * hf + T, :], in0=PB[4 + hf][:, T * D:T * D + D],
                                    scalar=by_expert[:, 2 * t + k, 4 * hf + T:4 * hf + T + 1], in1=acc[:, 4 * hf + T, :],
                                    op0=ALU.mult, op1=ALU.add).then_inc(e_acc, 1)

            def experts_out(which, s, gate_col):
                dve.wait_ge(e_acc, 8 + 4 * 2 * E1 * (which + 1))
                for m in range(2):
                    dve.scalar_tensor_tensor(out=x[:, 4 * m:4 * m + 4, :], in0=acc[:, 4 * m:4 * m + 4, :],
                                             scalar=tg[:, gate_col:gate_col + 1], in1=x[:, 4 * m:4 * m + 4, :],
                                             op0=ALU.mult, op1=ALU.add).then_inc(x_ok, 4)

            n_res = 0
            for l in parts:
                norm(ln_at(l, 0))
                q_split(l)
                if l == 1:
                    local_split()
                for r in done:
                    if r.layer == l and not r.local:
                        k_split(r)
                for r in done:
                    if r.layer == l:
                        attention(r)
                        heads_out(r)
                residual(n_res, 6, BO[l], l, y_ps, 2 * l)
                n_res += 1
                if l in ffns:
                    norm(ln_at(l, 1))
                    if l == 0:
                        ffn0()
                        residual(n_res, 6, None, 4, f_dn, 0)
                        n_res += 1
                    if l == 2:
                        residual(n_res, 6, "L2_ffn_bias", 6, f_dn, 2)
                        n_res += 1
                    if l in (1, 3):
                        route(l // 2)
                        experts(l // 2)
                        experts_out(l // 2, n_res, 4 + l)

        @block.tensor
        def _(pe):
            pe.wait_ge(consts, 12)
            pe.sem_inc(pv, FREE_PT)
            pe.sem_inc(e_dn, FREE_HID)

            def ctx_turn(b):
                pe.wait_ge(ctx_in[b % 2], 32 * (b // 2 + 1))
                for m in range(4):
                    if b:
                        pe.wait_ge(v_ok, 4 * (b - 1) + m + 1)
                    if b == 2:
                        pe.wait_ge(prep_a, 10)
                    for k in range(4 * m, min(4 * m + 4, KT)):
                        pr = P if k < FULL else TAIL
                        ins = pe.transpose(PB[4 + m][:, (k % 4) * P:(k % 4) * P + pr], ctx_raw[0:pr, b % 2, k, :],
                                           ident[0:pr, 0:pr])
                    ins.then_inc(ctx_t, 1)

            def spread_vectors():
                pe.wait_ge(ld_cols, 16 * len(COLS))
                pe.transpose(PB[0][:, 0:NCOL], cols_raw[:, :], ident[0:NCOL, 0:NCOL]).then_inc(prep_p, 1)
                pe.wait_ge(ld_rows, 16 * (len(ROWS) - 1))
                pe.matmul(PB[1], ones[0:1, :], rows[0:1, 0:512], start=True, stop=True).then_inc(prep_p, 1)
                pe.matmul(PB[2][:, 0:NROW - 512], ones[0:1, :], rows[0:1, 512:NROW], start=True, stop=True
                          ).then_inc(prep_p, 1)
                pe.wait_ge(prep_a, 3)
                pe.wait_ge(ld_w, 16 * (len(SQUARE) - len(TURNED)))

            def weights():
                pe.wait_ge(k_2, 8)
                pe.wait_ge(v_ok, 8)
                pe.wait_ge(ld_wt, 16 * len(TURNED))
                for m in range(len(TURNED)):
                    ins = pe.transpose(PB[m // 4][:, (m % 4) * D:(m % 4) * D + D], wraw[:, m, :], ident[:, :])
                    if m % 4 == 3 or m == len(TURNED) - 1:
                        ins.then_inc(w_turned, 1)
                pe.wait_ge(prep_w, 2)
                pe.matmul(PB[7][:, 0:2], ones[:, :], wabs[:, :], start=True, stop=True).then_inc(prep_p0, 1)
                pe.wait_ge(prep_w, 10)
                for c in range(4):
                    ins = pe.transpose(PB[7][:, c * P:c * P + P], tern[:, 0, c * D:c * D + D], ident[:, :])
                ins.then_inc(prep_p, 1)
                for c in range(4):
                    ins = pe.transpose(PB[4][:, c * D:c * D + D], tern[:, 1, c * P:c * P + P], ident[:, :])
                ins.then_inc(prep_p, 1)
                pe.wait_ge(ld_misc, 16 * 9)
                C_, S_, N_ = dft[:, 0, :], dft[:, 1, :], dft[:, 2, :]
                pe.matmul(PB[5][:, 0:D], wfreq[:, 0, :], C_, start=True, stop=False)
                pe.matmul(PB[5][:, 0:D], wfreq[:, 1, :], S_, start=False, stop=True)
                pe.matmul(PB[5][:, D:2 * D], wfreq[:, 1, :], C_, start=True, stop=False)
                pe.matmul(PB[5][:, D:2 * D], wfreq[:, 0, :], N_, start=False, stop=True).then_inc(prep_p, 1)
                pe.wait_ge(prep_a, 9)
                pe.matmul(PB[6][:, 0:D], a12[:, 0, :], C_, start=True, stop=False)
                pe.matmul(PB[6][:, 0:D], a12[:, 1, :], N_, start=False, stop=True).then_inc(prep_p, 1)
                pe.wait_ge(w_kept, 4)

            def normT(s):
                for T in range(NT):
                    pe.wait_ge(ln_xn, NT * s + T + 1)
                    ins = pe.transpose(PB[T // 4][:, (T % 4) * P:(T % 4) * P + P], xn[:, T, :], ident[:, :])
                    if T % 4 == 3:
                        ins.then_inc(ln_t, 1)

            def kv(r):
                g = r.ctx
                w = S2 // 4
                pe.wait_ge(q_f, 2 * (r.layer + 1))
                for b in range(B):
                    n = B * g + b
                    if r.layer == 0:
                        if b == 2:
                            weights()
                        if b:
                            ctx_turn(b)
                        pe.wait_ge(ctx_e, 4 * (b + 1))
                    else:
                        pe.wait_ge(c_ld[b % 2], 16 * ((n - B) // 2 + 1))
                    for c in range(4):
                        if b:
                            pe.wait_ge(k_2, 4 * (n - 1) + c + 1)
                        lo = c * w + min(c, 1)
                        pe.matmul(PB[c][:, 0:w + (c == 0)], sq(WK[r.index]), ctxT[:, b % 2, lo:lo + w + (c == 0)],
                                  start=True, stop=True).then_inc(k_ps, 1)
                    for c in range(4):
                        if b:
                            pe.wait_ge(v_ok, 4 * (n - 1) + c + 1)
                        for k in range(4 * c, min(4 * c + 4, KT)):
                            pr = P if k < FULL else TAIL
                            ins = pe.matmul(PB[4 + c][0:pr, (k % 4) * VW:(k % 4) * VW + VW],
                                            ctxT[:, b % 2, k * P:k * P + pr], sq(WV[r.index]), start=True, stop=True)
                        ins.then_inc(v_ps, 1)
                pe.wait_ge(k_2, 4 * B * (g + 1))
                pe.wait_ge(v_ok, 4 * B * (g + 1))

            def queries(l):
                for m in range(2):
                    pe.wait_ge(ln_xt, 2 * ln_at(l, 0) + m + 1)
                    pe.matmul(PB[2 + m], sq(WQ[l]), xnT[:, m * 512:m * 512 + 512], start=True, stop=True
                              ).then_inc(q_ps, 1)

            def local_kv():
                pe.wait_ge(q_f, 4)
                for m in range(2):
                    pe.matmul(PB[2 + m], sq(WK[LOCAL]), xnT[:, m * 512:m * 512 + 512], start=True, stop=True
                              ).then_inc(lk_ps, 1)
                for m in range(2):
                    for T in range(4 * m, 4 * m + 4):
                        ins = pe.matmul(PB[4 + m][:, (T % 4) * VW:(T % 4) * VW + VW], xnT[:, T * P:T * P + P],
                                        sq(WV[LOCAL]), start=True, stop=True)
                    ins.then_inc(lk_ps, 1)
                pe.wait_ge(lk_2, 2)
                pe.wait_ge(lv_ok, NT)

            def attention(r):
                cpt = len(r.chunks)

                def turn(par, slot, use):
                    pe.wait_ge(score_free, use + FREE_SCORE - 1)
                    for qt in range(QT):
                        ins = pe.transpose(pa[slot][:, 0, :].bitcast(F16)[0:2 * HG, qt * P:qt * P + P],
                                           m16[par][:, qt, :, :].rearrange("p a i -> p (a i)"), ident16[:, :])
                    ins.then_inc(score, 1)

                def piece(n, par, k, first=False):
                    use, slot = r.use(n, k, first), r.slot(par, k, first)
                    if k == r.turn:
                        pe.wait_ge(m_ok, 2 * (r.u0 + n))
                        turn(1 - par, slot, use)
                        return
                    j = k - (k > r.turn)
                    pe.wait_ge(score_free, use + FREE_SCORE - 1)
                    if k == 0:
                        pe.wait_ge(in1[par], IN_DMAS * (r.u0 + n - par + 2))
                    qt, c, i = j // (cpt * HG), j // HG % cpt, j % HG
                    lo, w, nb = r.chunks[c]
                    for z in range(nb):
                        at = lo + z * (S2 // 4)
                        ins = pe.matmul(pa[slot][:, z, 0:w], qp1[par][:, i, qt * P:qt * P + P],
                                        kp1[par][:, at:at + w], start=True, stop=True)
                    ins.then_inc(score, 1)

                def fills(n, par, s, h):
                    f = par * r.fills + PAIRS * s + h
                    pe.wait_ge(exped, FREE_EXP + r.fill0 + n * r.fills + PAIRS * s + h - r.back(f) + 1)
                    if s == 0 and h == 0:
                        pe.wait_ge(in2[par], IN_DMAS * (r.u0 + n - par + 2))
                        pe.wait_ge(m_in[par], 8 * (r.u0 + n - par + 2))
                    bank, rows_ = pe_[r.banks[f]], r.keys(s)
                    ins = pe.matmul(bank[0:rows_, :], kp2[par][:, s * P:s * P + rows_],
                                    qp2[par][:, 2 * h:2 * h + 2, :], start=True, stop=True, skip_group_check=r.mask)
                    if r.mask:
                        for qt in range(QT):
                            ins = pe.matmul(bank[0:rows_, :].rearrange("p (i q) -> p i q", q=S)[:, :, qt * P:qt * P + P],
                                            mask01[:, qt, s * P:s * P + rows_],
                                            mask_eye[:, :].unsqueeze(1).broadcast_to([P, 2, P]),
                                            start=False, stop=True, skip_group_check=True)
                    ins.then_inc(fill, 1)

                def product(n, par, s):
                    if s == 0:
                        pe.wait_ge(vg_ok, r.u0 + n + 1)
                        pe.wait_ge(o_ok, r.u0 + n + 1)
                    pe.wait_ge(exped, FREE_EXP + r.fill0 + n * r.fills + PAIRS * (s + 1))
                    g, rows_ = (par * r.kt + s) % 2, r.keys(s)
                    for j in range(HG):
                        ins = pe.matmul(po[R * j:R * j + R, 0:S], vg[par][0:rows_, s, j, :], pt[g][0:rows_, j, :],
                                        start=(s == 0), stop=(s == r.kt - 1))
                    ins.then_inc(pv, 1)

                def unit(n, par, prev=True, ahead="unit"):
                    todo = [(1, k) for k in range(r.ahead, r.uses)] if ahead else []
                    todo += [(2, k) for k in range(r.ahead)] if ahead == "unit" else []
                    total, given = len(todo), 0
                    for s in range(r.kt):
                        for h in range(PAIRS):
                            fills(n, par, s, h)
                            while given < (PAIRS * s + h + 1) * total // r.fills:
                                d, k = todo[given]
                                piece(n + d, (par + d) % 2, k)
                                given += 1
                        if s:
                            product(n, par, s - 1)
                        elif prev:
                            product(n - 1, 1 - par, r.kt - 1)

                for k, _ in r.pieces(first=True):
                    piece(0, 0, k, first=True)
                for k in range(r.ahead):
                    piece(1, 1, k)
                unit(0, 0, prev=False)
                with pe.Fori(0, UNITS // 2 - 2) as t:
                    unit(2 * t + 1, 1)
                    unit(2 * t + 2, 0)
                unit(UNITS - 3, 1)
                unit(UNITS - 2, 0, ahead="rest")
                pe.wait_ge(m_ok, 2 * (r.u0 + UNITS))
                turn(1, 1, r.use0 + UNITS * r.uses - 1)
                unit(UNITS - 1, 1, ahead=None)
                product(UNITS - 1, 1, r.kt - 1)

            def heads_out(r):
                for T in range(NT):
                    b, qt = T // QT, T % QT
                    if T == 0:
                        pe.wait_ge(o_ok, 1 + r.u0 + UNITS)
                    if T >= 4:
                        pe.wait_ge(o_n, NT * r.index + T - 3)
                    for g in range(HG):
                        ins = pe.transpose(PB[T % 4][:, g * P:g * P + P], o_all[:, HG * b + g, qt * P:qt * P + P],
                                           ident[:, :])
                    ins.then_inc(o_t, 1)
                pe.wait_ge(o_n, NT * r.index + NT)

            def project(l):
                if l == 1:
                    pe.wait_ge(o_add, 1)
                for T in range(NT):
                    ins = pe.transpose(PB[4 + T // 4][:, (T % 4) * P:(T % 4) * P + P], on[:, T, :], ident[:, :])
                    if T % 4 == 3:
                        ins.then_inc(on_t, 1)
                for T in range(NT):
                    if T % 4 == 0:
                        pe.wait_ge(on_e, 2 * l + T // 4 + 1)
                    ins = pe.matmul(PB[6 + T // 4][:, (T % 4) * D:(T % 4) * D + D], onT[:, T * P:T * P + P],
                                    sq(WO[l]), start=True, stop=True)
                    if T % 4 == 3:
                        ins.then_inc(y_ps, 1)

            def ffn0():
                for T in range(NT):
                    if T % 4 == 0:
                        pe.wait_ge(ln_xt, 2 * ln_at(0, 1) + T // 4 + 1)
                    if T >= 4:
                        pe.wait_ge(f_act, T - 3)
                    pe.matmul(PB[2 + T % 4], xnT[:, T * P:T * P + P], wfcT[:, :], start=True, stop=True
                              ).then_inc(f_up, 1)
                pe.wait_ge(f_act, NT)
                for m in range(2):
                    for c in range(4):
                        if m:
                            pe.wait_ge(f_ht, c + 1)
                        for k in range(4):
                            pe.wait_ge(f_n, 4 * m + k + 1)
                            ins = pe.transpose(PB[c][:, k * P:k * P + P], h0[:, 4 * m + k, c * P:c * P + P],
                                               ident[:, :])
                        ins.then_inc(f_t, 1)
                for m in range(2):
                    for k in range(4):
                        for c in range(4):
                            pe.wait_ge(f_ht, 4 * m + c + 1)
                            ins = pe.matmul(PB[6 + m][:, k * D:k * D + D], hT[m][:, c, k * P:k * P + P],
                                            wprT[:, c, :], start=(c == 0), stop=(c == 3))
                    ins.then_inc(f_dn, 1)

            def ffn2():
                for T in range(NT):
                    if T % 4 == 0:
                        pe.wait_ge(ln_xt, 2 * ln_at(2, 1) + T // 4 + 1)
                    ins = pe.matmul(PB[6 + T // 4][:, (T % 4) * D:(T % 4) * D + D], xnT[:, T * P:T * P + P],
                                    mfreq[:, :], start=True, stop=True)
                    if T % 4 == 3:
                        ins.then_inc(f_dn, 1)

            def route(which, l):
                for T in range(NT):
                    if T % 4 == 0:
                        pe.wait_ge(ln_xt, 2 * ln_at(l, 1) + T // 4 + 1)
                    ins = pe.matmul(PB[2][:, T * E1:T * E1 + E1], xnT[:, T * P:T * P + P], wr[:, which, :],
                                    start=True, stop=True)
                ins.then_inc(r_ps, 1)
                pe.wait_ge(r_v, ROUTE_V[which][1])
                for T in range(NT):
                    ins = pe.transpose(PB[2 + T // 4][0:E1, (T % 4) * P:(T % 4) * P + P], comb[:, T, :], ident[:, :])
                    if T % 4 == 3:
                        ins.then_inc(r_ct, 1)
                for T in range(NT):
                    if T % 4 == 0:
                        pe.wait_ge(r_cc, 2 * which + T // 4 + 1)
                    ins = pe.matmul(PB[6 + T // 4][:, (T % 4) * D:(T % 4) * D + D], combT[:, T * P:T * P + P],
                                    b2[:, which, :], start=True, stop=True)
                    if T % 4 == 3:
                        ins.then_inc(r_b, 1)

            def experts(which, hid):
                cc = hid // P
                act0 = which and 2 * E1 * (HID1 // P)
                with pe.Fori(0, E1 // 2) as t:
                    for k in range(2):
                        e = 2 * t + k
                        pe.wait_ge(e_w[k], 16 * (E1 * which + 2 * t + 2))
                        for hf in range(2):
                            for c in range(cc):
                                pe.wait_ge(e_act, FREE_UP + act0 + e * 2 * cc + hf * cc + c - 3)
                                pe.matmul(PB[(hf * cc + c) % 4], w_up[k][:, c * P:c * P + P],
                                          xnT[:, hf * 512:hf * 512 + 512], start=True, stop=True).then_inc(e_up, 1)
                        for hf in range(2):
                            q = 2 * E1 * which + 2 * e + hf
                            pe.wait_ge(e_acc, 4 * q + 4)
                            pe.wait_ge(e_act, FREE_UP + act0 + e * 2 * cc + (hf + 1) * cc)
                            for T in range(4):
                                for c in range(cc):
                                    ins = pe.matmul(PB[4 + hf][:, T * D:T * D + D], hT[hf][:, c, T * P:T * P + P],
                                                    w_dn[k][:, c, :], start=(c == 0), stop=(c == cc - 1))
                            ins.then_inc(e_dn, 1)

            ctx_turn(0)
            spread_vectors()
            for l in parts:
                normT(ln_at(l, 0))
                queries(l)
                if l == 1:
                    local_kv()
                for r in done:
                    if r.layer == l and not r.local:
                        kv(r)
                for r in done:
                    if r.layer == l:
                        attention(r)
                        heads_out(r)
                project(l)
                if l in ffns:
                    normT(ln_at(l, 1))
                    if l == 0:
                        ffn0()
                    if l == 2:
                        ffn2()
                    if l in (1, 3):
                        route(l // 2, l)
                        experts(l // 2, HID1 if l == 1 else HID3)


_OUT = (B, S, D)
_NAMES = (["x", "ctx_1024", "ctxb_2048x8", "mask_1x1xSxS2_bk1"] + [n for n, _ in SQUARE] + [n for n, _ in COLS]
          + [n for n, _ in ROWS if n != "zero"]
          + ["L0_ffn_W_fc", "L0_ffn_W_proj", "L1_ffn_Wr", "L1_ffn_W1", "L1_ffn_W2", "L1_ffn_b2",
             "L2_ffn_w_freq_real", "L2_ffn_w_freq_imag", "L3_ffn_gate_w", "L3_ffn_w1", "L3_ffn_w2", "L3_ffn_b2"])


def kernel(last=4.0, **inputs):
    import numpy as np
    import concourse.bacc as bacc
    from concourse.bass_utils import run_bass_kernel_spmd

    nc = bacc.Bacc("TRN2", target_bir_lowering=False, num_devices=1)
    arrays, args = {}, {}
    angle = 2.0 * np.pi * (np.outer(np.arange(D), np.arange(D)) % D) / D
    tables = {"dft_cos": np.cos(angle), "dft_sin": np.sin(angle), "dft_nsin": -np.sin(angle)}
    for name in _NAMES + list(tables):
        v = tables[name].astype(np.float32) if name in tables else np.ascontiguousarray(inputs[name])
        if v.ndim == 0:
            v = v.reshape(1)
        arrays[f"in_{name}"] = v
        args[name] = nc.dram_tensor(f"in_{name}", v.shape, mybir.dt.from_np(v.dtype), kind="ExternalInput").ap()
    out = nc.dram_tensor("out", _OUT, F32, kind="ExternalOutput").ap()
    flamingo(nc, args, out, last)
    got = run_bass_kernel_spmd(nc, [arrays], core_ids=[0])
    return got.results[0]["out"]
```

```python
from contextlib import ExitStack

import concourse.bass as bass
from concourse import mybir

F32 = mybir.dt.float32
F16 = mybir.dt.float16
U8 = mybir.dt.uint8
ALU = mybir.AluOpType
ACT = mybir.ActivationFunctionType
AX = mybir.AxisListType

P = 128
B, S, D = 4, 256, 128
H, DH = 16, 8
S2 = 1601
TOK = B * S
LAYERS = 4
NT = TOK // P
QT = S // P
HG = 4
UNITS = B * H // HG
PAUSE = 2
PAIRS = HG // 2
R = 32
KQ = 3 * DH
KM = KQ + 2
SCALE = 1.0 / DH ** 0.5
LN_EPS = 1e-5
BIG = 60000.0
MIN_MAX = -30000.0
TINY = 1e-30
PRODUCTS = ((1, 0), (0, 0), (0, 1))
WSCALE = 256.0
FULL = S2 // P
TAIL = S2 - FULL * P
KT = FULL + 1
LKT = S // P
VW = D
E1, HID0, HID1, HID3 = 8, 512, 512, 256




def chunk_cols(nk):
    if nk == S2:
        w = S2 // 4
        return [(0, w + 1, 2), (2 * w + 1, w, 2)]
    return [(0, nk, 1)]


def ring(n, size):
    banks = [f % size for f in range(n)]
    if banks[-1] == banks[0]:
        banks[-1] = banks[-3]
    return banks


class Run:

    def __init__(self, index, layer, nk, mask, before):
        self.index, self.layer, self.nk, self.mask = index, layer, nk, mask
        self.ctx = {0: 0, 2: 1, 3: 2, 4: 3}.get(index)
        self.local = nk == S
        self.turn, self.ahead = (2, 9) if self.local else (3, 7)
        self.pause = 0 if self.local else PAUSE
        self.tail, self.gap = (3, 2) if self.local else (16, 6)
        self.chunks = chunk_cols(nk)
        self.kt = (nk + P - 1) // P
        self.fills = PAIRS * self.kt
        self.c = QT * HG * len(self.chunks)
        self.uses = self.c + 1
        self.banks = ring(2 * self.fills, 3)
        self.u0 = before.u0 + UNITS if before else 0
        self.use0 = before.use0 + UNITS * before.uses if before else 0
        self.fill0 = before.fill0 + UNITS * before.fills if before else 0
        self.step0 = before.step0 + UNITS * before.kt if before else 0

    def keys(self, s):
        return min(P, self.nk - s * P)

    def back(self, f):
        return next(d for d in range(1, 9) if self.banks[f - d] == self.banks[f])

    def use(self, n, k, first=False):
        return self.use0 + (k - (k > self.turn) if first else n * self.uses - 1 + k)

    def slot(self, par, k, first=False):
        return (k - (k > self.turn) if first else par + 1 + k) % 2

    def pieces(self, first=False):
        return [(k, None if k == self.turn else k - (k > self.turn)) for k in range(self.uses) if not (first and k == self.turn)]


def runs():
    out = []
    for layer, nk, mask in ((0, S2, False), (1, S, False), (1, S2, False), (2, S2, False), (3, S2, True)):
        out.append(Run(len(out), layer, nk, mask, out[-1] if out else None))
    return out


RUNS = runs()
LOCAL = 1
IN_DMAS = 16 * (1 + HG) // 2
FREE_SCORE, FREE_EXP, FREE_PT, FREE_PV = 2, 5, 2, 1
FREE_UP, FREE_HID, FREE_ACC, FREE_W = 4, 3, 8, 4
ROUTE_V = [(3, 12, 0), (15, 24, 12)]
SQUARE = [("L0_xattn_Wq", 0), ("L0_xattn_Wk", 0), ("L0_xattn_Wv", 0), ("L0_xattn_Wo", 0),
          ("L1_xattn_q_w", 1), ("L1_xattn_k_w", 1), ("L1_xattn_v_w", 1), ("L1_xattn_kg_w", 1),
          ("L1_xattn_vg_w", 1), ("L1_xattn_out_w", 1),
          ("L2_xattn_wq", 1), ("L2_xattn_wk", 1), ("L2_xattn_wv", 1), ("L2_xattn_wo", 1),
          ("L3_xattn_Wq", 1), ("L3_xattn_Wk", 1), ("L3_xattn_Wv", 1), ("L3_xattn_Wo", 1)]
SQ = {n: i for i, (n, _) in enumerate(SQUARE)}
TURNED = [i for i, (_, t) in enumerate(SQUARE) if t]
COLS = [("L1_ffn_b1", 32), ("L3_ffn_b1", 16), ("L0_ffn_ln_w", 4), ("L0_ffn_ln_b", 4), ("L0_xattn_bq", 1),
        ("L0_xattn_bk", 1), ("L1_xattn_q_b", 1), ("L1_xattn_k_b", 1), ("L1_xattn_kg_b", 1)]
COL, _at = {}, 0
for _n, _k in COLS:
    COL[_n] = _at
    _at += _k
NCOL = _at + 1
ZCOL = _at
ROWS = [("L0_xattn_bv", D), ("L0_xattn_bo", D), ("L1_xattn_v_b", D), ("L1_xattn_vg_b", D), ("L1_xattn_out_b", D),
        ("L2_ffn_bias", D), ("zero", D), ("L3_ffn_gate_b", 8), ("g_xattn", 4), ("g_ffn", 4), ("L1_xattn_gate", 1)]
ROW, _at = {}, 0
for _n, _k in ROWS:
    ROW[_n] = _at
    _at += _k
NROW = _at
WQ = ["L0_xattn_Wq", "L1_xattn_q_w", "L2_xattn_wq", "L3_xattn_Wq"]
WO = ["L0_xattn_Wo", "L1_xattn_out_w", "L2_xattn_wo", "L3_xattn_Wo"]
WK = ["L0_xattn_Wk", "L1_xattn_k_w", "L1_xattn_kg_w", "L2_xattn_wk", "L3_xattn_Wk"]
WV = ["L0_xattn_Wv", "L1_xattn_v_w", "L1_xattn_vg_w", "L2_xattn_wv", "L3_xattn_Wv"]
BQ = ["L0_xattn_bq", "L1_xattn_q_b", None, None]
BK = ["L0_xattn_bk", "L1_xattn_k_b", "L1_xattn_kg_b", None, None]
BV = ["L0_xattn_bv", "L1_xattn_v_b", "L1_xattn_vg_b", None, None]
BO = ["L0_xattn_bo", "L1_xattn_out_b", None, None]


def flamingo(nc, a, out):
    ctx = ExitStack()
    with ctx:
        def sb(name, shape, dt=F32):
            return ctx.enter_context(nc.sbuf_tensor(name, shape, dt))

        def sem(name):
            return ctx.enter_context(nc.semaphore(name))

        def dram(name, shape, dt):
            return nc.dram_tensor(name, shape, dt, kind="Internal").ap()

        x = sb("x", [P, NT, D])
        xn = sb("xn", [P, NT, D])
        xnT = sb("xnT", [P, TOK])
        wsq = sb("wsq", [P, len(SQUARE), D])
        ident = sb("ident", [P, P])
        ident16 = sb("ident16", [P, P], F16)
        mask_eye = sb("mask_eye", [P, P], F16)
        ones = sb("ones", [P, P])
        rows = sb("rows", [1, NROW])
        spread = sb("spread", [P, NROW])
        cols_raw = sb("cols_raw", [NCOL, P])
        cols = sb("cols", [P, NCOL])
        ctxT = sb("ctxT", [P, 2, S2])
        k1c = sb("k1c", [P, 2, S2 + 1], F16)
        k2c = sb("k2c", [P, 2, S2 + 1], F16)
        v_all = sb("v_all", [P, B, KT, VW])
        v_loc = sb("v_loc", [P, B, LKT, VW])
        gate = sb("gate", [P, B, KT])
        gate_e = sb("gate_e", [P, B, KT])
        qf = sb("qf", [P, TOK])
        q1c = sb("q1c", [P, TOK], F16)
        q2c = sb("q2c", [P, TOK], F16)
        kp1 = [sb(f"kp1_{i}", [P, S2 + 1], F16) for i in range(2)]
        kp2 = [sb(f"kp2_{i}", [P, S2 + 1], F16) for i in range(2)]
        qp1 = [sb(f"qp1_{i}", [P, HG, S], F16) for i in range(2)]
        qp2 = [sb(f"qp2_{i}", [P, HG, S], F16) for i in range(2)]
        vg = [sb(f"vg_{i}", [P, KT, HG, R]) for i in range(2)]
        early_mem = [sb(f"early_{i}", [P, 2, HG, S]) for i in range(2)]
        pt = [m[:, 0, :, :] for m in early_mem]
        mx = [sb(f"mx_{i}", [P, QT * HG, 2]) for i in range(2)]
        nm = [sb(f"nm_{i}", [P, QT, HG]) for i in range(2)]
        nmc = [sb(f"nmc_{i}", [P, QT, HG]) for i in range(2)]
        m16 = [sb(f"m16_{i}", [P, QT, 2, HG], F16) for i in range(2)]
        ms = [sb(f"ms_{i}", [2 * HG, S], F16) for i in range(2)]
        mask01 = sb("mask01", [P, QT, S2], F16)
        mask_add = sb("mask_add", [P, QT, 4, S2 // 4 + 1], F16)
        o_all = sb("o_all", [P, UNITS, S])
        on = sb("on", [P, NT, D])
        on_loc = sb("on_loc", [P, NT, D])
        rec = sb("rec", [P, NT, H])
        rec0 = sb("rec0", [P, NT, H])
        stats = sb("stats", [P, NT, 6])
        mv = sb("mv", [P, NT, 2])
        rstd = sb("rstd", [P, NT])
        var_eps = sb("var_eps", [P, NT])
        minus_half = sb("minus_half", [P, NT])
        tg = sb("tg", [P, 8])
        lgate = sb("lgate", [P, 3])
        wabs = sb("wabs", [P, 2])
        whalf = sb("whalf", [P, 2, 2])
        wfcT = sb("wfcT", [P, HID0])
        wprT = sb("wprT", [P, 4, D])
        dft = sb("dft", [P, 3, P])
        wfreq = sb("wfreq", [P, 2, D])
        a12 = sb("a12", [P, 2, D])
        mfreq = sb("mfreq", [P, D])
        w_up = [sb(f"w_up_{i}", [P, HID1]) for i in range(2)]
        w_dn = [sb(f"w_dn_{i}", [P, 4, D]) for i in range(2)]
        b1_now = [sb(f"b1_now_{i}", [P, 4]) for i in range(2)]
        wr = sb("wr", [P, 2, E1])
        b2 = sb("b2", [E1, 2, D])
        lg = sb("lg", [P, NT, E1])
        lmax = sb("lmax", [P, NT])
        lex = sb("lex", [P, NT, E1])
        lsh = sb("lsh", [P, NT, E1])
        lsum = sb("lsum", [P, NT])
        lrec = sb("lrec", [P, NT])
        prob = sb("prob", [P, NT, E1])
        earlier = sb("earlier", [P, E1, E1])
        rank = sb("rank", [P, NT, E1])
        chosen = sb("chosen", [P, NT, E1])
        comb = sb("comb", [P, NT, E1])
        comb_s = sb("comb_s", [P, NT, E1])
        combT = sb("combT", [E1, TOK])

        early = early_mem[0][:, :, :, :].rearrange("p a b q -> p (a b q)")
        wraw = early[:, 0:len(TURNED) * D].rearrange("p (k d) -> p k d", d=D)
        early = early_mem[1][:, :, :, :].rearrange("p a b q -> p (a b q)")
        tern = early[:, 0:2 * HID0].rearrange("p (k d) -> p k d", k=2)
        tern_neg = early[:, 2 * HID0:4 * HID0].rearrange("p (k d) -> p k d", k=2)
        h0 = o_all[:, :, :].rearrange("p u q -> p (u q)").rearrange("p (t n) -> p t n", n=HID0)
        hT = [m[:, :, :, :].rearrange("p a b q -> p (a b q)").rearrange("p (c n) -> p c n", c=4) for m in early_mem]
        one16 = v_loc[:, :, :, :].rearrange("p b k d -> p (b k d)").bitcast(F16)[:, 0:S2]
        masked = [m.bitcast(F16)[:, 0:2 * (S2 // 4 + 1)].rearrange("p (z n) -> p z n", z=2)
                  for m in (wfcT[:, :], wprT[:, :, :].rearrange("p c d -> p (c d)"))]
        ctx_raw = o_all[:, :, :].rearrange("p u q -> p (u q)")[:, 0:2 * KT * D].rearrange(
            "p (b k d) -> p b k d", b=2, d=D)
        mask8 = kp1[1][:, 0:S2].bitcast(U8).rearrange("p (t n) -> p t n", t=QT)
        wfc_raw = kp1[0][:, 0:2 * HID0].bitcast(F32).rearrange("p (c d) -> p c d", d=D)
        wpr_raw = kp2[0][:, 0:2 * HID0].bitcast(F32)
        gate_in = kp2[1][:, 0:2 * B * KT * 8].bitcast(F32).rearrange("p (b k c) -> p b k c", b=B, k=KT)
        above, tied = [k2c[:, i, 0:2 * NT * E1 * E1].bitcast(F32).rearrange("p (t e j) -> p t e j", t=NT, e=E1)
                       for i in range(2)]
        lk1, lk2 = [xn[:, 4 * i:4 * i + 4, :].rearrange("p t d -> p (t d)").bitcast(F16) for i in range(2)]
        free16 = v_all[:, :, :, :].rearrange("p b k d -> p (b k d)").bitcast(F16)
        hs = [[free16[:, (2 * i + part) * 4 * 512:(2 * i + part + 1) * 4 * 512].rearrange("p (c n) -> p c n", c=4)
               for part in range(2)] for i in range(2)]
        ws = [[[free16[:, (16 + 4 * i + 2 * k + part) * 512:(17 + 4 * i + 2 * k + part) * 512] for part in range(2)]
               for k in range(2)] for i in range(2)]
        wus, wds = ws
        xs = [q1c, q2c]
        onT = qf
        acc = on
        ytmp = on_loc

        pa = [ctx.enter_context(nc.psum_tensor(f"score_ring_{i}", [P, 2, 512], F32)) for i in range(2)]
        pe_ = [ctx.enter_context(nc.psum_tensor(f"exp_ring_{i}", [P, 512], F32)) for i in range(3)]
        po = ctx.enter_context(nc.psum_tensor("pv_bank", [P, 512], F32))
        PB = [pa[0][:, 0, :], pa[0][:, 1, :], pa[1][:, 0, :], pa[1][:, 1, :],
              pe_[0][:, :], pe_[1][:, :], pe_[2][:, :], po[:, :]]

        ctxT_d = dram("ctxT_d", [B, P, S2], F32)
        k_d = [dram(f"k_d{r.index}", [UNITS, P, r.nk], F16) for r in RUNS]
        q_d = [dram(f"q_d{l}", [UNITS, P, S], F16) for l in range(4)]

        ld_x, ld_w, ld_wt, ld_cols, ld_rows, ld_mask, ld_gate, ld_misc, ld_fc = [
            sem(n) for n in ("ld_x", "ld_w", "ld_wt", "ld_cols", "ld_rows", "ld_mask", "ld_gate", "ld_misc", "ld_fc")]
        consts = sem("consts")
        dconst = sem("dconst")
        padded0, padded = sem("padded0"), sem("padded")
        w_turned, w_kept = sem("w_turned"), sem("w_kept")
        prep_v = sem("prep_v")
        prep_a = sem("prep_a")
        prep_p = sem("prep_p")
        ctx_t, ctx_e = sem("ctx_t"), sem("ctx_e")
        prep_w, prep_p0, f_ve, f_rs, r_acc = [sem(n) for n in ("prep_w", "prep_p0", "f_ve", "f_rs", "r_acc")]
        ctx_in, ctx_out, c_ld, k_out, in1, in2, m_in, e_w = [
            [sem(f"{n}_{i}") for i in range(2)] for n in ("ctx_in", "ctx_out", "c_ld", "k_out", "in1", "in2", "m_in", "e_w")]
        ln_st, ln_mv, ln_ve, ln_rs, ln_xn, ln_t, ln_xt = [
            sem(n) for n in ("ln_st", "ln_mv", "ln_ve", "ln_rs", "ln_xn", "ln_t", "ln_xt")]
        q_ps, q_f, q_1, q_2, q_out, q_out2 = [sem(n) for n in ("q_ps", "q_f", "q_1", "q_2", "q_out", "q_out2")]
        k_ps, v_ps, k_1, k_2, v_ok = [sem(n) for n in ("k_ps", "v_ps", "k_1", "k_2", "v_ok")]
        lk_ps, lk_1, lk_2, lk_out, lv_ok = [sem(n) for n in ("lk_ps", "lk_1", "lk_2", "lk_out", "lv_ok")]
        score, score_free = sem("score"), sem("score_free")
        q_kept = sem("q_kept")
        mx_done, m_ok = sem("mx_done"), sem("m_ok")
        fill, exped = sem("fill"), sem("exped")
        pv, o_ok, vg_ok = sem("pv"), sem("o_ok"), sem("vg_ok")
        o_t, o_rec, o_inv, o_n, o_add, on_t, on_e, y_ps, y_t, x_ok = [
            sem(n) for n in ("o_t", "o_rec", "o_inv", "o_n", "o_add", "on_t", "on_e", "y_ps", "y_t", "x_ok")]
        f_up, f_act, f_st0, f_st, f_n, f_t, f_ht, f_dn, f_x = [
            sem(n) for n in ("f_up", "f_act", "f_st0", "f_st", "f_n", "f_t", "f_ht", "f_dn", "f_x")]
        r_ps, r_v, r_a, r_ct, r_cc, r_b = [sem(n) for n in ("r_ps", "r_v", "r_a", "r_ct", "r_cc", "r_b")]
        e_up, e_act, e_dn, e_acc, e_b = [sem(n) for n in ("e_up", "e_act", "e_dn", "e_acc", "e_b")]
        x_1, x_2, e_w1, e_w2, e_h2 = [sem(n) for n in ("x_1", "x_2", "e_w1", "e_w2", "e_h2")]
        stored, passed, passed_sp, passed_p = [sem(n) for n in ("stored", "passed", "passed_sp", "passed_p")]

        block = ctx.enter_context(nc.Block())
        sq = lambda name: wsq[:, SQ[name], :]
        col = lambda name, k=0: cols[:, (COL[name] if name else ZCOL) + k:(COL[name] if name else ZCOL) + k + 1]
        row = lambda name, n: spread[:, ROW[name or "zero"]:ROW[name or "zero"] + n]


        def ln_at(layer, ffn):
            return 2 * layer + ffn


        @block.sync
        def _(sp):
            sp.dma_start(x[:, :, :], a["x"].rearrange("b (t p) d -> p (b t) d", p=P)).then_inc(ld_x, 16)
            def ctx_load(b):
                if b >= 2:
                    sp.wait_ge(ctx_t, 4 * (b - 1))
                sp.dma_start(ctx_raw[:, b % 2, 0:FULL, :],
                             a["ctx_1024"][b, 0:FULL * P, :].rearrange("(t p) d -> p t d", p=P)
                             ).then_inc(ctx_in[b % 2], 16)
                sp.dma_start(ctx_raw[0:TAIL, b % 2, FULL, :], a["ctx_1024"][b, FULL * P:S2, :]
                             ).then_inc(ctx_in[b % 2], 16)

            ctx_load(0)
            sp.wait_ge(dconst, 3)
            for name, k in COLS:
                src = a[name]
                if len(src.shape) == 2:
                    src = src.rearrange("e (c p) -> (e c) p", p=P)
                else:
                    src = src.rearrange("(c p) -> c p", p=P)
                sp.dma_start(cols_raw[COL[name]:COL[name] + k, :], src).then_inc(ld_cols, 16)
            for name, k in ROWS:
                if name != "zero":
                    src = a[name]
                    src = src.rearrange("(a n) -> a n", a=1) if len(src.shape) == 1 else src
                    sp.dma_start(rows[0:1, ROW[name]:ROW[name] + k], src).then_inc(ld_rows, 16)
            ctx_load(1)
            for b in range(B):
                sp.dma_start(gate_in[:, b, 0:FULL, :],
                             a["ctxb_2048x8"][b, 0:FULL * P, :].rearrange("(t p) c -> p t c", p=P)
                             ).then_inc(ld_gate, 16)
                sp.dma_start(gate_in[0:TAIL, b, FULL, :], a["ctxb_2048x8"][b, FULL * P:S2, :]).then_inc(ld_gate, 16)
            for k, name in enumerate(("dft_cos", "dft_sin", "dft_nsin")):
                sp.dma_start(dft[:, k, :], a[name]).then_inc(ld_misc, 16)
            sp.dma_start(wfreq[:, 0, :], a["L2_ffn_w_freq_real"]).then_inc(ld_misc, 16)
            sp.dma_start(wfreq[:, 1, :], a["L2_ffn_w_freq_imag"]).then_inc(ld_misc, 16)
            sp.dma_start(wr[:, 0, :], a["L1_ffn_Wr"]).then_inc(ld_misc, 16)
            sp.dma_start(wr[:, 1, :], a["L3_ffn_gate_w"]).then_inc(ld_misc, 16)
            sp.dma_start(b2[:, 0, :], a["L1_ffn_b2"]).then_inc(ld_misc, 16)
            sp.dma_start(b2[:, 1, :], a["L3_ffn_b2"]).then_inc(ld_misc, 16)

            def split_rows(dst, b, part):
                v = dst[4 * b:4 * b + 4].rearrange("g (i r) n -> (g i) r n", r=R)
                return v[:, DH * part:DH * part + DH, :]

            def constant_rows(r):
                for b in range(B):
                    sp.dma_start(k_d[r.index][4 * b:4 * b + 4].rearrange("g (i r) n -> (g i) r n", r=R)[:, KQ:R, :],
                                 one16[:, 0:r.nk]).then_inc(padded0, 16)

            def k_prep(r):
                g = r.ctx
                if r.layer == 0:
                    sp.wait_ge(dconst, 4)
                    constant_rows(r)
                    ctx_load(2)
                else:
                    for i in range(2):
                        sp.wait_ge(ctx_out[i], 16 * B // 2)
                    c_load(r, g, 0)
                    c_load(r, g, 1)
                q_store(r.layer)
                for b in range(B):
                    if r.layer == 0:
                        sp.wait_ge(ctx_e, 4 * b + 4)
                        sp.dma_start(ctxT_d[b], ctxT[:, b % 2, :]).then_inc(ctx_out[b % 2], 16)
                        if b == 0:
                            ctx_load(3)
                    elif b + 2 < B:
                        c_load(r, g, b + 2)
                    k_store(r, g, b)
                    if b == 1:
                        sp.wait_ge(q_out, 16 * (12 + 8 * r.layer))
                        if r.layer:
                            sp.wait_ge(q_out2, 16 * 4 * r.layer)
                        if r.layer == 0:
                            sp.wait_ge(padded0, 16 * B)
                            sp.wait_ge(dconst, 7)
                            sp.wait_ge(prep_w, 10)
                            sp.wait_ge(prep_v, 11)
                        if r.layer == 1:
                            sp.wait_ge(padded, 16 * B * (len(RUNS) - 1))
                            sp.wait_ge(lk_out, 16 * 12)
                        else:
                            sp.wait_ge(k_out[0], 48 * (B // 2 * g + 1))
                        loads_start(RUNS[LOCAL] if r.layer == 1 else r)

            def c_load(r, g, b):
                n = B * g + b
                sp.wait_ge(k_ps, 4 * (n - 1))
                sp.wait_ge(v_ps, 4 * (n - 1))
                sp.dma_start(ctxT[:, b % 2, :], ctxT_d[b]).then_inc(c_ld[b % 2], 16)

            def k_store(r, g, b):
                n = B * g + b
                sp.wait_ge(k_1, 4 * (n + 1))
                for part in (0, 2):
                    sp.dma_start(split_rows(k_d[r.index], b, part), k1c[:, b % 2, 0:S2]).then_inc(k_out[b % 2], 16)
                sp.wait_ge(k_2, 4 * (n + 1))
                sp.dma_start(split_rows(k_d[r.index], b, 1), k2c[:, b % 2, 0:S2]).then_inc(k_out[b % 2], 16)

            def q_store(l):
                sp.wait_ge(q_2, 2 * (l + 1))
                for b in range(B):
                    for part, src in ((0, q1c), (1, q1c), (2, q2c))[:2 if l else 3]:
                        sp.dma_start(split_rows(q_d[l], b, part), src[:, b * S:b * S + S]).then_inc(q_out, 16)

            def pass1(r, n, par):
                sp.dma_start(kp1[par][:, 0:r.nk], k_d[r.index][n]).then_inc(in1[par], 16)
                for i in range(HG):
                    sp.dma_start(qp1[par][R * i:R * i + KQ, i, :], q_d[r.layer][n, R * i:R * i + KQ, :]
                                 ).then_inc(in1[par], 16)

            def pass2(r, n, par):
                sp.dma_start(kp2[par][:, 0:r.nk], k_d[r.index][n]).then_inc(in2[par], 16)

            def loads_start(r):
                pass1(r, 0, 0)
                pass1(r, 1, 1)
                if r.u0:
                    sp.wait_ge(fill, r.fill0)
                pass2(r, 0, 0)

            def loads(r):
                def maxima(n, par):
                    sp.dma_start(qp2[par][KQ:KQ + 2, :, :], ms[par][:, :]).then_inc(m_in[par], 16)

                def unit(n, par, p1=True, p2=True, first=False):
                    sp.wait_ge(q_kept, r.u0 + n + 1)
                    sp.sem_inc(passed_sp, 1)
                    if p1:
                        pass1(r, n + 2, par)
                    sp.wait_ge(score_free, FREE_SCORE + (r.use(n + 1, r.turn) if p2 else
                                                         r.use0 + UNITS * r.uses - 1) + 1)
                    maxima(n, par)
                    if p2:
                        if not first:
                            sp.wait_ge(fill, r.fill0 + n * r.fills)
                        pass2(r, n + 1, 1 - par)

                unit(0, 0, first=True)
                with sp.Fori(0, (UNITS - 4) // 2) as t:
                    unit(2 * t + 1, 1)
                    unit(2 * t + 2, 0)
                unit(UNITS - 3, 1)
                unit(UNITS - 2, 0, p1=False)
                unit(UNITS - 1, 1, p1=False, p2=False)

            def experts(l, which, w_up_d, w_dn_d, hid):
                cc = hid // P
                with sp.Fori(0, E1 // 2) as t:
                    for k in range(2):
                        sp.wait_ge(e_w2, FREE_W - 2 + 2 * (E1 * which + 2 * t + k))
                        sp.dma_start(w_up[k][:, 0:hid], w_up_d[2 * t + k]).then_inc(e_w[k], 16)
                        sp.dma_start(w_dn[k][:, 0:cc, :],
                                     w_dn_d[2 * t + k].rearrange("(c p) d -> p c d", p=P)).then_inc(e_w[k], 16)

            for l in range(LAYERS):
                for r in RUNS:
                    if r.layer == l and not r.local:
                        k_prep(r)
                for r in RUNS:
                    if r.layer == l:
                        if not r.local:
                            for i in range(2):
                                sp.wait_ge(k_out[i], 48 * (B // 2) * (r.ctx + 1))
                            if r.layer == 1:
                                loads_start(r)
                        loads(r)
                if l == 1:
                    experts(l, 0, a["L1_ffn_W1"], a["L1_ffn_W2"], HID1)
                if l == 3:
                    experts(l, 1, a["L3_ffn_w1"], a["L3_ffn_w2"], HID3)
            sp.wait_ge(x_ok, 2 * NT * LAYERS)
            sp.dma_start(out.rearrange("b (t p) d -> p (b t) d", p=P), x[:, :, :]).then_inc(stored, 16)
            sp.wait_ge(stored, 16)

        @block.gpsimd
        def _(pool):
            pool.memset(ident[:, :], 0.0).then_inc(consts, 1)
            pool.memset(ident16[:, :], 0.0).then_inc(consts, 1)
            pool.memset(mask_eye[:, :], 0.0).then_inc(consts, 1)
            pool.memset(earlier[:, :, :], 1.0).then_inc(consts, 1)
            pool.wait_ge(consts, 4)
            for m, v in ((ident, 1.0), (ident16, 1.0), (mask_eye, -BIG)):
                pool.affine_select(out=m[:, :], in_=m[:, :], compare_op=ALU.not_equal, fill=v, base=0,
                                   pattern=[[-1, P]], channel_multiplier=1).then_inc(consts, 1)
            pool.affine_select(out=earlier[:, :, :], in_=earlier[:, :, :], compare_op=ALU.is_gt, fill=0.0, base=0,
                               pattern=[[1, E1], [-1, E1]], channel_multiplier=0).then_inc(consts, 1)
            pool.memset(ones[:, :], 1.0).then_inc(consts, 1)
            pool.memset(minus_half[:, :], -0.5).then_inc(consts, 1)
            for i in range(2):
                pool.memset(vg[i][:, :, :, :], 1.0).then_inc(consts, 1)
            def weights(which):
                for i, (name, turned) in which:
                    dst = wraw[:, TURNED.index(i), :] if turned else wsq[:, i, :]
                    pool.dma_start(dst, a[name]).then_inc(ld_wt if turned else ld_w, 16)

            weights([w for w in enumerate(SQUARE) if not w[1][1]])

            def norm(s):
                for m in range(2):
                    half = slice(4 * m, 4 * m + 4)
                    pool.wait_ge(ln_mv, NT * s + 4 * m + 4)
                    pool.tensor_scalar(var_eps[:, half], mv[:, half, 1], LN_EPS, None, ALU.add).then_inc(ln_ve, 1)
                    pool.wait_ge(ln_ve, 2 * s + m + 1)
                    pool.tensor_tensor(rstd[:, half], var_eps[:, half], minus_half[:, half], ALU.pow).then_inc(ln_rs, 1)

            def local_store():
                pool.wait_ge(lk_2, 2)
                for b in range(B):
                    rows_ = k_d[LOCAL][4 * b:4 * b + 4].rearrange("g (i r) n -> (g i) r n", r=R)
                    for part, src in ((0, lk1), (2, lk1), (1, lk2)):
                        pool.dma_start(rows_[:, DH * part:DH * part + DH, :], src[:, b * S:b * S + S]
                                       ).then_inc(lk_out, 16)

            def expert_bias(which, hid, bcol):
                cc = hid // P
                biases = cols[:, COL[bcol]:COL[bcol] + E1 * cc].rearrange("p (e c) -> p e c", c=cc)
                with pool.Fori(0, E1 // 2) as t:
                    for k in range(2):
                        pool.wait_ge(e_dn, FREE_HID + 2 * E1 * which + 2 * (2 * t + k) - 2)
                        pool.tensor_copy(b1_now[k][:, 0:cc], biases[:, 2 * t + k, :]).then_inc(e_b, 1)
                        pool.wait_ge(e_w[k], 16 * (E1 * which + 2 * t + 2))
                        pool.sem_inc(passed_p, 1)
                        pool.tensor_scalar(wus[k][0][:, 0:hid], w_up[k][:, 0:hid], WSCALE, None, ALU.mult
                                           ).then_inc(e_w1, 1)
                        pool.tensor_scalar(wds[k][0][:, 0:hid], w_dn[k][:, 0:cc, :].rearrange("p c d -> p (c d)"),
                                           WSCALE, None, ALU.mult).then_inc(e_w1, 1)

            def unit_v(r):
                v = v_loc if r.local else v_all
                if r.local:
                    pool.wait_ge(lv_ok, NT)
                else:
                    pool.wait_ge(v_ok, 4 * B * (r.ctx + 1))

                def copy(b, g, par):
                    src = v[:, b, :, R * g:R * g + R].rearrange("p k (j d) -> p k j d", d=DH)
                    if r.layer == 0:
                        pool.tensor_tensor(vg[par][:, :, :, 0:DH], src,
                                           gate[:, b, :].unsqueeze(2).unsqueeze(3).broadcast_to([P, KT, HG, DH]),
                                           ALU.mult).then_inc(vg_ok, 1)
                    else:
                        pool.tensor_copy(vg[par][:, 0:r.kt, :, 0:DH], src).then_inc(vg_ok, 1)

                for g in range(2):
                    if r.u0:
                        pool.wait_ge(pv, FREE_PT + r.step0)
                    copy(0, g, g)
                for g in range(2, 4):
                    pool.wait_ge(pv, FREE_PT + r.step0 + (g - 1) * r.kt)
                    copy(0, g, g % 2)
                with pool.Fori(1, B) as b:
                    for g in range(4):
                        pool.wait_ge(pv, FREE_PT + r.step0 + (4 * b + g - 1) * r.kt)
                        copy(b, g, g % 2)

            for l in range(LAYERS):
                norm(ln_at(l, 0))
                if l:
                    pool.wait_ge(q_2, 2 * (l + 1))
                    for b in range(B):
                        pool.dma_start(
                            q_d[l][4 * b:4 * b + 4].rearrange("g (i r) n -> (g i) r n", r=R)[:, 2 * DH:3 * DH, :],
                            q2c[:, b * S:b * S + S]).then_inc(q_out2, 16)
                if l == 1:
                    local_store()
                if l == 0:
                    weights([w for w in enumerate(SQUARE) if w[1][1]])
                    pool.wait_ge(dconst, 4)
                    for r in RUNS[1:]:
                        for b in range(B):
                            pool.dma_start(
                                k_d[r.index][4 * b:4 * b + 4].rearrange("g (i r) n -> (g i) r n", r=R)[:, KQ:R, :],
                                one16[:, 0:r.nk]).then_inc(padded, 16)
                    pool.wait_ge(prep_v, 3)
                for r in RUNS:
                    if r.layer == l:
                        unit_v(r)
                if l == 1:
                    pool.wait_ge(o_n, NT * 3)
                    pool.tensor_tensor(on[:, :, :], on[:, :, :], on_loc[:, :, :], ALU.add).then_inc(o_add, 1)
                norm(ln_at(l, 1))
                if l in (1, 3):
                    expert_bias(l // 2, HID1 if l == 1 else HID3, "L1_ffn_b1" if l == 1 else "L3_ffn_b1")
                if l == 0:
                    for m in range(2):
                        half = slice(4 * m, 4 * m + 4)
                        pool.wait_ge(f_st, 4 * (m + 1))
                        pool.tensor_scalar(var_eps[:, half], mv[:, half, 1], LN_EPS, None, ALU.add
                                           ).then_inc(f_ve, 1)
                        pool.wait_ge(f_ve, m + 1)
                        pool.tensor_tensor(rstd[:, half], var_eps[:, half], minus_half[:, half], ALU.pow
                                           ).then_inc(f_rs, 1)

        @block.scalar
        def _(act):
            act.sem_inc(exped, FREE_EXP)
            act.sem_inc(o_ok, FREE_PV)
            act.sem_inc(e_act, FREE_UP)
            act.dma_start(mask8[:, :, :], a["mask_1x1xSxS2_bk1"].rearrange("a b (t p) n -> p (a b t) n", p=P)
                          ).then_inc(ld_mask, 16)
            act.dma_start(wfc_raw[:, :, :], a["L0_ffn_W_fc"].rearrange("(c p) d -> p c d", p=P)).then_inc(ld_fc, 16)
            act.dma_start(wpr_raw[:, :], a["L0_ffn_W_proj"]).then_inc(ld_fc, 16)
            def spread_vectors():
                act.wait_ge(prep_p, 1)
                act.activation(cols[:, :], PB[0][:, 0:NCOL], ACT.Copy).then_inc(prep_a, 1)
                act.wait_ge(prep_p, 2)
                act.activation(spread[:, 0:512], PB[1], ACT.Copy).then_inc(prep_a, 1)
                act.wait_ge(prep_p, 3)
                act.activation(spread[:, 512:NROW], PB[2][:, 0:NROW - 512], ACT.Copy).then_inc(prep_a, 1)
                act.wait_ge(prep_a, 3)
                act.activation(tg[:, :], spread[:, ROW["g_xattn"]:ROW["g_xattn"] + 8], ACT.Tanh).then_inc(prep_a, 1)
                act.activation(lgate[:, 0:1], row("L1_xattn_gate", 1), ACT.Exp, scale=-1.0).then_inc(prep_a, 1)

            def weights():
                for m in range(0, len(TURNED), 4):
                    k = min(4, len(TURNED) - m)
                    act.wait_ge(w_turned, m // 4 + 1)
                    act.activation(wsq[:, TURNED[m]:TURNED[m] + k, :], PB[m // 4][:, 0:k * D].rearrange(
                        "p (k d) -> p k d", k=k), ACT.Copy).then_inc(w_kept, 1)
                act.wait_ge(prep_v, 1)
                act.activation(gate_e[:, :, :], gate[:, :, :], ACT.Exp, scale=-10.0 / 8, bias=1.0).then_inc(prep_a, 1)
                act.wait_ge(prep_p, 4)
                act.activation(wfcT[:, :], PB[7], ACT.Copy).then_inc(prep_a, 1)
                act.wait_ge(prep_p, 5)
                act.activation(wprT[:, :, :], PB[4].rearrange("p (c d) -> p c d", c=4), ACT.Copy).then_inc(prep_a, 1)
                act.wait_ge(prep_p, 6)
                act.activation(a12[:, :, :], PB[5][:, 0:2 * D].rearrange("p (k d) -> p k d", k=2), ACT.Copy
                               ).then_inc(prep_a, 1)
                act.wait_ge(prep_p, 7)
                act.activation(mfreq[:, :], PB[6][:, 0:D], ACT.Copy, scale=1.0 / D).then_inc(prep_a, 1)

            def ctx_turned(b):
                if b >= 2:
                    act.wait_ge(ctx_out[b % 2], 16 * (b // 2))
                for m in range(4):
                    k = min(4 * P, S2 - m * 4 * P)
                    act.wait_ge(ctx_t, 4 * b + m + 1)
                    act.activation(ctxT[:, b % 2, m * 4 * P:m * 4 * P + k], PB[4 + m][:, 0:k], ACT.Copy
                                   ).then_inc(ctx_e, 1)

            def normT(s):
                for m in range(2):
                    act.wait_ge(ln_t, 2 * s + m + 1)
                    act.activation(xnT[:, m * 512:m * 512 + 512], PB[m], ACT.Copy).then_inc(ln_xt, 1)

            def k_split(r):
                g = r.ctx
                w = S2 // 4
                for b in range(B):
                    n = B * g + b
                    if r.layer == 0:
                        if b == 2:
                            weights()
                        if b:
                            ctx_turned(b)
                    if n >= 2:
                        act.wait_ge(k_out[b % 2], 48 * (n // 2))
                    for c in range(4):
                        lo = c * w + min(c, 1)
                        act.wait_ge(k_ps, 4 * n + c + 1)
                        act.activation(k1c[:, b % 2, lo:lo + w + (c == 0)], PB[c][:, 0:w + (c == 0)], ACT.Identity,
                                       bias=col(BK[r.index])).then_inc(k_1, 1)
                    for c in range(0 if BV[r.index] else 4):
                        k = 4 if c < 3 else 1
                        pr = P if c < 3 else TAIL
                        act.wait_ge(v_ps, 4 * n + c + 1)
                        act.activation(v_all[0:pr, b, 4 * c:4 * c + k, :],
                                       PB[4 + c][0:pr, 0:k * VW].rearrange("p (k d) -> p k d", k=k), ACT.Copy
                                       ).then_inc(v_ok, 1)

            def q_split(l):
                for m in range(2):
                    act.wait_ge(q_f, 2 * l + m + 1)
                    if l:
                        act.wait_ge(q_out, 16 * (12 + 8 * (l - 1)))
                    act.activation(q1c[:, m * 512:m * 512 + 512], qf[:, m * 512:m * 512 + 512], ACT.Copy
                                   ).then_inc(q_1, 1)

            def local_split():
                for m in range(2):
                    act.wait_ge(lk_ps, m + 1)
                    act.activation(lk1[:, m * 512:m * 512 + 512], PB[2 + m], ACT.Identity,
                                   bias=col(BK[LOCAL])).then_inc(lk_1, 1)

            def attention(r):
                def evac(n):
                    act.wait_ge(pv, FREE_PT + r.step0 + (n + 1) * r.kt)
                    act.activation(o_all[:, n, :], po[:, 0:S], ACT.Copy).then_inc(o_ok, 1)

                def unit(n, par, prev=True):
                    for s in range(r.kt):
                        g = (par * r.kt + s) % 2
                        rows_ = r.keys(s)
                        act.wait_ge(pv, FREE_PT - 1 + r.step0 + n * r.kt + s)
                        for h in range(PAIRS):
                            act.wait_ge(fill, r.fill0 + n * r.fills + PAIRS * s + h + 1)
                            bank = pe_[r.banks[par * r.fills + PAIRS * s + h]]
                            act.activation(pt[g][0:rows_, 2 * h:2 * h + 2, :],
                                           bank[0:rows_, :].rearrange("p (i q) -> p i q", q=S),
                                           ACT.Exp).then_inc(exped, 1)
                        if s == 0 and prev:
                            evac(n - 1)

                unit(0, 0, prev=False)
                with act.Fori(0, UNITS // 2 - 1) as t:
                    unit(2 * t + 1, 1)
                    unit(2 * t + 2, 0)
                unit(UNITS - 1, 1)
                evac(UNITS - 1)

            def post(l):
                for m in range(2):
                    act.wait_ge(on_t, 2 * l + m + 1)
                    act.activation(onT[:, m * 512:m * 512 + 512], PB[4 + m], ACT.Copy).then_inc(on_e, 1)

            def ffn0():
                for T in range(NT):
                    act.wait_ge(f_up, T + 1)
                    act.activation(h0[:, T, :], PB[2 + T % 4], ACT.Gelu).then_inc(f_act, 1)
                for m in range(2):
                    for c in range(4):
                        act.wait_ge(f_t, 4 * m + c + 1)
                        act.activation(hT[m][:, c, :], PB[c], ACT.Identity, scale=col("L0_ffn_ln_w", c),
                                       bias=col("L0_ffn_ln_b", c)).then_inc(f_ht, 1)

            def route(which):
                for m in range(2):
                    sl = slice(m * 512, m * 512 + 512)
                    act.wait_ge(ln_xt, 2 * ln_at(2 * which + 1, 1) + m + 1)
                    act.activation(xs[0][:, sl], xnT[:, sl], ACT.Copy).then_inc(x_1, 1)
                act.wait_ge(r_v, ROUTE_V[which][0])
                act.activation(lex[:, :, :], lsh[:, :, :], ACT.Exp).then_inc(r_a, 1)
                for m in range(2):
                    act.wait_ge(r_ct, 2 * which + m + 1)
                    act.activation(combT[:, m * 512:m * 512 + 512], PB[2 + m][0:E1, :], ACT.Copy).then_inc(r_cc, 1)

            def experts(which, hid, func):
                cc = hid // P
                up0 = which and 2 * E1 * (HID1 // P)
                with act.Fori(0, E1 // 2) as t:
                    for k in range(2):
                        act.wait_ge(e_b, E1 * which + 2 * t + k + 1)
                        for hf in range(2):
                            act.wait_ge(e_dn, FREE_HID + 2 * E1 * which + 2 * (2 * t + k) + hf - 1)
                            for c in range(cc):
                                act.wait_ge(e_up, up0 + (2 * t + k) * 2 * cc + hf * cc + c + 1)
                                act.activation(hT[hf][:, c, :], PB[(hf * cc + c) % 4], func,
                                               bias=b1_now[k][:, c:c + 1], scale=1.0 / WSCALE)
                                act.activation(hs[hf][0][:, c, :], PB[(hf * cc + c) % 4], func,
                                               bias=b1_now[k][:, c:c + 1], scale=1.0 / WSCALE).then_inc(e_act, 1)

            ctx_turned(0)
            spread_vectors()
            for l in range(LAYERS):
                normT(ln_at(l, 0))
                q_split(l)
                if l == 1:
                    local_split()
                for r in RUNS:
                    if r.layer == l and not r.local:
                        k_split(r)
                for r in RUNS:
                    if r.layer == l:
                        attention(r)
                post(l)
                normT(ln_at(l, 1))
                if l == 0:
                    ffn0()
                if l == 1:
                    route(0)
                    experts(0, HID1, ACT.Gelu)
                if l == 3:
                    route(1)
                    experts(1, HID3, ACT.Relu)

        @block.vector
        def _(dve):
            dve.memset(cols_raw[:, :], 0.0).then_inc(dconst, 1)
            dve.memset(rows[0:1, :], 0.0).then_inc(dconst, 1)
            dve.memset(gate_in[:, :, :, :], 0.0).then_inc(dconst, 1)
            dve.memset(one16[:, :], 1.0).then_inc(dconst, 1)
            dve.memset(v_all[:, :, FULL, :], 0.0).then_inc(dconst, 1)
            for m in qp1:
                dve.memset(m[:, :, :], 0.0).then_inc(dconst, 1)
            def weights():
                dve.wait_ge(dconst, 5)
                dve.wait_ge(ld_fc, 32)
                dve.tensor_reduce(wabs[:, 0:1], wfc_raw[:, :, :].rearrange("p c d -> p (c d)"), AX.X, ALU.add,
                                  apply_absolute_value=True).then_inc(prep_w, 1)
                dve.tensor_reduce(wabs[:, 1:2], wpr_raw[:, :], AX.X, ALU.add, apply_absolute_value=True).then_inc(prep_w, 1)
                dve.wait_ge(prep_p0, 1)
                half = 0.5 / (HID0 * D)
                dve.tensor_scalar(whalf[:, 0, :], PB[7][:, 0:2], half, 0.5e-6, ALU.mult, ALU.add).then_inc(prep_w, 1)
                dve.wait_ge(prep_w, 3)
                dve.tensor_scalar(whalf[:, 1, :], whalf[:, 0, :], -1.0, None, ALU.mult).then_inc(prep_w, 1)
                dve.wait_ge(prep_w, 4)
                for k, src in enumerate((wfc_raw[:, :, :].rearrange("p c d -> p (c d)"), wpr_raw[:, :])):
                    dve.tensor_scalar(tern[:, k, :], src, whalf[:, 0, k:k + 1], None, ALU.is_gt).then_inc(prep_w, 1)
                    dve.tensor_scalar(tern_neg[:, k, :], src, whalf[:, 1, k:k + 1], None, ALU.is_lt).then_inc(prep_w, 1)
                dve.wait_ge(prep_w, 8)
                for k in range(2):
                    dve.tensor_tensor(tern[:, k, :], tern[:, k, :], tern_neg[:, k, :], ALU.subtract).then_inc(prep_w, 1)
                dve.wait_ge(ld_gate, 32 * B)
                dve.tensor_reduce(gate[:, :, :], gate_in[:, :, :, :], AX.X, ALU.add, apply_absolute_value=True
                                  ).then_inc(prep_v, 1)
                dve.wait_ge(prep_a, 6)
                dve.tensor_scalar(gate_e[:, :, :], gate_e[:, :, :], 1.0, None, ALU.add).then_inc(prep_v, 1)
                dve.wait_ge(prep_v, 2)
                dve.reciprocal(gate[:, :, :], gate_e[:, :, :]).then_inc(prep_v, 1)
                dve.tensor_scalar(lgate[:, 1:2], lgate[:, 0:1], 1.0, None, ALU.add).then_inc(prep_v, 1)
                dve.wait_ge(prep_v, 4)
                dve.reciprocal(lgate[:, 0:1], lgate[:, 1:2]).then_inc(prep_v, 1)
                dve.wait_ge(prep_v, 5)
                dve.tensor_scalar(lgate[:, 2:3], lgate[:, 0:1], -1.0, 1.0, ALU.mult, ALU.add).then_inc(prep_v, 1)
                dve.wait_ge(ld_mask, 16)
                dve.tensor_copy(mask01[:, :, :], mask8[:, :, :]).then_inc(prep_v, 1)
                for c, (lo, w, nb) in enumerate(chunk_cols(S2)):
                    for z in range(nb):
                        at = lo + z * (S2 // 4)
                        dve.tensor_scalar(mask_add[:, :, 2 * c + z, 0:w], mask8[:, :, at:at + w], -BIG, None, ALU.mult
                                          ).then_inc(prep_v, 1)
                dve.wait_ge(prep_v, 11)

            dve.sem_inc(score_free, FREE_SCORE)
            dve.sem_inc(e_acc, FREE_ACC)
            dve.sem_inc(e_w2, FREE_W)
            dve.wait_ge(ld_x, 16)

            def statistics(s, m):
                if s:
                    dve.wait_ge(x_ok, NT * (s - 1) + 4 * m + 4)
                for T in range(4 * m, 4 * m + 4):
                    dve.bn_stats(stats[:, T, :], x[:, T, :]).then_inc(ln_st, 1)
                for T in range(4 * m, 4 * m + 4):
                    dve.wait_ge(ln_st, NT * s + T + 1)
                    dve.bn_aggr(mv[:, T, :], stats[:, T, :]).then_inc(ln_mv, 1)

            def norm(s):
                for T in range(NT):
                    if T % 4 == 0:
                        dve.wait_ge(ln_rs, 2 * s + T // 4 + 1)
                    dve.tensor_scalar(xn[:, T, :], x[:, T, :], mv[:, T, 0:1], rstd[:, T:T + 1],
                                      ALU.subtract, ALU.mult).then_inc(ln_xn, 1)

            def k_split(r):
                g = r.ctx
                w = S2 // 4
                for b in range(B):
                    n = B * g + b
                    if r.layer == 0 and b == 2:
                        weights()
                    if n >= 2:
                        dve.wait_ge(k_out[b % 2], 48 * (n // 2))
                    for c in range(4):
                        lo = c * w + min(c, 1)
                        hi = lo + w + (c == 0)
                        dve.wait_ge(k_1, 4 * n + c + 1)
                        dve.scalar_tensor_tensor(out=k2c[:, b % 2, lo:hi], in0=PB[c][:, 0:hi - lo],
                                                 scalar=col(BK[r.index]), in1=k1c[:, b % 2, lo:hi],
                                                 op0=ALU.add, op1=ALU.subtract).then_inc(k_2, 1)
                    for c in range(4 if BV[r.index] else 0):
                        k = 4 if c < 3 else 1
                        pr = P if c < 3 else TAIL
                        dve.wait_ge(v_ps, 4 * n + c + 1)
                        dve.tensor_tensor(v_all[0:pr, b, 4 * c:4 * c + k, :],
                                          PB[4 + c][0:pr, 0:k * VW].rearrange("p (k d) -> p k d", k=k),
                                          row(BV[r.index], D)[0:pr].unsqueeze(1).broadcast_to([pr, k, D]),
                                          ALU.add).then_inc(v_ok, 1)

            def q_split(l):
                if l:
                    dve.wait_ge(q_2, 2 * l)
                for m in range(2):
                    sl = slice(m * 512, m * 512 + 512)
                    dve.wait_ge(q_ps, 2 * l + m + 1)
                    dve.tensor_scalar(qf[:, sl], PB[2 + m], col(BQ[l]), SCALE, ALU.add, ALU.mult).then_inc(q_f, 1)
                for m in range(2):
                    sl = slice(m * 512, m * 512 + 512)
                    dve.wait_ge(q_1, 2 * l + m + 1)
                    dve.tensor_tensor(q2c[:, sl], qf[:, sl], q1c[:, sl], ALU.subtract).then_inc(q_2, 1)

            def local_split():
                dve.wait_ge(padded, 16 * B * (len(RUNS) - 1))
                for m in range(2):
                    sl = slice(m * 512, m * 512 + 512)
                    dve.wait_ge(lk_1, m + 1)
                    dve.scalar_tensor_tensor(out=lk2[:, sl], in0=PB[2 + m], scalar=col(BK[LOCAL]),
                                             in1=lk1[:, sl], op0=ALU.add, op1=ALU.subtract).then_inc(lk_2, 1)
                for m in range(2):
                    dve.wait_ge(lk_ps, 3 + m)
                    dve.tensor_tensor(v_loc[:, 2 * m:2 * m + 2, :, :],
                                      PB[4 + m].rearrange("p (b k d) -> p b k d", b=2, k=2),
                                      row(BV[LOCAL], D).unsqueeze(1).unsqueeze(1).broadcast_to([P, 2, 2, D]),
                                      ALU.add).then_inc(lv_ok, 4)

            def attention(r):
                cpt = len(r.chunks)

                def piece(n, par, k, j, first):
                    qt, c, i = j // (cpt * HG), j // HG % cpt, j % HG
                    lo, w, nb = r.chunks[c]
                    src = pa[r.slot(par, k, first)][:, 0:nb, 0:w]
                    dst = mx[par][:, qt * HG + i, c:c + 1]
                    dve.wait_ge(score, r.use(n, k, first) + 1)
                    if r.mask:
                        dve.wait_ge(score_free, r.use(n, k, first) + (k != r.turn + 1))
                        dve.sem_inc(passed, 1)
                        dve.tensor_tensor_reduce(
                            out=masked[j % 2][:, :, 0:w], in0=src,
                            in1=mask_add[:, qt, 2 * c:2 * c + 2, 0:w],
                            scale=1.0, scalar=-3.0e38, op0=ALU.add, op1=ALU.max,
                            accum_out=dst).then_inc(score_free, 1)
                    else:
                        dve.tensor_reduce(dst, src, AX.XY, ALU.max).then_inc(score_free, 1)

                def split_maxima(n, par, first):
                    dve.wait_ge(score_free, FREE_SCORE + r.use(n, r.uses - 1, first) + 1)
                    dve.tensor_reduce(nm[par][:, :, :].rearrange("p q i -> p (q i)"), mx[par][:, :, 0:cpt], AX.X,
                                      ALU.max, negate=True).then_inc(mx_done, 1)
                    dve.wait_ge(mx_done, 2 * (r.u0 + n) + 1)
                    dve.tensor_scalar(nmc[par][:, :, :], nm[par][:, :, :], -MIN_MAX if r.mask else 3.0e38, None,
                                      ALU.min).then_inc(mx_done, 1)
                    dve.wait_ge(mx_done, 2 * (r.u0 + n) + 2)
                    dve.tensor_copy(m16[par][:, :, 0, :], nmc[par][:, :, :]).then_inc(m_ok, 1)
                    dve.wait_ge(m_ok, 2 * (r.u0 + n) + 1)
                    dve.tensor_tensor(m16[par][:, :, 1, :], nmc[par][:, :, :], m16[par][:, :, 0, :],
                                      ALU.subtract).then_inc(m_ok, 1)

                def keep_rows(par, slot, use):
                    dve.wait_ge(score, use + 1)
                    dve.tensor_copy(ms[par][:, :], pa[slot][:, 0, :].bitcast(F16)[0:2 * HG, 0:S]
                                    ).then_inc(score_free, 1)

                def unit(n, par, first=False):
                    for k, j in r.pieces(first):
                        if j is None:
                            keep_rows(1 - par, r.slot(par, k), r.use(n, k))
                        else:
                            piece(n, par, k, j, first)
                    split_maxima(n, par, first)
                    if r.local:
                        dve.wait_ge(fill, r.fill0 + (n - 1) * r.fills)
                    dve.tensor_copy(qp2[par][:, :, :], qp1[par][:, :, :]).then_inc(q_kept, 1)

                unit(0, 0, first=True)
                with dve.Fori(0, UNITS // 2 - 1) as t:
                    unit(2 * t + 1, 1)
                    unit(2 * t + 2, 0)
                unit(UNITS - 1, 1)
                keep_rows(1, 1, r.use0 + UNITS * r.uses - 1)

            def heads_out(r):
                dst = on_loc if r.local else on
                bank = lambda T: PB[T % 4].rearrange("p (h c) -> p h c", c=R)
                for m in range(0, NT, 4):
                    for T in range(m, m + 4):
                        dve.wait_ge(o_t, NT * r.index + T + 1)
                        dve.tensor_scalar(rec0[:, T, :], bank(T)[:, :, DH], TINY, None, ALU.max).then_inc(o_rec, 1)
                    dve.wait_ge(o_rec, NT * r.index + m + 4)
                    dve.reciprocal(rec[:, m:m + 4, :], rec0[:, m:m + 4, :]).then_inc(o_inv, 1)
                    dve.wait_ge(o_inv, 2 * r.index + m // 4 + 1)
                    coef = 1.0 if r.layer != 1 else lgate[:, 0:1] if r.local else lgate[:, 2:3]
                    for T in range(m, m + 4):
                        dve.scalar_tensor_tensor(
                            out=dst[:, T, :].rearrange("p (h d) -> p h d", d=DH), in0=bank(T)[:, :, 0:DH], scalar=coef,
                            in1=rec[:, T, :].unsqueeze(2).broadcast_to([P, H, DH]), op0=ALU.mult, op1=ALU.mult
                            ).then_inc(o_n, 1)

            biased = [0]

            def residual(s, bank_of, bias, gate_col, ready, at, then):
                for m in range(2):
                    dve.wait_ge(ready, at + m + 1)
                    y = PB[bank_of + m].rearrange("p (k d) -> p k d", k=4)
                    if bias:
                        dve.tensor_tensor(ytmp[:, 4 * m:4 * m + 4, :], y,
                                          row(bias, D).unsqueeze(1).broadcast_to([P, 4, D]), ALU.add).then_inc(y_t, 1)
                        biased[0] += 1
                        dve.wait_ge(y_t, biased[0])
                        y = ytmp[:, 4 * m:4 * m + 4, :]
                    dve.scalar_tensor_tensor(out=x[:, 4 * m:4 * m + 4, :], in0=y,
                                             scalar=tg[:, gate_col:gate_col + 1], in1=x[:, 4 * m:4 * m + 4, :],
                                             op0=ALU.mult, op1=ALU.add).then_inc(x_ok, 4)
                    if then is not None:
                        statistics(then, m)

            def ffn0():
                for T in range(NT):
                    dve.wait_ge(f_act, T + 1)
                    dve.bn_stats(stats[:, T, :], h0[:, T, :]).then_inc(f_st0, 1)
                    dve.wait_ge(f_st0, T + 1)
                    dve.bn_aggr(mv[:, T, :], stats[:, T, :]).then_inc(f_st, 1)
                    if T >= 4:
                        scale_h(T - 4)
                for T in range(4, NT):
                    scale_h(T)

            def scale_h(T):
                dve.wait_ge(f_rs, T // 4 + 1)
                dve.tensor_scalar(h0[:, T, :], h0[:, T, :], mv[:, T, 0:1], rstd[:, T:T + 1],
                                  ALU.subtract, ALU.mult).then_inc(f_n, 1)

            def route(which):
                cnt = [ROUTE_V[which][2]]

                def step(ins, n=1):
                    ins.then_inc(r_v, 1)
                    cnt[0] += 1

                for m in range(2):
                    sl = slice(m * 512, m * 512 + 512)
                    dve.wait_ge(x_1, 2 * which + m + 1)
                    dve.tensor_tensor(xs[1][:, sl], xnT[:, sl], xs[0][:, sl], ALU.subtract).then_inc(x_2, 1)
                dve.wait_ge(r_ps, which + 1)
                step(dve.tensor_tensor(lg[:, :, :], PB[2][:, 0:NT * E1].rearrange("p (t e) -> p t e", e=E1),
                                       (row("L3_ffn_gate_b", E1) if which else row("zero", E1)
                                        ).unsqueeze(1).broadcast_to([P, NT, E1]), ALU.add))
                dve.wait_ge(r_v, cnt[0])
                step(dve.tensor_reduce(lmax[:, :], lg[:, :, :], AX.X, ALU.max))
                dve.wait_ge(r_v, cnt[0])
                step(dve.tensor_tensor(lsh[:, :, :], lg[:, :, :], lmax[:, :].unsqueeze(2).broadcast_to([P, NT, E1]),
                                       ALU.subtract))
                assert cnt[0] == ROUTE_V[which][0]
                dve.wait_ge(r_a, which + 1)
                if which:
                    step(dve.tensor_reduce(lsum[:, :], lex[:, :, :], AX.X, ALU.add))
                    dve.wait_ge(r_v, cnt[0])
                    step(dve.reciprocal(lrec[:, :], lsum[:, :]))
                    dve.wait_ge(r_v, cnt[0])
                    step(dve.tensor_tensor(prob[:, :, :], lex[:, :, :],
                                           lrec[:, :].unsqueeze(2).broadcast_to([P, NT, E1]), ALU.mult))
                    dve.wait_ge(r_v, cnt[0])
                key = prob if which else lg
                val = prob if which else lex
                by_j = key[:, :, :].unsqueeze(2).broadcast_to([P, NT, E1, E1])
                by_e = key[:, :, :].unsqueeze(3).broadcast_to([P, NT, E1, E1])
                step(dve.tensor_tensor(above[:, :, :, :], by_j, by_e, ALU.is_gt))
                step(dve.tensor_tensor(tied[:, :, :, :], by_j, by_e, ALU.is_equal))
                dve.wait_ge(r_v, cnt[0])
                step(dve.tensor_tensor(tied[:, :, :, :], tied[:, :, :, :],
                                       earlier[:, :, :].unsqueeze(1).broadcast_to([P, NT, E1, E1]), ALU.mult))
                dve.wait_ge(r_v, cnt[0])
                step(dve.tensor_tensor(above[:, :, :, :], above[:, :, :, :], tied[:, :, :, :], ALU.add))
                dve.wait_ge(r_v, cnt[0])
                step(dve.tensor_reduce(rank[:, :, :], above[:, :, :, :], AX.X, ALU.add))
                dve.wait_ge(r_v, cnt[0])
                step(dve.scalar_tensor_tensor(out=(comb if which else chosen)[:, :, :], in0=rank[:, :, :], scalar=1.5,
                                              in1=val[:, :, :], op0=ALU.is_lt, op1=ALU.mult))
                dve.wait_ge(r_v, cnt[0])
                if not which:
                    step(dve.tensor_reduce(lsum[:, :], chosen[:, :, :], AX.X, ALU.add))
                    dve.wait_ge(r_v, cnt[0])
                    step(dve.reciprocal(lrec[:, :], lsum[:, :]))
                    dve.wait_ge(r_v, cnt[0])
                    step(dve.tensor_tensor(comb[:, :, :], chosen[:, :, :],
                                           lrec[:, :].unsqueeze(2).broadcast_to([P, NT, E1]), ALU.mult))
                assert cnt[0] == ROUTE_V[which][1], cnt
                dve.wait_ge(r_v, cnt[0])
                dve.tensor_scalar(comb_s[:, :, :], comb[:, :, :], 1.0 / WSCALE, None, ALU.mult).then_inc(r_acc, 1)
                for m in range(2):
                    dve.wait_ge(r_b, 2 * which + m + 1)
                    dve.tensor_copy(acc[:, 4 * m:4 * m + 4, :], PB[6 + m].rearrange("p (k d) -> p k d", k=4)
                                    ).then_inc(r_acc, 1)

            def experts(which, hid):
                cc = hid // P
                act0 = which and 2 * E1 * (HID1 // P)
                dve.wait_ge(r_acc, 3 * which + 3)
                by_expert = comb_s[:, :, :].rearrange("p t e -> p e t")

                def second_parts(e, k):
                    for i, (w, parts_) in enumerate(((w_up[k][:, 0:hid], wus[k]),
                                                     (w_dn[k][:, 0:cc, :].rearrange("p c d -> p (c d)"), wds[k]))):
                        dve.wait_ge(e_w1, 2 * (E1 * which + e) + i + 1)
                        dve.scalar_tensor_tensor(out=parts_[1][:, 0:hid], in0=w, scalar=WSCALE,
                                                 in1=parts_[0][:, 0:hid], op0=ALU.mult, op1=ALU.subtract
                                                 ).then_inc(e_w2, 1)

                def hidden(e, hf):
                    for c in range(cc):
                        dve.wait_ge(e_act, FREE_UP + act0 + e * 2 * cc + hf * cc + c + 1)
                        dve.tensor_tensor(hs[hf][1][:, c, :], hT[hf][:, c, :], hs[hf][0][:, c, :], ALU.subtract
                                          ).then_inc(e_h2, 1)

                def add(e, hf):
                    q = 2 * E1 * which + 2 * e + hf
                    dve.wait_ge(e_dn, FREE_HID + q + 1)
                    dve.wait_ge(e_acc, 4 * q + 4)
                    for T in range(4):
                        dve.scalar_tensor_tensor(
                            out=acc[:, 4 * hf + T, :], in0=PB[4 + hf][:, T * D:T * D + D],
                            scalar=by_expert[:, e, 4 * hf + T:4 * hf + T + 1], in1=acc[:, 4 * hf + T, :],
                            op0=ALU.mult, op1=ALU.add).then_inc(e_acc, 1)

                def expert(e, k, more=True):
                    if more:
                        second_parts(e + 1, 1 - k)
                    hidden(e, 1)
                    add(e, 0)
                    if more:
                        hidden(e + 1, 0)
                    add(e, 1)

                second_parts(0, 0)
                hidden(0, 0)
                with dve.Fori(0, E1 // 2 - 1) as t:
                    expert(2 * t, 0)
                    expert(2 * t + 1, 1)
                expert(E1 - 2, 0)
                expert(E1 - 1, 1, more=False)

            def experts_out(which, s, gate_col, then):
                dve.wait_ge(e_acc, 8 + 4 * 2 * E1 * (which + 1))
                for m in range(2):
                    dve.scalar_tensor_tensor(out=x[:, 4 * m:4 * m + 4, :], in0=acc[:, 4 * m:4 * m + 4, :],
                                             scalar=tg[:, gate_col:gate_col + 1], in1=x[:, 4 * m:4 * m + 4, :],
                                             op0=ALU.mult, op1=ALU.add).then_inc(x_ok, 4)
                    if then is not None:
                        statistics(then, m)

            for m in range(2):
                statistics(0, m)
            n_res = 0
            for l in range(LAYERS):
                norm(ln_at(l, 0))
                q_split(l)
                if l == 1:
                    local_split()
                for r in RUNS:
                    if r.layer == l and not r.local:
                        k_split(r)
                for r in RUNS:
                    if r.layer == l:
                        attention(r)
                        heads_out(r)
                residual(n_res, 6, BO[l], l, y_ps, 2 * l, ln_at(l, 1))
                n_res += 1
                after = ln_at(l + 1, 0) if l + 1 < LAYERS else None
                norm(ln_at(l, 1))
                if l == 0:
                    ffn0()
                    residual(n_res, 6, None, 4, f_dn, 0, after)
                    n_res += 1
                if l == 2:
                    residual(n_res, 6, "L2_ffn_bias", 6, f_dn, 2, after)
                    n_res += 1
                if l in (1, 3):
                    route(l // 2)
                    experts(l // 2, HID1 if l == 1 else HID3)
                    experts_out(l // 2, n_res, 4 + l, after)

        @block.tensor
        def _(pe):
            pe.wait_ge(consts, 12)
            pe.sem_inc(pv, FREE_PT)
            pe.sem_inc(e_dn, FREE_HID)

            def ctx_turn(b):
                pe.wait_ge(ctx_in[b % 2], 32 * (b // 2 + 1))
                for m in range(4):
                    if b:
                        pe.wait_ge(v_ok, 4 * (b - 1) + m + 1)
                    if b == 2:
                        pe.wait_ge(prep_a, 10)
                    for k in range(4 * m, min(4 * m + 4, KT)):
                        pr = P if k < FULL else TAIL
                        ins = pe.transpose(PB[4 + m][:, (k % 4) * P:(k % 4) * P + pr], ctx_raw[0:pr, b % 2, k, :],
                                           ident[0:pr, 0:pr])
                    ins.then_inc(ctx_t, 1)

            def spread_vectors():
                pe.wait_ge(ld_cols, 16 * len(COLS))
                pe.transpose(PB[0][:, 0:NCOL], cols_raw[:, :], ident[0:NCOL, 0:NCOL]).then_inc(prep_p, 1)
                pe.wait_ge(ld_rows, 16 * (len(ROWS) - 1))
                pe.matmul(PB[1], ones[0:1, :], rows[0:1, 0:512], start=True, stop=True).then_inc(prep_p, 1)
                pe.matmul(PB[2][:, 0:NROW - 512], ones[0:1, :], rows[0:1, 512:NROW], start=True, stop=True
                          ).then_inc(prep_p, 1)
                pe.wait_ge(prep_a, 3)
                pe.wait_ge(ld_w, 16 * (len(SQUARE) - len(TURNED)))

            def weights():
                pe.wait_ge(k_2, 8)
                pe.wait_ge(v_ok, 8)
                pe.wait_ge(ld_wt, 16 * len(TURNED))
                for m in range(len(TURNED)):
                    ins = pe.transpose(PB[m // 4][:, (m % 4) * D:(m % 4) * D + D], wraw[:, m, :], ident[:, :])
                    if m % 4 == 3 or m == len(TURNED) - 1:
                        ins.then_inc(w_turned, 1)
                pe.wait_ge(prep_w, 2)
                pe.matmul(PB[7][:, 0:2], ones[:, :], wabs[:, :], start=True, stop=True).then_inc(prep_p0, 1)
                pe.wait_ge(prep_w, 10)
                for c in range(4):
                    ins = pe.transpose(PB[7][:, c * P:c * P + P], tern[:, 0, c * D:c * D + D], ident[:, :])
                ins.then_inc(prep_p, 1)
                for c in range(4):
                    ins = pe.transpose(PB[4][:, c * D:c * D + D], tern[:, 1, c * P:c * P + P], ident[:, :])
                ins.then_inc(prep_p, 1)
                pe.wait_ge(ld_misc, 16 * 9)
                C_, S_, N_ = dft[:, 0, :], dft[:, 1, :], dft[:, 2, :]
                pe.matmul(PB[5][:, 0:D], wfreq[:, 0, :], C_, start=True, stop=False)
                pe.matmul(PB[5][:, 0:D], wfreq[:, 1, :], S_, start=False, stop=True)
                pe.matmul(PB[5][:, D:2 * D], wfreq[:, 1, :], C_, start=True, stop=False)
                pe.matmul(PB[5][:, D:2 * D], wfreq[:, 0, :], N_, start=False, stop=True).then_inc(prep_p, 1)
                pe.wait_ge(prep_a, 9)
                pe.matmul(PB[6][:, 0:D], a12[:, 0, :], C_, start=True, stop=False)
                pe.matmul(PB[6][:, 0:D], a12[:, 1, :], N_, start=False, stop=True).then_inc(prep_p, 1)
                pe.wait_ge(w_kept, 4)

            def normT(s):
                for T in range(NT):
                    pe.wait_ge(ln_xn, NT * s + T + 1)
                    ins = pe.transpose(PB[T // 4][:, (T % 4) * P:(T % 4) * P + P], xn[:, T, :], ident[:, :])
                    if T % 4 == 3:
                        ins.then_inc(ln_t, 1)

            def kv(r):
                g = r.ctx
                w = S2 // 4
                pe.wait_ge(q_f, 2 * (r.layer + 1))
                for b in range(B):
                    n = B * g + b
                    if r.layer == 0:
                        if b == 2:
                            weights()
                        if b:
                            ctx_turn(b)
                        pe.wait_ge(ctx_e, 4 * (b + 1))
                    else:
                        pe.wait_ge(c_ld[b % 2], 16 * ((n - B) // 2 + 1))
                    for c in range(4):
                        if b:
                            pe.wait_ge(k_2, 4 * (n - 1) + c + 1)
                        lo = c * w + min(c, 1)
                        pe.matmul(PB[c][:, 0:w + (c == 0)], sq(WK[r.index]), ctxT[:, b % 2, lo:lo + w + (c == 0)],
                                  start=True, stop=True).then_inc(k_ps, 1)
                    for c in range(4):
                        if b:
                            pe.wait_ge(v_ok, 4 * (n - 1) + c + 1)
                        for k in range(4 * c, min(4 * c + 4, KT)):
                            pr = P if k < FULL else TAIL
                            ins = pe.matmul(PB[4 + c][0:pr, (k % 4) * VW:(k % 4) * VW + VW],
                                            ctxT[:, b % 2, k * P:k * P + pr], sq(WV[r.index]), start=True, stop=True)
                        ins.then_inc(v_ps, 1)
                pe.wait_ge(k_2, 4 * B * (g + 1))
                pe.wait_ge(v_ok, 4 * B * (g + 1))

            def queries(l):
                for m in range(2):
                    pe.wait_ge(ln_xt, 2 * ln_at(l, 0) + m + 1)
                    pe.matmul(PB[2 + m], sq(WQ[l]), xnT[:, m * 512:m * 512 + 512], start=True, stop=True
                              ).then_inc(q_ps, 1)

            def local_kv():
                pe.wait_ge(q_f, 4)
                for m in range(2):
                    pe.matmul(PB[2 + m], sq(WK[LOCAL]), xnT[:, m * 512:m * 512 + 512], start=True, stop=True
                              ).then_inc(lk_ps, 1)
                for m in range(2):
                    for T in range(4 * m, 4 * m + 4):
                        ins = pe.matmul(PB[4 + m][:, (T % 4) * VW:(T % 4) * VW + VW], xnT[:, T * P:T * P + P],
                                        sq(WV[LOCAL]), start=True, stop=True)
                    ins.then_inc(lk_ps, 1)
                pe.wait_ge(lk_2, 2)
                pe.wait_ge(lv_ok, NT)

            def attention(r):
                cpt = len(r.chunks)

                def turn(par, slot, use):
                    pe.wait_ge(score_free, use + FREE_SCORE - 1)
                    for qt in range(QT):
                        ins = pe.transpose(pa[slot][:, 0, :].bitcast(F16)[0:2 * HG, qt * P:qt * P + P],
                                           m16[par][:, qt, :, :].rearrange("p a i -> p (a i)"), ident16[:, :])
                    ins.then_inc(score, 1)

                def piece(n, par, k, first=False):
                    use, slot = r.use(n, k, first), r.slot(par, k, first)
                    if k == r.turn:
                        pe.wait_ge(m_ok, 2 * (r.u0 + n))
                        turn(1 - par, slot, use)
                        return
                    j = k - (k > r.turn)
                    pe.wait_ge(score_free, use + FREE_SCORE - 1)
                    if k == 0:
                        pe.wait_ge(in1[par], IN_DMAS * (r.u0 + n - par + 2))
                    qt, c, i = j // (cpt * HG), j // HG % cpt, j % HG
                    lo, w, nb = r.chunks[c]
                    for z in range(nb):
                        at = lo + z * (S2 // 4)
                        ins = pe.matmul(pa[slot][:, z, 0:w], qp1[par][:, i, qt * P:qt * P + P],
                                        kp1[par][:, at:at + w], start=True, stop=True)
                    ins.then_inc(score, 1)

                def fills(n, par, s, h):
                    f = par * r.fills + PAIRS * s + h
                    pe.wait_ge(exped, FREE_EXP + r.fill0 + n * r.fills + PAIRS * s + h - r.back(f) + 1)
                    if s == 0 and h == 0:
                        pe.wait_ge(in2[par], 8 * (r.u0 + n - par + 2))
                        pe.wait_ge(m_in[par], 8 * (r.u0 + n - par + 2))
                    bank, rows_ = pe_[r.banks[f]], r.keys(s)
                    ins = pe.matmul(bank[0:rows_, :], kp2[par][:, s * P:s * P + rows_],
                                    qp2[par][:, 2 * h:2 * h + 2, :], start=True, stop=True, skip_group_check=r.mask)
                    if r.mask:
                        for qt in range(QT):
                            ins = pe.matmul(bank[0:rows_, :].rearrange("p (i q) -> p i q", q=S)[:, :, qt * P:qt * P + P],
                                            mask01[:, qt, s * P:s * P + rows_],
                                            mask_eye[:, :].unsqueeze(1).broadcast_to([P, 2, P]),
                                            start=False, stop=True, skip_group_check=True)
                    ins.then_inc(fill, 1)

                def product(n, par, s):
                    if s == 0:
                        pe.wait_ge(vg_ok, r.u0 + n + 1)
                        pe.wait_ge(o_ok, r.u0 + n + 1)
                    pe.wait_ge(exped, FREE_EXP + r.fill0 + n * r.fills + PAIRS * (s + 1))
                    g, rows_ = (par * r.kt + s) % 2, r.keys(s)
                    for j in range(HG):
                        ins = pe.matmul(po[R * j:R * j + R, 0:S], vg[par][0:rows_, s, j, :], pt[g][0:rows_, j, :],
                                        start=(s == 0), stop=(s == r.kt - 1))
                    ins.then_inc(pv, 1)

                def unit(n, par, prev=True, ahead="unit"):
                    todo = [(1, k) for k in range(r.ahead, r.uses)] if ahead else []
                    if ahead == "unit":
                        todo += [None] * r.pause + [(2, k) for k in range(r.ahead)]
                    elif ahead:
                        todo += [None]
                    total, given = len(todo), 0
                    if ahead == "rest":
                        total = len(todo) * r.fills // r.tail
                    for s in range(r.kt):
                        for h in range(PAIRS):
                            fills(n, par, s, h)
                            while given < min(len(todo), (PAIRS * s + h + 1) * total // r.fills):
                                if todo[given]:
                                    d, k = todo[given]
                                    piece(n + d, (par + d) % 2, k)
                                elif ahead == "rest" and PAIRS * s + h >= r.fills - r.gap:
                                    pe.wait_ge(m_ok, 2 * (r.u0 + UNITS))
                                    turn(1, 1, r.use0 + UNITS * r.uses - 1)
                                elif ahead == "rest":
                                    break
                                given += 1
                        if s:
                            product(n, par, s - 1)
                        elif prev:
                            product(n - 1, 1 - par, r.kt - 1)
                        if ahead is None and s == r.kt // 2:
                            heads_out(r, range(0, NT // 2))

                for k, _ in r.pieces(first=True):
                    piece(0, 0, k, first=True)
                for k in range(r.ahead):
                    piece(1, 1, k)
                unit(0, 0, prev=False)
                with pe.Fori(0, UNITS // 2 - 2) as t:
                    unit(2 * t + 1, 1)
                    unit(2 * t + 2, 0)
                unit(UNITS - 3, 1)
                unit(UNITS - 2, 0, ahead="rest")
                unit(UNITS - 1, 1, ahead=None)
                product(UNITS - 1, 1, r.kt - 1)

            def heads_out(r, tiles):
                if tiles[0] == 0:
                    pe.wait_ge(score_free, FREE_SCORE + r.use0 + UNITS * r.uses)
                pe.wait_ge(o_ok, FREE_PV + r.u0 + (tiles[-1] // QT + 1) * HG)
                for T in tiles:
                    b, qt = T // QT, T % QT
                    if T >= 4:
                        pe.wait_ge(o_n, NT * r.index + T - 3)
                    for g in range(HG):
                        ins = pe.transpose(PB[T % 4][:, g * P:g * P + P], o_all[:, HG * b + g, qt * P:qt * P + P],
                                           ident[:, :])
                    ins.then_inc(o_t, 1)

            def project(l):
                if l == 1:
                    pe.wait_ge(o_add, 1)
                for T in range(NT):
                    ins = pe.transpose(PB[4 + T // 4][:, (T % 4) * P:(T % 4) * P + P], on[:, T, :], ident[:, :])
                    if T % 4 == 3:
                        ins.then_inc(on_t, 1)
                for T in range(NT):
                    if T % 4 == 0:
                        pe.wait_ge(on_e, 2 * l + T // 4 + 1)
                    ins = pe.matmul(PB[6 + T // 4][:, (T % 4) * D:(T % 4) * D + D], onT[:, T * P:T * P + P],
                                    sq(WO[l]), start=True, stop=True)
                    if T % 4 == 3:
                        ins.then_inc(y_ps, 1)

            def ffn0():
                for T in range(NT):
                    if T % 4 == 0:
                        pe.wait_ge(ln_xt, 2 * ln_at(0, 1) + T // 4 + 1)
                    if T >= 4:
                        pe.wait_ge(f_act, T - 3)
                    pe.matmul(PB[2 + T % 4], xnT[:, T * P:T * P + P], wfcT[:, :], start=True, stop=True
                              ).then_inc(f_up, 1)
                pe.wait_ge(f_act, NT)
                for m in range(2):
                    for c in range(4):
                        if m:
                            pe.wait_ge(f_ht, c + 1)
                        for k in range(4):
                            pe.wait_ge(f_n, 4 * m + k + 1)
                            ins = pe.transpose(PB[c][:, k * P:k * P + P], h0[:, 4 * m + k, c * P:c * P + P],
                                               ident[:, :])
                        ins.then_inc(f_t, 1)
                for m in range(2):
                    for k in range(4):
                        for c in range(4):
                            pe.wait_ge(f_ht, 4 * m + c + 1)
                            ins = pe.matmul(PB[6 + m][:, k * D:k * D + D], hT[m][:, c, k * P:k * P + P],
                                            wprT[:, c, :], start=(c == 0), stop=(c == 3))
                    ins.then_inc(f_dn, 1)

            def ffn2():
                for T in range(NT):
                    if T % 4 == 0:
                        pe.wait_ge(ln_xt, 2 * ln_at(2, 1) + T // 4 + 1)
                    ins = pe.matmul(PB[6 + T // 4][:, (T % 4) * D:(T % 4) * D + D], xnT[:, T * P:T * P + P],
                                    mfreq[:, :], start=True, stop=True)
                    if T % 4 == 3:
                        ins.then_inc(f_dn, 1)

            def route(which, l):
                for T in range(NT):
                    if T % 4 == 0:
                        pe.wait_ge(ln_xt, 2 * ln_at(l, 1) + T // 4 + 1)
                    ins = pe.matmul(PB[2][:, T * E1:T * E1 + E1], xnT[:, T * P:T * P + P], wr[:, which, :],
                                    start=True, stop=True)
                ins.then_inc(r_ps, 1)
                pe.wait_ge(r_v, ROUTE_V[which][1])
                for T in range(NT):
                    ins = pe.transpose(PB[2 + T // 4][0:E1, (T % 4) * P:(T % 4) * P + P], comb[:, T, :], ident[:, :])
                    if T % 4 == 3:
                        ins.then_inc(r_ct, 1)
                for T in range(NT):
                    if T % 4 == 0:
                        pe.wait_ge(r_cc, 2 * which + T // 4 + 1)
                    ins = pe.matmul(PB[6 + T // 4][:, (T % 4) * D:(T % 4) * D + D], combT[:, T * P:T * P + P],
                                    b2[:, which, :], start=True, stop=True)
                    if T % 4 == 3:
                        ins.then_inc(r_b, 1)

            def experts(which, hid):
                cc = hid // P
                act0 = which and 2 * E1 * (HID1 // P)
                pe.wait_ge(x_2, 2 * which + 2)

                def up(e, k, hf):
                    if hf == 0:
                        pe.wait_ge(e_w2, FREE_W + 2 * (E1 * which + e) + 2)
                    for c in range(cc):
                        pe.wait_ge(e_act, FREE_UP + act0 + e * 2 * cc + hf * cc + c - 3)
                        for i, (wp, xp) in enumerate(PRODUCTS):
                            ins = pe.matmul(PB[(hf * cc + c) % 4], wus[k][wp][:, c * P:c * P + P],
                                            xs[xp][:, hf * 512:hf * 512 + 512], start=(i == 0), stop=(i == 2))
                        ins.then_inc(e_up, 1)

                def down(e, k, hf):
                    q = 2 * E1 * which + 2 * e + hf
                    pe.wait_ge(e_acc, 4 * q + 4)
                    pe.wait_ge(e_h2, act0 + e * 2 * cc + (hf + 1) * cc)
                    for T in range(4):
                        for c in range(cc):
                            for i, (wp, hp) in enumerate(PRODUCTS):
                                ins = pe.matmul(PB[4 + hf][:, T * D:T * D + D], hs[hf][hp][:, c, T * P:T * P + P],
                                                wds[k][wp][:, c * D:c * D + D], start=(c == 0 and i == 0),
                                                stop=(c == cc - 1 and i == 2))
                    ins.then_inc(e_dn, 1)

                def expert(e, k, more=True):
                    up(e, k, 1)
                    down(e, k, 0)
                    if more:
                        up(e + 1, 1 - k, 0)
                    down(e, k, 1)

                up(0, 0, 0)
                with pe.Fori(0, E1 // 2 - 1) as t:
                    expert(2 * t, 0)
                    expert(2 * t + 1, 1)
                expert(E1 - 2, 0)
                expert(E1 - 1, 1, more=False)

            ctx_turn(0)
            spread_vectors()
            for l in range(LAYERS):
                normT(ln_at(l, 0))
                queries(l)
                if l == 1:
                    local_kv()
                for r in RUNS:
                    if r.layer == l and not r.local:
                        kv(r)
                for r in RUNS:
                    if r.layer == l:
                        attention(r)
                        heads_out(r, range(NT // 2, NT))
                        pe.wait_ge(o_n, NT * r.index + NT)
                project(l)
                normT(ln_at(l, 1))
                if l == 0:
                    ffn0()
                if l == 2:
                    ffn2()
                if l in (1, 3):
                    route(l // 2, l)
                    experts(l // 2, HID1 if l == 1 else HID3)


_OUT = (B, S, D)
_NAMES = (["x", "ctx_1024", "ctxb_2048x8", "mask_1x1xSxS2_bk1"] + [n for n, _ in SQUARE] + [n for n, _ in COLS]
          + [n for n, _ in ROWS if n != "zero"]
          + ["L0_ffn_W_fc", "L0_ffn_W_proj", "L1_ffn_Wr", "L1_ffn_W1", "L1_ffn_W2", "L1_ffn_b2",
             "L2_ffn_w_freq_real", "L2_ffn_w_freq_imag", "L3_ffn_gate_w", "L3_ffn_w1", "L3_ffn_w2", "L3_ffn_b2"])


def kernel(**inputs):
    import numpy as np
    import concourse.bacc as bacc
    from concourse.bass_utils import run_bass_kernel_spmd

    nc = bacc.Bacc("TRN2", target_bir_lowering=False, num_devices=1)
    arrays, args = {}, {}
    angle = 2.0 * np.pi * (np.outer(np.arange(D), np.arange(D)) % D) / D
    tables = {"dft_cos": np.cos(angle), "dft_sin": np.sin(angle), "dft_nsin": -np.sin(angle)}
    for name in _NAMES + list(tables):
        v = tables[name].astype(np.float32) if name in tables else np.ascontiguousarray(inputs[name])
        if v.ndim == 0:
            v = v.reshape(1)
        arrays[f"in_{name}"] = v
        args[name] = nc.dram_tensor(f"in_{name}", v.shape, mybir.dt.from_np(v.dtype), kind="ExternalInput").ap()
    out = nc.dram_tensor("out", _OUT, F32, kind="ExternalOutput").ap()
    flamingo(nc, args, out)
    got = run_bass_kernel_spmd(nc, [arrays], core_ids=[0])
    return got.results[0]["out"]
```
